# Optimizing a Trainium2 kernel written in Bass

```python
import numpy as np
import jax
import jax.numpy as jnp

def _softmax(x, axis=-1):
    return jax.nn.softmax(x, axis=axis)
def _gelu(x):
    return jax.nn.gelu(x, approximate=True)
def _silu(x):
    return jax.nn.silu(x)
def _sigmoid(x):
    return jax.nn.sigmoid(x)
def _layernorm(x, axis=-1, eps=1e-5):
    m = jnp.mean(x, axis=axis, keepdims=True)
    v = jnp.var(x, axis=axis, keepdims=True)
    return (x - m) / jnp.sqrt(v + eps)
def _scatter_add(tgt, idx, src, axis=0):
    return tgt.at[idx].add(src)
def _segment_sum(src, seg, n):
    return jax.ops.segment_sum(src, seg, n)

kernel_name = 'mk_conv_attn_hybrid_d2_conv_nchw512_bed553'

def setup_inputs(seed: int = 0):
    np.random.seed(seed)
    _w = jnp.asarray
    def _rec_inputs():
        import jax
        import jax.numpy as jnp
        _gk = jax.random.key(seed)
        x = -0.0002928 + 1 * jax.random.normal(jax.random.fold_in(_gk, 1), (8, 512, 32, 32), jnp.float32)
        return x
    x = _rec_inputs()
    def _L0_conv_setup():
        import jax, jax.numpy as jnp
        from jax import lax
        import numpy as np
        D_IN = 512
        HID = 128
        D_INNER = 2 * HID
        D_PROJ = 2 * D_INNER
        N_STATE = 16
        R_DT = 8
        B, H, W = (8, 32, 32)

        def _layernorm(y, g, b):
            mu = y.mean(-1, keepdims=True)
            var = ((y - mu) ** 2).mean(-1, keepdims=True)
            return (y - mu) / jnp.sqrt(var + 1e-05) * g + b

        def _ssm(x, xw, dtw, dtb, Al, Dv, g, be):
            Bb, D, L = x.shape
            n = Al.shape[1]
            xd = jnp.einsum('bdl,kd->blk', x, xw)
            dts = xd[..., :R_DT]
            Bs = xd[..., R_DT:R_DT + n]
            Cs = xd[..., R_DT + n:]
            delta = jax.nn.softplus(jnp.einsum('blr,dr->bld', dts, dtw) + dtb)
            A = -jnp.exp(Al)
            xt = x.transpose(0, 2, 1)
            dA = jnp.exp(delta[..., None] * A)
            dBx = delta[..., None] * Bs[:, :, None, :] * xt[..., None]

            def step(h, inp):
                da, dbx, c = inp
                h = h * da + dbx
                return (h, jnp.einsum('bdn,bn->bd', h, c))
            h0 = jnp.zeros((Bb, D, n), x.dtype)
            _, ys = lax.scan(step, h0, (dA.transpose(1, 0, 2, 3), dBx.transpose(1, 0, 2, 3), Cs.transpose(1, 0, 2)))
            y = ys.transpose(1, 0, 2) + xt * Dv
            return _layernorm(y, g, be)

        def _up2(y, h, w):
            Bb, L, C = y.shape
            img = y.transpose(0, 2, 1).reshape(Bb, C, h, w)
            img = jnp.repeat(jnp.repeat(img, 2, axis=2), 2, axis=3)
            return img.reshape(Bb, C, 4 * L).transpose(0, 2, 1)

        def _conv1x1(x, w, b):
            return jnp.einsum('bchw,oc->bohw', x, w) + b[None, :, None, None]

        def _conv2s2(x, w, b):
            out = lax.conv_general_dilated(x, w, (2, 2), 'VALID', dimension_numbers=('NCHW', 'OIHW', 'NCHW'))
            return out + b[None, :, None, None]

        def _forward(input_f, in_w, in_b, c1_w, c1_b, c2_w, c2_b, c3_w, c3_b, out_w, out_b, xw1, dtw1, dtb1, Al1, Dv1, g1, be1, xw2, dtw2, dtb2, Al2, Dv2, g2, be2, xw3, dtw3, dtb3, Al3, Dv3, g3, be3):
            xz = _conv1x1(input_f, in_w, in_b)
            x, z = jnp.split(xz, 2, axis=1)
            f1 = _conv1x1(x, c1_w, c1_b)
            f2 = _conv2s2(f1, c2_w, c2_b)
            f3 = _conv2s2(f2, c3_w, c3_b)
            Bb, C, h3, w3 = f3.shape
            fx3 = f3.reshape(Bb, C, h3 * w3)
            y3 = _ssm(fx3, xw3, dtw3, dtb3, Al3, Dv3, g3, be3) + jnp.flip(_ssm(jnp.flip(fx3, -1), xw3, dtw3, dtb3, Al3, Dv3, g3, be3), 1)
            y2_ = _up2(y3, h3, w3)
            _, _, h2, w2 = f2.shape
            fx2 = f2.reshape(Bb, C, h2 * w2)
            y2 = _ssm(fx2, xw2, dtw2, dtb2, Al2, Dv2, g2, be2) + jnp.flip(_ssm(jnp.flip(fx2, -1), xw2, dtw2, dtb2, Al2, Dv2, g2, be2), 1) + y2_
            y1_ = _up2(y2, h2, w2)
            _, _, h1, w1 = f1.shape
            fx1 = f1.reshape(Bb, C, h1 * w1)
            y1 = _ssm(fx1, xw1, dtw1, dtb1, Al1, Dv1, g1, be1) + jnp.flip(_ssm(jnp.flip(fx1, -1), xw2, dtw2, dtb2, Al2, Dv2, g2, be2), 1) + y1_
            out1 = y1.transpose(0, 2, 1).reshape(Bb, C, h1, w1)
            out = out1 * jax.nn.silu(z)
            return _conv1x1(out, out_w, out_b)
        key = jax.random.key(seed)
        ks = iter(jax.random.split(key, 64))

        def nrm(shape, s=0.05):
            return jax.random.normal(next(ks), shape, dtype=jnp.float32) * s
        inp = {'input_f': jax.random.normal(next(ks), (B, D_IN, H, W), dtype=jnp.float32), 'in_w': nrm((D_PROJ, D_IN)), 'in_b': nrm((D_PROJ,)), 'c1_w': nrm((D_INNER, D_INNER)), 'c1_b': nrm((D_INNER,)), 'c2_w': nrm((D_INNER, D_INNER, 2, 2)), 'c2_b': nrm((D_INNER,)), 'c3_w': nrm((D_INNER, D_INNER, 2, 2)), 'c3_b': nrm((D_INNER,)), 'out_w': nrm((D_IN, D_INNER)), 'out_b': nrm((D_IN,))}
        Al = jnp.log(jnp.tile(jnp.arange(1, N_STATE + 1, dtype=jnp.float32), (D_INNER, 1)))
        for i in (1, 2, 3):
            inp[f'xw{i}'] = nrm((R_DT + 2 * N_STATE, D_INNER))
            inp[f'dtw{i}'] = nrm((D_INNER, R_DT), s=R_DT ** (-0.5))
            inp[f'dtb{i}'] = nrm((D_INNER,)) - 4.0
            inp[f'Al{i}'] = Al
            inp[f'Dv{i}'] = jnp.ones((D_INNER,), jnp.float32)
            inp[f'g{i}'] = jnp.ones((D_INNER,), jnp.float32)
            inp[f'be{i}'] = jnp.zeros((D_INNER,), jnp.float32)
        return inp
    _L0_conv_all = _L0_conv_setup()
    _L0_conv_in = {k: v for k, v in _L0_conv_all.items() if k in ('in_w', 'in_b', 'c1_w', 'c1_b', 'c2_w', 'c2_b', 'c3_w', 'c3_b', 'out_w', 'out_b', 'xw1', 'dtw1', 'dtb1', 'Al1', 'Dv1', 'g1', 'be1', 'xw2', 'dtw2', 'dtb2', 'Al2', 'Dv2', 'g2', 'be2', 'xw3', 'dtw3', 'dtb3', 'Al3', 'Dv3', 'g3', 'be3', )}
    del _L0_conv_all

    def _L1_attn_setup():
        import jax, jax.numpy as jnp
        import numpy as np
        EMBED_DIM = 512
        NUM_HEADS = 8
        HEAD_DIM = EMBED_DIM // NUM_HEADS
        SCALE = HEAD_DIM ** (-0.5)
        key = jax.random.key(seed)
        ks = jax.random.split(key, 5)
        B, N, C = (4, 2048, EMBED_DIM)
        s = 0.02
        return {'x': jax.random.normal(ks[0], (B, N, C), jnp.float32), 'qkv_w': jax.random.normal(ks[1], (3 * C, C), jnp.float32) * s, 'qkv_b': jax.random.normal(ks[2], (3 * C,), jnp.float32) * s, 'proj_w': jax.random.normal(ks[3], (C, C), jnp.float32) * s, 'proj_b': jax.random.normal(ks[4], (C,), jnp.float32) * s}
    _L1_attn_all = _L1_attn_setup()
    _L1_attn_in = {k: v for k, v in _L1_attn_all.items() if k in ('qkv_w', 'qkv_b', 'proj_w', 'proj_b', )}
    del _L1_attn_all

    def _L1_ffn_setup():
        import jax, jax.numpy as jnp
        import numpy as np

        def _haar_dwt2(x):
            a = x[:, ::2, ::2]
            b = x[:, ::2, 1::2]
            c = x[:, 1::2, ::2]
            d = x[:, 1::2, 1::2]
            ll = (a + b + c + d) * 0.5
            lh = (a + b - c - d) * 0.5
            hl = (a - b + c - d) * 0.5
            hh = (a - b - c + d) * 0.5
            return (ll, lh, hl, hh)

        def _haar_idwt2(ll, lh, hl, hh):
            a = (ll + lh + hl + hh) * 0.5
            b = (ll + lh - hl - hh) * 0.5
            c = (ll - lh + hl - hh) * 0.5
            d = (ll - lh - hl + hh) * 0.5
            B, H2, W2 = ll.shape
            out = jnp.zeros((B, 2 * H2, 2 * W2), ll.dtype)
            out = out.at[:, ::2, ::2].set(a)
            out = out.at[:, ::2, 1::2].set(b)
            out = out.at[:, 1::2, ::2].set(c)
            out = out.at[:, 1::2, 1::2].set(d)
            return out

        def _interp_linear_last(x, m):
            n = x.shape[-1]
            pos = jnp.linspace(0.0, 1.0, m, dtype=x.dtype) * (n - 1)
            i0 = jnp.clip(jnp.floor(pos).astype(jnp.int32), 0, n - 2)
            w = pos - i0.astype(x.dtype)
            return x[..., i0] * (1.0 - w) + x[..., i0 + 1] * w
        key = jax.random.key(seed)
        k0, k1, k2 = jax.random.split(key, 3)
        b, f, c, hidden = (128, 256, 512, 2048)
        x = jax.random.normal(k0, (b, f, c), dtype=jnp.float32)
        fc1_w = jax.random.normal(k1, (hidden, c), dtype=jnp.float32) * 0.02
        fc1_b = jnp.zeros((hidden,), dtype=jnp.float32)
        fc2_w = jax.random.normal(k2, (c // 2, hidden), dtype=jnp.float32) * 0.02
        fc2_b = jnp.zeros((c // 2,), dtype=jnp.float32)
        return {'x': x, 'fc1_w': fc1_w, 'fc1_b': fc1_b, 'fc2_w': fc2_w, 'fc2_b': fc2_b}
    _L1_ffn_all = _L1_ffn_setup()
    _L1_ffn_in = {k: v for k, v in _L1_ffn_all.items() if k in ('fc1_w', 'fc1_b', 'fc2_w', 'fc2_b', )}
    del _L1_ffn_all

    return {
        "x": x,
        "L0_conv_in_w": _L0_conv_in["in_w"],
        "L0_conv_in_b": _L0_conv_in["in_b"],
        "L0_conv_c1_w": _L0_conv_in["c1_w"],
        "L0_conv_c1_b": _L0_conv_in["c1_b"],
        "L0_conv_c2_w": _L0_conv_in["c2_w"],
        "L0_conv_c2_b": _L0_conv_in["c2_b"],
        "L0_conv_c3_w": _L0_conv_in["c3_w"],
        "L0_conv_c3_b": _L0_conv_in["c3_b"],
        "L0_conv_out_w": _L0_conv_in["out_w"],
        "L0_conv_out_b": _L0_conv_in["out_b"],
        "L0_conv_xw1": _L0_conv_in["xw1"],
        "L0_conv_dtw1": _L0_conv_in["dtw1"],
        "L0_conv_dtb1": _L0_conv_in["dtb1"],
        "L0_conv_Al1": _L0_conv_in["Al1"],
        "L0_conv_Dv1": _L0_conv_in["Dv1"],
        "L0_conv_g1": _L0_conv_in["g1"],
        "L0_conv_be1": _L0_conv_in["be1"],
        "L0_conv_xw2": _L0_conv_in["xw2"],
        "L0_conv_dtw2": _L0_conv_in["dtw2"],
        "L0_conv_dtb2": _L0_conv_in["dtb2"],
        "L0_conv_Al2": _L0_conv_in["Al2"],
        "L0_conv_Dv2": _L0_conv_in["Dv2"],
        "L0_conv_g2": _L0_conv_in["g2"],
        "L0_conv_be2": _L0_conv_in["be2"],
        "L0_conv_xw3": _L0_conv_in["xw3"],
        "L0_conv_dtw3": _L0_conv_in["dtw3"],
        "L0_conv_dtb3": _L0_conv_in["dtb3"],
        "L0_conv_Al3": _L0_conv_in["Al3"],
        "L0_conv_Dv3": _L0_conv_in["Dv3"],
        "L0_conv_g3": _L0_conv_in["g3"],
        "L0_conv_be3": _L0_conv_in["be3"],
        "L1_attn_qkv_w": _L1_attn_in["qkv_w"],
        "L1_attn_qkv_b": _L1_attn_in["qkv_b"],
        "L1_attn_proj_w": _L1_attn_in["proj_w"],
        "L1_attn_proj_b": _L1_attn_in["proj_b"],
        "L1_ffn_fc1_w": _L1_ffn_in["fc1_w"],
        "L1_ffn_fc1_b": _L1_ffn_in["fc1_b"],
        "L1_ffn_fc2_w": _L1_ffn_in["fc2_w"],
        "L1_ffn_fc2_b": _L1_ffn_in["fc2_b"],
    }

def reference(x, L0_conv_in_w, L0_conv_in_b, L0_conv_c1_w, L0_conv_c1_b, L0_conv_c2_w, L0_conv_c2_b, L0_conv_c3_w, L0_conv_c3_b, L0_conv_out_w, L0_conv_out_b, L0_conv_xw1, L0_conv_dtw1, L0_conv_dtb1, L0_conv_Al1, L0_conv_Dv1, L0_conv_g1, L0_conv_be1, L0_conv_xw2, L0_conv_dtw2, L0_conv_dtb2, L0_conv_Al2, L0_conv_Dv2, L0_conv_g2, L0_conv_be2, L0_conv_xw3, L0_conv_dtw3, L0_conv_dtb3, L0_conv_Al3, L0_conv_Dv3, L0_conv_g3, L0_conv_be3, L1_attn_qkv_w, L1_attn_qkv_b, L1_attn_proj_w, L1_attn_proj_b, L1_ffn_fc1_w, L1_ffn_fc1_b, L1_ffn_fc2_w, L1_ffn_fc2_b):
    import jax
    import jax.numpy as jnp
    def _L0_conv_ref(input_f, in_w, in_b, c1_w, c1_b, c2_w, c2_b, c3_w, c3_b, out_w, out_b, xw1, dtw1, dtb1, Al1, Dv1, g1, be1, xw2, dtw2, dtb2, Al2, Dv2, g2, be2, xw3, dtw3, dtb3, Al3, Dv3, g3, be3):
        import jax, jax.numpy as jnp
        from jax import lax
        import numpy as np
        D_IN = 512
        HID = 128
        D_INNER = 2 * HID
        D_PROJ = 2 * D_INNER
        N_STATE = 16
        R_DT = 8
        B, H, W = (8, 32, 32)

        def _layernorm(y, g, b):
            mu = y.mean(-1, keepdims=True)
            var = ((y - mu) ** 2).mean(-1, keepdims=True)
            return (y - mu) / jnp.sqrt(var + 1e-05) * g + b

        def _ssm(x, xw, dtw, dtb, Al, Dv, g, be):
            Bb, D, L = x.shape
            n = Al.shape[1]
            xd = jnp.einsum('bdl,kd->blk', x, xw)
            dts = xd[..., :R_DT]
            Bs = xd[..., R_DT:R_DT + n]
            Cs = xd[..., R_DT + n:]
            delta = jax.nn.softplus(jnp.einsum('blr,dr->bld', dts, dtw) + dtb)
            A = -jnp.exp(Al)
            xt = x.transpose(0, 2, 1)
            dA = jnp.exp(delta[..., None] * A)
            dBx = delta[..., None] * Bs[:, :, None, :] * xt[..., None]

            def step(h, inp):
                da, dbx, c = inp
                h = h * da + dbx
                return (h, jnp.einsum('bdn,bn->bd', h, c))
            h0 = jnp.zeros((Bb, D, n), x.dtype)
            _, ys = lax.scan(step, h0, (dA.transpose(1, 0, 2, 3), dBx.transpose(1, 0, 2, 3), Cs.transpose(1, 0, 2)))
            y = ys.transpose(1, 0, 2) + xt * Dv
            return _layernorm(y, g, be)

        def _up2(y, h, w):
            Bb, L, C = y.shape
            img = y.transpose(0, 2, 1).reshape(Bb, C, h, w)
            img = jnp.repeat(jnp.repeat(img, 2, axis=2), 2, axis=3)
            return img.reshape(Bb, C, 4 * L).transpose(0, 2, 1)

        def _conv1x1(x, w, b):
            return jnp.einsum('bchw,oc->bohw', x, w) + b[None, :, None, None]

        def _conv2s2(x, w, b):
            out = lax.conv_general_dilated(x, w, (2, 2), 'VALID', dimension_numbers=('NCHW', 'OIHW', 'NCHW'))
            return out + b[None, :, None, None]

        def _forward(input_f, in_w, in_b, c1_w, c1_b, c2_w, c2_b, c3_w, c3_b, out_w, out_b, xw1, dtw1, dtb1, Al1, Dv1, g1, be1, xw2, dtw2, dtb2, Al2, Dv2, g2, be2, xw3, dtw3, dtb3, Al3, Dv3, g3, be3):
            xz = _conv1x1(input_f, in_w, in_b)
            x, z = jnp.split(xz, 2, axis=1)
            f1 = _conv1x1(x, c1_w, c1_b)
            f2 = _conv2s2(f1, c2_w, c2_b)
            f3 = _conv2s2(f2, c3_w, c3_b)
            Bb, C, h3, w3 = f3.shape
            fx3 = f3.reshape(Bb, C, h3 * w3)
            y3 = _ssm(fx3, xw3, dtw3, dtb3, Al3, Dv3, g3, be3) + jnp.flip(_ssm(jnp.flip(fx3, -1), xw3, dtw3, dtb3, Al3, Dv3, g3, be3), 1)
            y2_ = _up2(y3, h3, w3)
            _, _, h2, w2 = f2.shape
            fx2 = f2.reshape(Bb, C, h2 * w2)
            y2 = _ssm(fx2, xw2, dtw2, dtb2, Al2, Dv2, g2, be2) + jnp.flip(_ssm(jnp.flip(fx2, -1), xw2, dtw2, dtb2, Al2, Dv2, g2, be2), 1) + y2_
            y1_ = _up2(y2, h2, w2)
            _, _, h1, w1 = f1.shape
            fx1 = f1.reshape(Bb, C, h1 * w1)
            y1 = _ssm(fx1, xw1, dtw1, dtb1, Al1, Dv1, g1, be1) + jnp.flip(_ssm(jnp.flip(fx1, -1), xw2, dtw2, dtb2, Al2, Dv2, g2, be2), 1) + y1_
            out1 = y1.transpose(0, 2, 1).reshape(Bb, C, h1, w1)
            out = out1 * jax.nn.silu(z)
            return _conv1x1(out, out_w, out_b)
        return _forward(input_f, in_w, in_b, c1_w, c1_b, c2_w, c2_b, c3_w, c3_b, out_w, out_b, xw1, dtw1, dtb1, Al1, Dv1, g1, be1, xw2, dtw2, dtb2, Al2, Dv2, g2, be2, xw3, dtw3, dtb3, Al3, Dv3, g3, be3)

    def _L1_attn_ref(x, qkv_w, qkv_b, proj_w, proj_b):
        import jax, jax.numpy as jnp
        import numpy as np
        EMBED_DIM = 512
        NUM_HEADS = 8
        HEAD_DIM = EMBED_DIM // NUM_HEADS
        SCALE = HEAD_DIM ** (-0.5)
        B, N, C = x.shape
        H, D = (NUM_HEADS, HEAD_DIM)
        qkv = x @ qkv_w.T + qkv_b
        qkv = qkv.reshape(B, N, 3, H, D).transpose(2, 0, 3, 1, 4)
        q, k, v = (qkv[0], qkv[1], qkv[2])
        attn = jnp.einsum('bhnd,bhmd->bhnm', q, k) * SCALE
        attn = jax.nn.softmax(attn, axis=-1)
        out = jnp.einsum('bhnm,bhmd->bhnd', attn, v)
        out = out.transpose(0, 2, 1, 3).reshape(B, N, C)
        return out @ proj_w.T + proj_b

    def _L1_ffn_ref(x, fc1_w, fc1_b, fc2_w, fc2_b):
        import jax, jax.numpy as jnp
        import numpy as np

        def _haar_dwt2(x):
            a = x[:, ::2, ::2]
            b = x[:, ::2, 1::2]
            c = x[:, 1::2, ::2]
            d = x[:, 1::2, 1::2]
            ll = (a + b + c + d) * 0.5
            lh = (a + b - c - d) * 0.5
            hl = (a - b + c - d) * 0.5
            hh = (a - b - c + d) * 0.5
            return (ll, lh, hl, hh)

        def _haar_idwt2(ll, lh, hl, hh):
            a = (ll + lh + hl + hh) * 0.5
            b = (ll + lh - hl - hh) * 0.5
            c = (ll - lh + hl - hh) * 0.5
            d = (ll - lh - hl + hh) * 0.5
            B, H2, W2 = ll.shape
            out = jnp.zeros((B, 2 * H2, 2 * W2), ll.dtype)
            out = out.at[:, ::2, ::2].set(a)
            out = out.at[:, ::2, 1::2].set(b)
            out = out.at[:, 1::2, ::2].set(c)
            out = out.at[:, 1::2, 1::2].set(d)
            return out

        def _interp_linear_last(x, m):
            n = x.shape[-1]
            pos = jnp.linspace(0.0, 1.0, m, dtype=x.dtype) * (n - 1)
            i0 = jnp.clip(jnp.floor(pos).astype(jnp.int32), 0, n - 2)
            w = pos - i0.astype(x.dtype)
            return x[..., i0] * (1.0 - w) + x[..., i0 + 1] * w
        b, f, c = x.shape
        ll, lh, hl, hh = _haar_dwt2(x)
        ll_up = _interp_linear_last(ll, c)
        h = jax.nn.gelu(jnp.einsum('bfc,hc->bfh', ll_up, fc1_w) + fc1_b, approximate=False)
        ll_new = jnp.einsum('bfh,oh->bfo', h, fc2_w) + fc2_b
        return _haar_idwt2(ll_new, lh, hl, hh)

    def _gn(v, G=32, eps=1e-5):
        B_, C_, H_, W_ = v.shape
        g = v.reshape(B_, G, C_ // G, H_, W_)
        m = jnp.mean(g, axis=(2, 3, 4), keepdims=True)
        s = jnp.var(g, axis=(2, 3, 4), keepdims=True)
        return ((g - m) / jnp.sqrt(s + eps)).reshape(v.shape)

    def _ln_c(v, eps=1e-6):
        m = jnp.mean(v, axis=1, keepdims=True)
        s = jnp.var(v, axis=1, keepdims=True)
        return (v - m) / jnp.sqrt(s + eps)

    def _ln_t(v, eps=1e-5):
        m = jnp.mean(v, axis=-1, keepdims=True)
        s = jnp.var(v, axis=-1, keepdims=True)
        return (v - m) / jnp.sqrt(s + eps)

    def _to_tokens(v):
        B_, C_, H_, W_ = v.shape
        return v.reshape(B_, C_, H_ * W_).transpose(0, 2, 1)
    def _from_tokens(t, like):
        B_, C_, H_, W_ = like.shape
        return t.transpose(0, 2, 1).reshape(B_, C_, H_, W_)

    x = x + _L0_conv_ref(_gn(x), L0_conv_in_w, L0_conv_in_b, L0_conv_c1_w, L0_conv_c1_b, L0_conv_c2_w, L0_conv_c2_b, L0_conv_c3_w, L0_conv_c3_b, L0_conv_out_w, L0_conv_out_b, L0_conv_xw1, L0_conv_dtw1, L0_conv_dtb1, L0_conv_Al1, L0_conv_Dv1, L0_conv_g1, L0_conv_be1, L0_conv_xw2, L0_conv_dtw2, L0_conv_dtb2, L0_conv_Al2, L0_conv_Dv2, L0_conv_g2, L0_conv_be2, L0_conv_xw3, L0_conv_dtw3, L0_conv_dtb3, L0_conv_Al3, L0_conv_Dv3, L0_conv_g3, L0_conv_be3)
    t = _to_tokens(x)
    t = t + _L1_attn_ref(_ln_t(t), L1_attn_qkv_w, L1_attn_qkv_b, L1_attn_proj_w, L1_attn_proj_b)
    t = t + _L1_ffn_ref(_ln_t(t), L1_ffn_fc1_w, L1_ffn_fc1_b, L1_ffn_fc2_w, L1_ffn_fc2_b)
    x = _from_tokens(t, x)
    return x


_drawn_inputs = setup_inputs


def setup_inputs(seed=0):
    import zlib

    import numpy as np

    out = dict(_drawn_inputs(seed))
    spreads = {'L0_conv_Dv1': (1.0, 0.2),
     'L0_conv_g1': (1.0, 0.2),
     'L0_conv_be1': (0.0, 0.3),
     'L0_conv_Dv2': (1.0, 0.2),
     'L0_conv_g2': (1.0, 0.2),
     'L0_conv_be2': (0.0, 0.1),
     'L0_conv_Dv3': (1.0, 0.6),
     'L0_conv_g3': (1.0, 0.2),
     'L0_conv_be3': (0.0, 0.1),
     'L1_ffn_fc1_b': (0.0, 2.0),
     'L1_ffn_fc2_b': (0.0, 1.788)}
    factors = {'L0_conv_c3_b': 2.96,
     'L0_conv_dtb1': 64.0,
     'L0_conv_dtb2': 54.072,
     'L0_conv_dtb3': 37.28,
     'L1_attn_qkv_w': 8.0,
     'L1_attn_qkv_b': 8.0,
     'L1_attn_proj_w': 7.484,
     'L1_attn_proj_b': 31.986,
     'L0_conv_xw1': 8.0,
     'L0_conv_dtw1': 8.0,
     'L0_conv_xw2': 8.0,
     'L0_conv_dtw2': 8.0,
     'L0_conv_xw3': 8.0,
     'L0_conv_dtw3': 8.0,
     'L0_conv_Al3': 8.0,
     'L1_ffn_fc1_w': 6.057,
     'L0_conv_Al1': 8.0}
    for name, (base, spread) in spreads.items():
        noise = np.random.default_rng([zlib.crc32(name.encode()), seed]).standard_normal(out[name].shape)
        drawn = base * np.exp(spread * noise) if base else spread * noise
        out[name] = jnp.asarray(drawn.astype(out[name].dtype))
    for name, factor in factors.items():
        out[name] = (out[name] * factor).astype(out[name].dtype)
    return out
```

```python
from contextlib import ExitStack

import concourse.bass as bass
from concourse import mybir

ALU = mybir.AluOpType
ACT = mybir.ActivationFunctionType
AX_X = mybir.AxisListType.X
F32 = mybir.dt.float32
BF16 = mybir.dt.bfloat16

P = 128
BANK = 512
B = 8
C, CT = 512, 4
D, DT = 256, 2
L1, L2, L3 = 1024, 256, 64
N_STATE, R_DT = 16, 8
XD = 3 * 2 * N_STATE + R_DT
DT_ROW = 3 * 2 * N_STATE
HEADS, HD = 8, 64
PAIRS = HEADS // 2
KT = L1 // P
HID, HT = 2048, 16
LN_EPS = 1e-5
SCALE = HD ** -0.5
E_SMALL = 1 / 64

VEC = {}
_at = 0
for _name, _n in [("in_bx", 2), ("in_bz", 2), ("c1_b", 2), ("c2_b", 2), ("c3_b", 2), ("out_b", 4), ("q_b", 4), ("k_b", 4),
                  ("v_b", 4), ("proj_b", 4), ("fc1_b", 16), ("fc2_b", 2)] + \
        [(f"{v}{s}", 2) for s in (1, 2, 3) for v in ("dtb", "Dv", "g", "be")] + [(f"Al{s}", 32) for s in (1, 2, 3)]:
    VEC[_name] = (_at, _n)
    _at += _n
N_VEC = _at


class Signal:

    def __init__(self, sem, per_image):
        self.sem, self.per_image = sem, per_image

    def __call__(self, k):
        assert 0 < k <= self.per_image
        return self.sem, k


class Group:

    def __init__(self, level, params, dirs, c0, n, first, keep_state, banks):
        self.level, self.params, self.dirs, self.c0, self.n = level, params, dirs, c0, n
        self.first, self.keep_state, self.banks = first, keep_state, banks
        self.streams = [(half, d) for half in range(DT) for d in dirs]


GROUPS = [
    Group(3, 3, (0, 1), 0, L3, True, False, (4, 5, 6, 7)),
    Group(2, 2, (0, 1), 0, L2, True, False, (4, 5, 6, 7)),
    Group(1, 1, (0,), 0, BANK, True, True, (4, 5)),
    Group(1, 1, (0,), BANK, BANK, False, False, (6, 7)),
    Group(1, 2, (1,), BANK, BANK, True, True, (4, 5)),
    Group(1, 2, (1,), 0, BANK, False, False, (6, 7)),
]
PREPS = {0: (3, 3, [(0, L3)]), 1: (2, 2, [(0, L2)]), 2: (1, 1, [(0, BANK), (BANK, BANK)]), 4: (1, 2, [(0, BANK), (BANK, BANK)])}
N_UNITS = len(GROUPS) * N_STATE
N_CHUNKS = sum(len(p[2]) for p in PREPS.values())
N_STREAMS = sum(len(g.streams) for g in GROUPS) * N_STATE
N_NORMS = sum(len(g.dirs) for g in GROUPS)
PIX = {1: L1, 2: L2, 3: L3}


def build(nc, t):
    with ExitStack() as ctx:
        def sb(name, shape, dt=F32):
            return ctx.enter_context(nc.sbuf_tensor(name, shape, dt))

        signals = []

        def signal(name, per_image):
            signals.append(Signal(ctx.enter_context(nc.semaphore(name)), per_image))
            return signals[-1]

        def sem(name):
            return ctx.enter_context(nc.semaphore(name))

        wf = sb("wf", [P, CT, D])
        wz = sb("wz", [P, CT, D])
        wout = sb("wout", [P, DT, C])
        xw = {s: sb(f"xw{s}", [P, DT, XD]) for s in (1, 2, 3)}
        dtw = {s: sb(f"dtw{s}", [P, D]) for s in (1, 2, 3)}
        wqkv = sb("wqkv", [P, CT, 3 * C])
        wproj = sb("wproj", [P, CT, C])
        w1 = sb("w1", [P, DT, HID])
        w2 = sb("w2", [P, HT, D])
        vecs = sb("vecs", [P, N_VEC])
        ident = sb("ident", [P, P])
        gmat = sb("gmat", [P, P])
        ones = sb("ones", [P, P])
        ones_c = sb("ones_c", [P, P])
        ones_d = sb("ones_d", [P, P])
        zero_b = sb("zero_b", [P, 1])
        eps_b = sb("eps_b", [P, 1])
        one_b = sb("one_b", [P, 1])
        sel = sb("sel", [96, 2 * N_STATE, P], BF16)
        neg = sb("neg", [P, P], BF16)
        mask8 = sb("mask8", [P, KT])
        f1_b = sb("f1_b", [P, DT])
        o_b = sb("o_b", [P, CT])
        small = sb("small", [P, 96])
        gn_stats = small[:, 0:48].rearrange("p (c j s) -> p c j s", c=CT, j=2)
        gn_mv = small[:, 48:56].rearrange("p (c s) -> p c s", c=CT)
        gn_d, gn_sq, gn_m = small[:, 56:60], small[:, 60:64], small[:, 64:66]
        gn_r = small[:, 84:86]
        maxima = sb("maxima", [P, 2, 64])
        rows = sb("rows", [P, P], BF16)

        arena = sb("arena", [P, 27600])
        taken = [0]

        def region(at, shape, dt=F32):
            n = 1
            for s in shape:
                n *= s
            words = n if dt == F32 else n // 2
            taken[0] = max(taken[0], at + words)
            a = arena[:, at:at + words]
            if dt != F32:
                a = a.bitcast(dt)
            if len(shape) == 2:
                a = a.rearrange("p (a b) -> p a b", a=shape[0])
            elif len(shape) == 3:
                a = a.rearrange("p (a b c) -> p a b c", a=shape[0], b=shape[1])
            return a

        T = region(0, [CT, L1])
        XN = region(4096, [CT, L1])
        C2 = region(8192, [DT, 4, D])
        C3 = region(10240, [DT, 4, D])
        F1 = region(12288, [DT, L1])
        F2 = region(14336, [DT, L2])
        F3 = region(14848, [DT, L3])
        Z = region(14976, [DT, L1])
        Y1 = region(17024, [DT, L1])
        Y2 = region(19072, [DT, L2])
        Y3 = region(19584, [DT, L3])
        ZE = region(19712, [DT, L1])
        F = {1: F1, 2: F2, 3: F3}
        Y = {1: Y1, 2: Y2, 3: Y3}
        DELTA = region(4096, [DT, L1])
        DU = region(6144, [DT, L1])
        SPL = region(8192, [L1], BF16)
        SPLR = region(8704, [BANK])
        SPLT = region(9216, [BANK], BF16)
        DTS = region(9472, [BANK])
        SPA = region(9984, [DT, BANK])
        SPM = region(11008, [DT, BANK])
        SPE = region(19712, [DT, BANK])
        SPP = region(20736, [DT, BANK])
        DBX = region(19712, [DT, BANK])
        H = region(20736, [4, BANK])
        HC = region(22784, [4, BANK])
        CB = region(24832, [2, BANK])
        LY = region(25856, [DT, BANK])
        LR = region(26880, [BANK])
        STATE = region(27392, [DT, N_STATE])
        TN = region(4096, [CT, L1])
        QK = region(8192, [2, 2, L1])
        V = region(12288, [KT, C])
        PR = region(16384, [4, L1])
        O = region(20480, [CT, L1])
        DEN = region(24576, [2, L1])
        RH = region(26624, [KT, P], BF16)
        LSQ = region(20480, [2, BANK])
        LRS = region(21504, [BANK])
        LL = region(8192, [DT, BANK])
        LS = region(9216, [DT, L1])
        HM = region(11264, [HT, BANK])
        DL = region(19456, [DT, BANK])
        S_INW = region(0, [DT, C])
        S_C1 = region(1024, [DT, D])
        S_U = region(1536, [CT, D])
        S_FC1 = region(2560, [CT, HID])
        S_SEL = region(10752, [2 * N_STATE, P])
        S_NEG = region(14848, [P])
        assert taken[0] <= 27600

        ps = ctx.enter_context(nc.psum_tensor("ps", [P, 8, BANK], F32))

        def vec(name, i, rows=slice(0, P)):
            a = VEC[name][0] + i
            return vecs[rows, a:a + 1]

        weights_in = sem("weights_in")
        consts_set = sem("consts_set")
        setup_pe = sem("setup_pe")
        setup_act = sem("setup_act")
        setup_dve = sem("setup_dve")

        x_in = signal("x_in", 32)
        c23_in = signal("c23_in", 32)
        stored = signal("stored", 32)
        gn_dve = signal("gn_dve", 8 + 4 + 3 + 1 + 4)
        gn_pe = signal("gn_pe", 2)
        gn_act = signal("gn_act", 2)
        conv_pe = signal("conv_pe", 8 + 4)
        conv_act = signal("conv_act", 4 + 4 + 4 + 2)
        conv_dve = signal("conv_dve", 6)
        prep_pe = signal("prep_pe", 2 * N_CHUNKS)
        prep_act = signal("prep_act", 9 * N_CHUNKS)
        prep_dve = signal("prep_dve", 21 * N_CHUNKS)
        b_rows = signal("b_rows", N_UNITS)
        c_rows = signal("c_rows", N_UNITS)
        c_kept = signal("c_kept", N_UNITS)
        decay = signal("decay", DT * N_UNITS)
        driven = signal("driven", DT * N_UNITS)
        scanned = signal("scanned", N_STREAMS)
        state_kept = signal("state_kept", DT * N_STATE * 2)
        weighed = signal("weighed", N_STREAMS)
        summed = signal("summed", N_STREAMS)
        ln_pe = signal("ln_pe", 2 * N_NORMS)
        ln_act = signal("ln_act", 4 * N_NORMS)
        ln_dve = signal("ln_dve", 8 * N_NORMS)
        y_start = signal("y_start", 1 + 4 + 4)
        gated = signal("gated", 2)
        out_pe = signal("out_pe", 8)
        out_dve = signal("out_dve", 8)
        tn_pe = signal("tn_pe", 4)
        tn_sq = signal("tn_sq", 4 * 2)
        tn_dve = signal("tn_dve", 4 * 8)
        tn_act = signal("tn_act", 4 * 6)
        v_pe = signal("v_pe", KT)
        v_act = signal("v_act", KT)
        qk_pe = signal("qk_pe", 4 * PAIRS)
        qk_kept = signal("qk_kept", 4 * PAIRS)
        smax_pe = signal("smax_pe", 2 * KT * PAIRS)
        smax_dve = signal("smax_dve", 2 * KT * PAIRS)
        mt_dve = signal("mt_dve", 5 * PAIRS)
        mt_pe = signal("mt_pe", PAIRS)
        s_pe = signal("s_pe", 2 * KT * PAIRS)
        s_exp = signal("s_exp", 2 * KT * PAIRS)
        pv_pe = signal("pv_pe", KT * PAIRS)
        den_pool = signal("den_pool", 2 * (KT - 1) * PAIRS)
        den_pe = signal("den_pe", 2 * PAIRS)
        o_dve = signal("o_dve", 4 * PAIRS)
        proj_pe = signal("proj_pe", 8)
        proj_dve = signal("proj_dve", 8)
        ll_dve = signal("ll_dve", 6)
        fc1_pe = signal("fc1_pe", HT)
        fc1_act = signal("fc1_act", HT)
        fc2_pe = signal("fc2_pe", 2)
        fin_dve = signal("fin_dve", 4 + 8)

        def halves(n):
            return [(j, slice(BANK * j, BANK * j + BANK)) for j in range(n // BANK)]

        SETUP_DVE, SETUP_ACT, SETUP_PE, CONSTS = 4, 9, 10, 9
        W_ALL = 16 * 21

        with nc.Block() as block:
            @block.sync
            def _(sp):
                for dst, src in [
                    (S_INW, t["in_x"]), (S_C1, t["c1"]), (S_U, t["up"]), (S_FC1, t["fc1"]), (vecs[:], t["vecs"]), (ident[:], t["ident"]),
                    (gmat[:], t["gmat"]), (S_SEL[0:96], t["sel"]), (S_NEG, t["neg"]), (mask8[:], t["mask8"]),
                    (wz[:], t["in_z"]), (wout[:], t["out"]), (wqkv[:], t["qkv"]), (wproj[:], t["proj"]), (w2[:], t["fc2"]),
                    (xw[1][:], t["xw1"]), (xw[2][:], t["xw2"]), (xw[3][:], t["xw3"]),
                    (dtw[1][DT_ROW:DT_ROW + R_DT, :], t["dtw1"]), (dtw[2][DT_ROW:DT_ROW + R_DT, :], t["dtw2"]),
                    (dtw[3][DT_ROW:DT_ROW + R_DT, :], t["dtw3"]),
                ]:
                    sp.dma_start(dst, src).then_inc(weights_in, 16)
                sp.wait_ge(setup_dve, SETUP_DVE)
                sp.wait_ge(setup_act, SETUP_ACT)
                sp.wait_ge(setup_pe, SETUP_PE)
            @block.tensor
            def _(pe):
                pe.wait_ge(weights_in, W_ALL)
                for ct in range(CT):
                    for m in range(DT):
                        mm = pe.matmul(ps[:, ct, 0:D], S_INW[:, m, P * ct:P * ct + P], S_C1[:, m, :], start=m == 0, stop=m == DT - 1)
                mm.then_inc(setup_pe, 1)
                for o in range(DT):
                    for m in range(DT):
                        pe.matmul(ps[:, 4, o:o + 1], S_C1[:, m, P * o:P * o + P], vec("in_bx", m), start=m == 0, stop=m == DT - 1)
                for o in range(CT):
                    for m in range(CT):
                        mm = pe.matmul(ps[:, 4, 2 + o:3 + o], wproj[:, m, P * o:P * o + P], vec("v_b", m), start=m == 0, stop=m == CT - 1)
                mm.then_inc(setup_pe, 1)
                pe.wait_ge(setup_dve, 1 + 1)
                for j in range(DT):
                    for h in range(4):
                        if j == 1 and h == 0:
                            pe.wait_ge(setup_act, 4)
                        for ct in range(CT):
                            mm = pe.matmul(ps[:, h, :], S_U[:, ct, P * j:P * j + P], S_FC1[:, ct, BANK * h:BANK * h + BANK],
                                           start=ct == 0, stop=ct == CT - 1)
                        mm.then_inc(setup_pe, 1)
                pe.wait_ge(consts_set, CONSTS)

            @block.scalar
            def _(act):
                act.wait_ge(weights_in, W_ALL)
                act.wait_ge(consts_set, CONSTS)
                for h in range(4):
                    act.wait_ge(setup_pe, 3 + h)
                    nc.scalar.activation(w1[:, 0, BANK * h:BANK * h + BANK], ps[:, h, :], ACT.Copy).then_inc(setup_act, 1)
                for h in range(4):
                    act.wait_ge(setup_pe, 7 + h)
                    nc.scalar.activation(w1[:, 1, BANK * h:BANK * h + BANK], ps[:, h, :], ACT.Copy).then_inc(setup_act, 1)
                a, n = VEC["Al1"][0], 96
                nc.scalar.activation(vecs[:, a:a + n], vecs[:, a:a + n], ACT.Exp, bias=zero_b[:]).then_inc(setup_act, 1)

            @block.vector
            def _(dve):
                nc.vector.memset(ones[:], 1.0).then_inc(consts_set, 1)
                nc.vector.memset(ones_c[:], 1.0 / C).then_inc(consts_set, 1)
                nc.vector.memset(ones_d[:], 1.0 / D).then_inc(consts_set, 1)
                nc.vector.memset(zero_b[:], 0.0).then_inc(consts_set, 1)
                nc.vector.memset(eps_b[:], LN_EPS).then_inc(consts_set, 1)
                nc.vector.memset(one_b[:], 1.0).then_inc(consts_set, 1)
                dve.wait_ge(weights_in, W_ALL)
                nc.vector.tensor_copy(sel[:], S_SEL[0:96]).then_inc(consts_set, 1)
                nc.vector.tensor_copy(neg[:], S_NEG).then_inc(consts_set, 1)
                nc.vector.memset(maxima[:], 0.0).then_inc(consts_set, 1)
                dve.wait_ge(setup_pe, 1)
                nc.vector.tensor_copy(wf[:], ps[:, 0:4, 0:D]).then_inc(setup_dve, 1)
                dve.wait_ge(setup_pe, 2)
                a = VEC["c1_b"][0]
                nc.vector.tensor_tensor(f1_b[:], ps[:, 4, 0:2], vecs[:, a:a + 2], ALU.add).then_inc(setup_dve, 1)
                a = VEC["proj_b"][0]
                nc.vector.tensor_tensor(o_b[:], ps[:, 4, 2:6], vecs[:, a:a + 4], ALU.add).then_inc(setup_dve, 1)
                dve.wait_ge(setup_act, SETUP_ACT)
                a = VEC["Al1"][0]
                nc.vector.tensor_scalar(vecs[:, a:a + 96], vecs[:, a:a + 96], -1.0, None, ALU.mult).then_inc(setup_dve, 1)
                dve.wait_ge(setup_dve, SETUP_DVE)


        with nc.Fori(0, B) as b:
            with nc.Block() as block:
                @block.sync
                def _(sp):
                    for two in range(2):
                        sp.dma_start(T[:, 2 * two:2 * two + 2, :], t["x"][b].rearrange("(j p two) l -> two p j l", p=P, two=2)[two]).then_inc(x_in.sem, 16)
                    sp.dma_start(C2, t["c2"]).then_inc(c23_in.sem, 16)
                    sp.dma_start(C3, t["c3"]).then_inc(c23_in.sem, 16)
                    sp.wait_ge(*fin_dve(12))
                    for two in range(2):
                        sp.dma_start(t["y"][b].rearrange("(j p two) l -> two p j l", p=P, two=2)[two], T[:, 2 * two:2 * two + 2, :]).then_inc(stored.sem, 16)
                    sp.wait_ge(*stored(32))

                @block.tensor
                def _(pe):
                    for k in range(2):
                        pe.wait_ge(*gn_dve((12, 15)[k]))
                        src = (gn_mv[:, :, 0], gn_sq)[k]
                        pe.matmul(ps[:, k, 0:2], gmat[:], src[:, 0:2], start=True, stop=False)
                        pe.matmul(ps[:, k, 0:2], gmat[:], src[:, 2:4], start=False, stop=True).then_inc(gn_pe.sem, 1)
                    pe.wait_ge(*gn_dve(20))
                    for k, w in enumerate((wf, wz)):
                        for o in range(DT):
                            for j, cs in halves(L1):
                                n = k * 4 + o * 2 + j
                                for ct in range(CT):
                                    mm = pe.matmul(ps[:, n, :], w[:, ct, P * o:P * o + P], XN[:, ct, cs], start=ct == 0, stop=ct == CT - 1)
                                mm.then_inc(conv_pe.sem, 1)
                    pe.wait_ge(*c23_in(32))
                    for k, (w, src, side) in enumerate([(C2, F1, 32), (C3, F2, 16)]):
                        pe.wait_ge(*conv_act((8, 10)[k]))
                        n = side * side // 4
                        for o in range(DT):
                            for ci in range(DT):
                                v = src[:, ci, :].rearrange("p (h a w c) -> p h a w c", h=side // 2, a=2, c=2)
                                for q in range(4):
                                    mm = pe.matmul(ps[:, 2 * k + o, 0:n], w[:, ci, q, P * o:P * o + P], v[:, :, q // 2, :, q % 2],
                                                   start=ci == 0 and q == 0, stop=ci == DT - 1 and q == 3)
                            mm.then_inc(conv_pe.sem, 1)

                    unit = 0
                    stream = 0
                    chunk = 0
                    norm = 0

                    def sum_states(g, streams, n, first_stream):
                        for i, (half, d) in enumerate(g.streams):
                            s = first_stream + i
                            pe.wait_ge(*weighed(s + 1))
                            pe.matmul(ps[:, g.banks[i], 0:g.n], ident[:], HC[:, s % 4, 0:g.n], start=n == 0, stop=n == N_STATE - 1)\
                                .then_inc(summed.sem, 1)

                    for gi, g in enumerate(GROUPS):
                        if gi in PREPS:
                            level, prm, chunks = PREPS[gi]
                            for c0, n in chunks:
                                if chunk == 0:
                                    pe.wait_ge(*conv_act(12))
                                else:
                                    pe.wait_ge(*prep_dve(21 * chunk))
                                if unit:
                                    pe.wait_ge(*driven(2 * unit))
                                for m in range(DT):
                                    mm = pe.matmul(ps[0:XD, 0, 0:n], xw[prm][:, m, :], F[level][:, m, c0:c0 + n], start=m == 0, stop=m == DT - 1)
                                mm.then_inc(prep_pe.sem, 1)
                                if unit:
                                    pe.wait_ge(*scanned(stream))
                                pe.wait_ge(*prep_dve(21 * chunk + 2))
                                for o in range(DT):
                                    mm = pe.matmul(ps[:, 2 + o, 0:n], dtw[prm][DT_ROW:DT_ROW + R_DT, P * o:P * o + P],
                                                   DTS[DT_ROW:DT_ROW + R_DT, 0:n], start=True, stop=True)
                                mm.then_inc(prep_pe.sem, 1)
                                chunk += 1
                        for n in range(N_STATE):
                            if n == 0 and gi in PREPS:
                                pe.wait_ge(*prep_dve(21 * chunk))
                            if n > 0 or gi not in PREPS:
                                pe.wait_ge(*driven(2 * unit))
                            pe.matmul(ps[:, 0, 0:g.n], sel[:, n, :], SPL[0:96, g.c0:g.c0 + g.n], start=True, stop=True).then_inc(b_rows.sem, 1)
                            if unit:
                                pe.wait_ge(*c_kept(unit))
                            pe.matmul(ps[:, 1, 0:g.n], sel[:, N_STATE + n, :], SPL[0:96, g.c0:g.c0 + g.n], start=True, stop=True)\
                                .then_inc(c_rows.sem, 1)
                            if n > 0:
                                sum_states(g, g.streams, n - 1, stream - len(g.streams))
                            unit += 1
                            stream += len(g.streams)
                        sum_states(g, g.streams, N_STATE - 1, stream - len(g.streams))
                        for i, d in enumerate(g.dirs):
                            banks = [g.banks[k] for k, s in enumerate(g.streams) if s[1] == d]
                            pe.wait_ge(*ln_dve(8 * norm + 2))
                            for h in range(DT):
                                mm = pe.matmul(ps[:, banks[0], 0:g.n], ones_d[:], LY[:, h, 0:g.n], start=h == 0, stop=h == DT - 1)
                            mm.then_inc(ln_pe.sem, 1)
                            pe.wait_ge(*ln_act(4 * norm + 2))
                            for h in range(DT):
                                mm = pe.matmul(ps[:, banks[1], 0:g.n], ones_d[:], SPM[:, h, 0:g.n], start=h == 0, stop=h == DT - 1)
                            mm.then_inc(ln_pe.sem, 1)
                            norm += 1

                    pe.wait_ge(*gated(2))
                    for ct in range(CT):
                        for j, cs in halves(L1):
                            n = ct * 2 + j
                            for m in range(DT):
                                mm = pe.matmul(ps[:, n, :], wout[:, m, P * ct:P * ct + P], Y1[:, m, cs], start=m == 0, stop=m == DT - 1)
                            mm.then_inc(out_pe.sem, 1)

                    def token_norm(which):
                        for j, cs in halves(L1):
                            k = which * 2 + j
                            if which == 0:
                                pe.wait_ge(*out_dve(8))
                            else:
                                pe.wait_ge(*proj_dve(8))
                            for ct in range(CT):
                                mm = pe.matmul(ps[:, 2 * j, :], ones_c[:], T[:, ct, cs], start=ct == 0, stop=ct == CT - 1)
                            mm.then_inc(tn_pe.sem, 1)
                            for ct in range(CT):
                                pe.wait_ge(*tn_act(6 * k + ct + 1))
                                mm = pe.matmul(ps[:, 2 * j + 1, :], ones_c[:], LSQ[:, ct % 2, :], start=ct == 0, stop=ct == CT - 1)
                                if ct in (1, 3):
                                    mm.then_inc(tn_sq.sem, 1)

                    token_norm(0)

                    pe.wait_ge(*tn_dve(16))
                    for kt in range(KT):
                        if kt >= 6:
                            pe.wait_ge(*v_act(kt - 5))
                        for ct in range(CT):
                            mm = pe.matmul(ps[:, kt % 6, :], TN[:, ct, P * kt:P * kt + P], wqkv[:, ct, 2 * C:3 * C], start=ct == 0, stop=ct == CT - 1)
                        mm.then_inc(v_pe.sem, 1)

                    for c in range(PAIRS):
                        for i in range(2):
                            for j, cs in halves(L1):
                                n = 2 * i + j
                                if c == 0:
                                    pe.wait_ge(*v_act(KT))
                                elif n == 0:
                                    pe.wait_ge(*s_exp(16 * c))
                                    pe.wait_ge(*o_dve(4 * c))
                                for ct in range(CT):
                                    mm = pe.matmul(ps[:, n, :], wqkv[:, ct, C * i + P * c:C * i + P * c + P], TN[:, ct, cs],
                                                   start=ct == 0, stop=ct == CT - 1)
                                mm.then_inc(qk_pe.sem, 1)
                        q, k = QK[:, c % 2, 0, :], QK[:, c % 2, 1, :]
                        pe.wait_ge(*qk_kept(4 * c + 4))
                        for qt in range(KT):
                            for e in range(2):
                                i = 16 * c + 2 * qt + e
                                slot = i % 3
                                if i % 16 >= 3:
                                    pe.wait_ge(*smax_dve(i - 2))
                                for j, cs in halves(L1):
                                    mm = pe.matmul(ps[:, 2 * slot + j, :], q[64 * e:64 * e + 64, P * qt:P * qt + P], k[64 * e:64 * e + 64, cs],
                                                   start=True, stop=True)
                                mm.then_inc(smax_pe.sem, 1)
                        pe.wait_ge(*mt_dve(5 * c + 1))
                        pe.transpose(ps[:, 6, 0:P], maxima[:].rearrange("p e m -> p (e m)"), ident[:]).then_inc(mt_pe.sem, 1)
                        pe.wait_ge(*mt_dve(5 * c + 5))
                        for kt in range(KT + 1):
                            if kt < KT:
                                for e in range(2):
                                    i = 16 * c + 2 * kt + e
                                    slot = i % 3
                                    if kt * 2 + e < 3:
                                        pe.wait_ge(*smax_dve(16 * c + 16))
                                    else:
                                        pe.wait_ge(*s_exp(i - 2))
                                    for j, cs in halves(L1):
                                        pe.matmul(ps[:, 2 * slot + j, :], k[64 * e:64 * e + 64, P * kt:P * kt + P], q[64 * e:64 * e + 64, cs],
                                                  start=True, stop=False)
                                    for j, cs in halves(L1):
                                        mm = pe.matmul(ps[:, 2 * slot + j, :], neg[64 * e:64 * e + 64, :], RH[64 * e:64 * e + 64, 4 * j:4 * j + 4, :], start=False, stop=True)
                                    mm.then_inc(s_pe.sem, 1)
                            if kt > 0:
                                pk = kt - 1
                                pe.wait_ge(*s_exp(16 * c + 2 * pk + 2))
                                for j, cs in halves(L1):
                                    for e in range(2):
                                        h = 2 * c + e
                                        mm = pe.matmul(ps[64 * e:64 * e + 64, 6 + j, :], V[:, pk, HD * h:HD * h + HD],
                                                       PR[:, (2 * pk + e) % 4, cs], start=pk == 0, stop=pk == KT - 1)
                                mm.then_inc(pv_pe.sem, 1)
                        for j, cs in halves(L1):
                            if j == 0:
                                pe.wait_ge(*den_pool(14 * c + 14))
                                pe.wait_ge(*s_exp(16 * c + 16))
                            for e in range(2):
                                mm = pe.matmul(ps[64 * e:64 * e + 64, j, :], ones[:, 0:64], DEN[:, e, cs], start=True, stop=True)
                            mm.then_inc(den_pe.sem, 1)

                    pe.wait_ge(*o_dve(4 * PAIRS))
                    for ct in range(CT):
                        for j, cs in halves(L1):
                            for m in range(CT):
                                mm = pe.matmul(ps[:, ct * 2 + j, :], wproj[:, m, P * ct:P * ct + P], O[:, m, cs], start=m == 0, stop=m == CT - 1)
                            mm.then_inc(proj_pe.sem, 1)

                    token_norm(1)

                    pe.wait_ge(*ll_dve(6))
                    for ht in range(HT):
                        if ht >= 6:
                            pe.wait_ge(*fc1_act(ht - 5))
                        elif ht == 0:
                            pe.wait_ge(*tn_dve(32))
                        for j in range(DT):
                            mm = pe.matmul(ps[:, ht % 6, :], w1[:, j, P * ht:P * ht + P], LL[:, j, :], start=j == 0, stop=j == DT - 1)
                        mm.then_inc(fc1_pe.sem, 1)
                    for o in range(DT):
                        for ht in range(HT):
                            if o == 0:
                                pe.wait_ge(*fc1_act(ht + 1))
                            mm = pe.matmul(ps[:, 6 + o, :], w2[:, ht, P * o:P * o + P], HM[:, ht, :], start=ht == 0, stop=ht == HT - 1)
                        mm.then_inc(fc2_pe.sem, 1)

                @block.scalar
                def _(act):
                    act.wait_ge(*gn_pe(2))
                    nc.scalar.activation(small[:, 80:82], ps[:, 1, 0:2], ACT.Ln, bias=eps_b[:]).then_inc(gn_act.sem, 1)
                    act.wait_ge(*gn_act(1))
                    nc.scalar.activation(gn_r, small[:, 80:82], ACT.Exp, bias=zero_b[:], scale=-0.5).then_inc(gn_act.sem, 1)
                    for k, (dst, bias) in enumerate([(F1, f1_b), (Z, None)]):
                        for o in range(DT):
                            for j, cs in halves(L1):
                                n = k * 4 + o * 2 + j
                                act.wait_ge(*conv_pe(n + 1))
                                bb = f1_b[:, o:o + 1] if k == 0 else vec("in_bz", o)
                                nc.scalar.activation(dst[:, o, cs], ps[:, n, :], ACT.Identity, bias=bb).then_inc(conv_act.sem, 1)
                    for k, (dst, n, name) in enumerate([(F2, L2, "c2_b"), (F3, L3, "c3_b")]):
                        for o in range(DT):
                            act.wait_ge(*conv_pe(8 + 2 * k + o + 1))
                            nc.scalar.activation(dst[:, o, :], ps[:, 2 * k + o, 0:n], ACT.Identity, bias=vec(name, o)).then_inc(conv_act.sem, 1)
                    act.wait_ge(*conv_act(8))
                    for o in range(DT):
                        nc.scalar.activation(ZE[:, o, :], Z[:, o, :], ACT.Exp, bias=zero_b[:], scale=-1.0).then_inc(conv_act.sem, 1)

                    unit = 0
                    stream = 0
                    chunk = 0
                    norm = 0
                    for gi, g in enumerate(GROUPS):
                        if gi in PREPS:
                            level, prm, chunks = PREPS[gi]
                            for c0, n in chunks:
                                k = 9 * chunk
                                act.wait_ge(*prep_pe(2 * chunk + 1))
                                if unit:
                                    act.wait_ge(*summed(stream))
                                nc.scalar.activation(SPL[0:96, c0:c0 + n], ps[0:96, 0, 0:n], ACT.Copy).then_inc(prep_act.sem, 1)
                                act.wait_ge(*prep_dve(21 * chunk + 1))
                                nc.scalar.activation(SPL[32:64, c0:c0 + n], SPLR[32:64, 0:n], ACT.Copy).then_inc(prep_act.sem, 1)
                                nc.scalar.activation(SPLT[64:96, 0:n], SPLR[64:96, 0:n], ACT.Copy).then_inc(prep_act.sem, 1)
                                act.wait_ge(*prep_pe(2 * chunk + 2))
                                for o in range(DT):
                                    nc.scalar.activation(SPA[:, o, 0:n], ps[:, 2 + o, 0:n], ACT.Abs, bias=vec(f"dtb{prm}", o)).then_inc(prep_act.sem, 1)
                                for o in range(DT):
                                    act.wait_ge(*prep_act(k + 4 + o))
                                    nc.scalar.activation(SPA[:, o, 0:n], SPA[:, o, 0:n], ACT.Exp, bias=zero_b[:], scale=-1.0).then_inc(prep_act.sem, 1)
                                for o in range(DT):
                                    act.wait_ge(*prep_act(k + 6 + o))
                                    if unit == 0:
                                        act.wait_ge(*conv_dve(6))
                                    nc.scalar.activation(SPE[:, o, 0:n], SPA[:, o, 0:n], ACT.Ln, bias=one_b[:]).then_inc(prep_act.sem, 1)
                                chunk += 1
                            act.wait_ge(*prep_dve(21 * chunk))
                        a0 = VEC[f"Al{g.params}"][0]
                        per = len(g.dirs)
                        for n in range(N_STATE):
                            act.wait_ge(*c_rows(unit + 1))
                            if unit >= 2:
                                before = stream - len(g.streams) if n >= 1 else stream - len(GROUPS[gi - 1].streams)
                                act.wait_ge(*weighed(before))
                            nc.scalar.activation(CB[:, unit % 2, 0:g.n], ps[:, 1, 0:g.n], ACT.Copy).then_inc(c_kept.sem, 1)
                            for half in range(DT):
                                if n > 0:
                                    act.wait_ge(*scanned(stream - len(g.streams) + per * (half + 1)))
                                nc.scalar.activation(ps[:, 2 + half, 0:g.n], DELTA[:, half, g.c0:g.c0 + g.n], ACT.Exp, bias=zero_b[:],
                                                     scale=vecs[:, a0 + 16 * half + n:a0 + 16 * half + n + 1]).then_inc(decay.sem, 1)
                            unit += 1
                            stream += len(g.streams)
                        for d in g.dirs:
                            k = 4 * norm
                            banks = [g.banks[i] for i, s in enumerate(g.streams) if s[1] == d]
                            for h in range(DT):
                                act.wait_ge(*ln_dve(8 * norm + 3 + h))
                                nc.scalar.activation(SPM[:, h, 0:g.n], LY[:, h, 0:g.n], ACT.Square, bias=zero_b[:]).then_inc(ln_act.sem, 1)
                            act.wait_ge(*ln_pe(2 * norm + 2))
                            nc.scalar.activation(LR[:, 0:g.n], ps[:, banks[1], 0:g.n], ACT.Ln, bias=eps_b[:]).then_inc(ln_act.sem, 1)
                            act.wait_ge(*ln_act(k + 3))
                            nc.scalar.activation(LR[:, 0:g.n], LR[:, 0:g.n], ACT.Exp, bias=zero_b[:], scale=-0.5).then_inc(ln_act.sem, 1)
                            norm += 1
                        if gi in (0, 1):
                            act.wait_ge(*ln_dve(8 * norm))
                            level = g.level
                            side = 8 if level == 3 else 16
                            for h in range(DT):
                                src = Y[level][:, h, :].rearrange("p (h w) -> p h w", h=side).unsqueeze(3).broadcast_to((P, side, side, 2))
                                dst = Y[level - 1][:, h, :].rearrange("p (h a w c) -> p h a w c", h=side, a=2, c=2)
                                for a in range(2):
                                    nc.scalar.activation(dst[:, :, a, :, :], src, ACT.Copy).then_inc(y_start.sem, 1)

                    def token_norm(which):
                        for j, cs in halves(L1):
                            k = which * 2 + j
                            for ct in range(CT):
                                act.wait_ge(*tn_dve(8 * k + ct + 1))
                                if ct >= 2:
                                    act.wait_ge(*tn_sq(2 * k + 1))
                                elif k > 0:
                                    act.wait_ge(*tn_sq(2 * k))
                                nc.scalar.activation(LSQ[:, ct % 2, :], TN[:, ct, cs], ACT.Square, bias=zero_b[:]).then_inc(tn_act.sem, 1)
                            act.wait_ge(*tn_sq(2 * k + 2))
                            if j == 1:
                                act.wait_ge(*tn_dve(8 * k))
                            nc.scalar.activation(LRS, ps[:, 2 * j + 1, :], ACT.Ln, bias=eps_b[:]).then_inc(tn_act.sem, 1)
                            act.wait_ge(*tn_act(6 * k + 5))
                            nc.scalar.activation(LRS, LRS, ACT.Exp, bias=zero_b[:], scale=-0.5).then_inc(tn_act.sem, 1)

                    token_norm(0)
                    for kt in range(KT):
                        act.wait_ge(*v_pe(kt + 1))
                        nc.scalar.activation(V[:, kt, :], ps[:, kt % 6, :], ACT.Copy).then_inc(v_act.sem, 1)
                    for c in range(PAIRS):
                        for i in range(2):
                            for j, cs in halves(L1):
                                act.wait_ge(*qk_pe(4 * c + 2 * i + j + 1))
                                nc.scalar.activation(QK[:, c % 2, i, cs], ps[:, 2 * i + j, :], ACT.Identity, bias=vec("qk"[i] + "_b", c))\
                                    .then_inc(qk_kept.sem, 1)
                        for kt in range(KT):
                            for e in range(2):
                                i = 16 * c + 2 * kt + e
                                act.wait_ge(*s_pe(i + 1))
                                if i >= 4:
                                    lc, lk = (i - 4) // 16, (i - 4) % 16 // 2
                                    act.wait_ge(*pv_pe(KT * lc + lk + 1))
                                    act.wait_ge(*den_pool(14 * lc + 2 * max(lk - 1, 0) + e + 1))
                                nc.scalar.activation(PR[:, i % 4, :], ps[:, 2 * (i % 3):2 * (i % 3) + 2, :], ACT.Exp, bias=zero_b[:], scale=SCALE)\
                                    .then_inc(s_exp.sem, 1)
                    token_norm(1)
                    for ht in range(HT):
                        act.wait_ge(*fc1_pe(ht + 1))
                        nc.scalar.activation(HM[:, ht, :], ps[:, ht % 6, :], ACT.Gelu, bias=vec("fc1_b", ht)).then_inc(fc1_act.sem, 1)

                @block.vector
                def _(dve):
                    dve.wait_ge(*x_in(32))
                    for ct in range(CT):
                        for j, cs in halves(L1):
                            nc.vector.bn_stats(gn_stats[:, ct, j, :], T[:, ct, cs]).then_inc(gn_dve.sem, 1)
                    dve.wait_ge(*gn_dve(8))
                    for ct in range(CT):
                        nc.vector.bn_aggr(gn_mv[:, ct, :], gn_stats[:, ct, :, :]).then_inc(gn_dve.sem, 1)
                    dve.wait_ge(*gn_pe(1))
                    nc.vector.tensor_tensor(gn_d.rearrange("p (a c) -> p a c", a=2), gn_mv[:, :, 0].rearrange("p (a c) -> p a c", a=2),
                                            ps[:, 0, 0:2].unsqueeze(1).broadcast_to((P, 2, 2)), ALU.subtract).then_inc(gn_dve.sem, 1)
                    dve.wait_ge(*gn_dve(13))
                    nc.vector.tensor_tensor(gn_sq, gn_d, gn_d, ALU.mult).then_inc(gn_dve.sem, 1)
                    dve.wait_ge(*gn_dve(14))
                    nc.vector.tensor_tensor(gn_sq, gn_sq, gn_mv[:, :, 1], ALU.add).then_inc(gn_dve.sem, 1)
                    nc.vector.tensor_copy(gn_m, ps[:, 0, 0:2]).then_inc(gn_dve.sem, 1)
                    dve.wait_ge(*gn_dve(16))
                    dve.wait_ge(*gn_act(2))
                    for ct in range(CT):
                        nc.vector.tensor_scalar(XN[:, ct, :], T[:, ct, :], gn_m[:, ct % 2:ct % 2 + 1], gn_r[:, ct % 2:ct % 2 + 1],
                                                ALU.subtract, ALU.mult).then_inc(gn_dve.sem, 1)
                    nc.vector.memset(Y3, 0.0).then_inc(y_start.sem, 1)
                    for o in range(DT):
                        dve.wait_ge(*conv_act(13 + o))
                        nc.vector.tensor_scalar(ZE[:, o, :], ZE[:, o, :], 1.0, None, ALU.add).then_inc(conv_dve.sem, 1)
                    for o in range(DT):
                        dve.wait_ge(*conv_dve(1 + o))
                        nc.vector.reciprocal(ZE[:, o, :], ZE[:, o, :]).then_inc(conv_dve.sem, 1)
                    for o in range(DT):
                        dve.wait_ge(*conv_dve(3 + o))
                        nc.vector.tensor_tensor(Z[:, o, :], Z[:, o, :], ZE[:, o, :], ALU.mult).then_inc(conv_dve.sem, 1)

                    unit = 0
                    stream = 0
                    chunk = 0
                    norm = 0
                    saved = 0
                    for gi, g in enumerate(GROUPS):
                        if gi in PREPS:
                            level, prm, chunks = PREPS[gi]
                            for c0, n in chunks:
                                k = 21 * chunk
                                dve.wait_ge(*prep_act(9 * chunk + 1))
                                nc.vector.tensor_tensor(SPLR[0:96, 0:n], ps[0:96, 0, 0:n], SPL[0:96, c0:c0 + n], ALU.subtract).then_inc(prep_dve.sem, 1)
                                nc.vector.tensor_copy(DTS[DT_ROW:DT_ROW + R_DT, 0:n], ps[DT_ROW:DT_ROW + R_DT, 0, 0:n]).then_inc(prep_dve.sem, 1)
                                dve.wait_ge(*prep_act(9 * chunk + 3))
                                nc.vector.tensor_tensor(SPL[64:96, c0:c0 + n], SPLR[64:96, 0:n], SPLT[64:96, 0:n], ALU.subtract).then_inc(prep_dve.sem, 1)
                                dve.wait_ge(*prep_act(9 * chunk + 5))
                                for o in range(DT):
                                    nc.vector.tensor_scalar(SPM[:, o, 0:n], ps[:, 2 + o, 0:n], vec(f"dtb{prm}", o), 0.0, ALU.add, ALU.max).then_inc(prep_dve.sem, 1)
                                if unit == 0:
                                    dve.wait_ge(*conv_dve(6))
                                for o in range(DT):
                                    dve.wait_ge(*prep_act(9 * chunk + 6 + o))
                                    nc.vector.tensor_scalar(SPP[:, o, 0:n], SPA[:, o, 0:n], -0.25, None, ALU.mult).then_inc(prep_dve.sem, 1)
                                for step, coef in enumerate((1 / 3, -0.5, 1.0)):
                                    for o in range(DT):
                                        dve.wait_ge(*prep_dve(k + 6 + 2 * step + o))
                                        nc.vector.scalar_tensor_tensor(out=SPP[:, o, 0:n], in0=SPP[:, o, 0:n], scalar=coef, in1=SPA[:, o, 0:n],
                                                                       op0=ALU.add, op1=ALU.mult).then_inc(prep_dve.sem, 1)
                                for o in range(DT):
                                    dve.wait_ge(*prep_act(9 * chunk + 8 + o))
                                    nc.vector.scalar_tensor_tensor(out=SPE[:, o, 0:n], in0=SPA[:, o, 0:n], scalar=E_SMALL, in1=SPE[:, o, 0:n],
                                                                   op0=ALU.is_ge, op1=ALU.mult).then_inc(prep_dve.sem, 1)
                                for o in range(DT):
                                    dve.wait_ge(*prep_dve(k + 14 + o))
                                    nc.vector.tensor_tensor(SPP[:, o, 0:n], SPP[:, o, 0:n], SPE[:, o, 0:n], ALU.max).then_inc(prep_dve.sem, 1)
                                for o in range(DT):
                                    dve.wait_ge(*prep_dve(k + 16 + o))
                                    nc.vector.tensor_tensor(DELTA[:, o, c0:c0 + n], SPM[:, o, 0:n], SPP[:, o, 0:n], ALU.add).then_inc(prep_dve.sem, 1)
                                for o in range(DT):
                                    dve.wait_ge(*prep_dve(k + 18 + o))
                                    nc.vector.tensor_tensor(DU[:, o, c0:c0 + n], DELTA[:, o, c0:c0 + n], F[level][:, o, c0:c0 + n], ALU.mult).then_inc(prep_dve.sem, 1)
                                chunk += 1
                            dve.wait_ge(*prep_dve(21 * chunk))
                        for n in range(N_STATE):
                            dve.wait_ge(*b_rows(unit + 1))
                            for half in range(DT):
                                if unit:
                                    dve.wait_ge(*scanned(stream))
                                nc.vector.tensor_tensor(DBX[:, half, 0:g.n], DU[:, half, g.c0:g.c0 + g.n], ps[:, 0, 0:g.n], ALU.mult).then_inc(driven.sem, 1)
                            for i, (half, d) in enumerate(g.streams):
                                s = stream + i
                                dve.wait_ge(*driven(2 * unit + half + 1))
                                dve.wait_ge(*decay(2 * unit + half + 1))
                                if s >= 4:
                                    dve.wait_ge(*weighed(s - 3))
                                start = 0.0
                                if not g.first:
                                    dve.wait_ge(*state_kept(saved * 32 - 32 + 2 * n + half + 1))
                                    start = STATE[:, half, n:n + 1]
                                w = slice(None, None, -1 if d else 1)
                                nc.vector.tensor_tensor_scan(H[:, s % 4, 0:g.n][:, w], ps[:, 2 + half, 0:g.n][:, w], DBX[:, half, 0:g.n][:, w],
                                                             start, ALU.mult, ALU.add).then_inc(scanned.sem, 1)
                            unit += 1
                            stream += len(g.streams)
                        saved += g.keep_state
                        for d in g.dirs:
                            k = 8 * norm
                            banks = [g.banks[i] for i, s in enumerate(g.streams) if s[1] == d]
                            cols = slice(g.c0, g.c0 + g.n)
                            f, y = F[g.level], Y[g.level]
                            dve.wait_ge(*summed(stream))
                            if norm:
                                dve.wait_ge(*ln_dve(k))
                            for h in range(DT):
                                nc.vector.scalar_tensor_tensor(out=LY[:, h, 0:g.n], in0=f[:, h, cols], scalar=vec(f"Dv{g.params}", h),
                                                               in1=ps[:, banks[h], 0:g.n], op0=ALU.mult, op1=ALU.add).then_inc(ln_dve.sem, 1)
                            dve.wait_ge(*ln_pe(2 * norm + 1))
                            for h in range(DT):
                                nc.vector.tensor_tensor(LY[:, h, 0:g.n], LY[:, h, 0:g.n], ps[:, banks[0], 0:g.n], ALU.subtract).then_inc(ln_dve.sem, 1)
                            dve.wait_ge(*ln_act(4 * norm + 4))
                            for h in range(DT):
                                nc.vector.scalar_tensor_tensor(out=LY[:, h, 0:g.n], in0=LY[:, h, 0:g.n], scalar=vec(f"g{g.params}", h),
                                                               in1=LR[:, 0:g.n], op0=ALU.mult, op1=ALU.mult).then_inc(ln_dve.sem, 1)
                            dve.wait_ge(*y_start({3: 1, 2: 5, 1: 9}[g.level]))
                            for h in range(DT):
                                dve.wait_ge(*ln_dve(k + 5 + h))
                                nc.vector.scalar_tensor_tensor(out=y[:, h, cols], in0=LY[:, h, 0:g.n], scalar=vec(f"be{g.params}", h),
                                                               in1=y[:, h, cols], op0=ALU.add, op1=ALU.add).then_inc(ln_dve.sem, 1)
                            norm += 1
                    dve.wait_ge(*ln_dve(8 * norm))
                    dve.wait_ge(*conv_dve(6))
                    for h in range(DT):
                        nc.vector.tensor_tensor(Y1[:, h, :], Y1[:, h, :], Z[:, h, :], ALU.mult).then_inc(gated.sem, 1)
                    for ct in range(CT):
                        for j, cs in halves(L1):
                            n = ct * 2 + j
                            dve.wait_ge(*out_pe(n + 1))
                            nc.vector.scalar_tensor_tensor(out=T[:, ct, cs], in0=ps[:, n, :], scalar=vec("out_b", ct), in1=T[:, ct, cs],
                                                           op0=ALU.add, op1=ALU.add).then_inc(out_dve.sem, 1)

                    def token_norm(which):
                        for j, cs in halves(L1):
                            k = which * 2 + j
                            dve.wait_ge(*(out_dve, proj_dve)[which](8))
                            dve.wait_ge(*tn_pe(k + 1))
                            for ct in range(CT):
                                nc.vector.tensor_tensor(TN[:, ct, cs], T[:, ct, cs], ps[:, 2 * j, :], ALU.subtract).then_inc(tn_dve.sem, 1)
                            dve.wait_ge(*tn_act(6 * k + 6))
                            for ct in range(CT):
                                nc.vector.tensor_tensor(TN[:, ct, cs], TN[:, ct, cs], LRS, ALU.mult).then_inc(tn_dve.sem, 1)

                    token_norm(0)
                    for c in range(PAIRS):
                        for i in range(2 * KT):
                            qt, e, slot = i // 2, i % 2, (16 * c + i) % 3
                            dve.wait_ge(*smax_pe(16 * c + i + 1))
                            nc.vector.tensor_reduce(maxima[:, e, qt:qt + 1], ps[:, 2 * slot:2 * slot + 2, :].rearrange("p a b -> p (a b)"),
                                                    AX_X, ALU.max).then_inc(smax_dve.sem, 1)
                        dve.wait_ge(*smax_dve(16 * c + 16))
                        nc.vector.tensor_copy(maxima[:, :, 32:40], maxima[:, :, 0:8]).then_inc(mt_dve.sem, 1)
                        dve.wait_ge(*mt_pe(c + 1))
                        nc.vector.tensor_copy(rows[:], ps[:, 6, 0:P]).then_inc(mt_dve.sem, 1)
                        dve.wait_ge(*mt_dve(5 * c + 2))
                        for r in (32, 96):
                            nc.vector.tensor_tensor(rows[r:r + 32, :], ps[r:r + 32, 6, 0:P], rows[r:r + 32, :], ALU.subtract).then_inc(mt_dve.sem, 1)
                        dve.wait_ge(*mt_dve(5 * c + 4))
                        nc.vector.tensor_tensor(RH, rows[:].unsqueeze(1).broadcast_to((P, KT, P)), mask8[:].unsqueeze(2).broadcast_to((P, KT, P)),
                                                ALU.mult).then_inc(mt_dve.sem, 1)
                        for j, cs in halves(L1):
                            dve.wait_ge(*den_pe(2 * c + 2))
                            nc.vector.reciprocal(DEN[:, 0, cs], ps[:, j, :]).then_inc(o_dve.sem, 1)
                        for j, cs in halves(L1):
                            dve.wait_ge(*o_dve(4 * c + j + 1))
                            dve.wait_ge(*pv_pe(KT * c + KT))
                            nc.vector.tensor_tensor(O[:, c, cs], DEN[:, 0, cs], ps[:, 6 + j, :], ALU.mult).then_inc(o_dve.sem, 1)
                    for ct in range(CT):
                        for j, cs in halves(L1):
                            n = ct * 2 + j
                            dve.wait_ge(*proj_pe(n + 1))
                            nc.vector.scalar_tensor_tensor(out=T[:, ct, cs], in0=ps[:, n, :], scalar=o_b[:, ct:ct + 1], in1=T[:, ct, cs],
                                                           op0=ALU.add, op1=ALU.add).then_inc(proj_dve.sem, 1)
                    token_norm(1)
                    dve.wait_ge(*tn_dve(32))
                    for j in range(DT):
                        nc.vector.tensor_tensor(LS[:, j, :], TN[:, j, :], TN[:, j + 2, :], ALU.add).then_inc(ll_dve.sem, 1)
                    for j in range(DT):
                        dve.wait_ge(*ll_dve(1 + j))
                        nc.vector.tensor_tensor(LL[:, j, :], LS[:, j, 0:L1:2], LS[:, j, 1:L1:2], ALU.add).then_inc(ll_dve.sem, 1)
                    for j in range(DT):
                        dve.wait_ge(*ll_dve(3 + j))
                        nc.vector.tensor_scalar(LL[:, j, :], LL[:, j, :], 0.5, None, ALU.mult).then_inc(ll_dve.sem, 1)
                    dve.wait_ge(*ll_dve(6))
                    for ct in range(CT):
                        nc.vector.tensor_tensor(T[:, ct, :], T[:, ct, :], TN[:, ct, :], ALU.add).then_inc(fin_dve.sem, 1)
                    for o in range(DT):
                        dve.wait_ge(*fc2_pe(o + 1))
                        nc.vector.scalar_tensor_tensor(out=DL[:, o, :], in0=ps[:, 6 + o, :], scalar=vec("fc2_b", o), in1=LL[:, o, :],
                                                       op0=ALU.add, op1=ALU.subtract).then_inc(fin_dve.sem, 1)
                    for o in range(DT):
                        dve.wait_ge(*fin_dve(5 + o))
                        nc.vector.tensor_scalar(DL[:, o, :], DL[:, o, :], 0.5, None, ALU.mult).then_inc(fin_dve.sem, 1)
                    dve.wait_ge(*fin_dve(8))
                    for ct in range(CT):
                        tv = T[:, ct, :].rearrange("p (f two) -> p f two", two=2)
                        nc.vector.tensor_tensor(tv, tv, DL[:, ct % 2, :].unsqueeze(2).broadcast_to((P, BANK, 2)), ALU.add).then_inc(fin_dve.sem, 1)

                @block.gpsimd
                def _(pool):
                    unit = 0
                    stream = 0
                    saved = 0
                    for g in GROUPS:
                        for n in range(N_STATE):
                            pool.wait_ge(*c_kept(unit + 1))
                            for i, (half, d) in enumerate(g.streams):
                                s = stream + i
                                pool.wait_ge(*scanned(s + 1))
                                if g.keep_state:
                                    last = 0 if d else g.n - 1
                                    nc.gpsimd.tensor_copy(STATE[:, half, n:n + 1], H[:, s % 4, last:last + 1]).then_inc(state_kept.sem, 1)
                                if s >= 4:
                                    pool.wait_ge(*summed(s - 3))
                                nc.gpsimd.tensor_tensor(HC[:, s % 4, 0:g.n], H[:, s % 4, 0:g.n], CB[:, unit % 2, 0:g.n], ALU.mult).then_inc(weighed.sem, 1)
                            unit += 1
                            stream += len(g.streams)
                    for c in range(PAIRS):
                        for kt in range(1, KT):
                            for e in range(2):
                                i = 2 * kt + e
                                pool.wait_ge(*s_exp(16 * c + i + 1))
                                if kt == 1 and c:
                                    pool.wait_ge(*o_dve(4 * c))
                                if kt > 1:
                                    pool.wait_ge(*den_pool(14 * c + 2 * (kt - 2) + e + 1))
                                a = PR[:, e, :] if kt == 1 else DEN[:, e, :]
                                nc.gpsimd.tensor_tensor(DEN[:, e, :], a, PR[:, i % 4, :], ALU.add).then_inc(den_pool.sem, 1)


            nc.all_engine_barrier(sems_to_clear=range(min(s.sem.num for s in signals), max(s.sem.num for s in signals) + 1))


def tiles(a):
    n = a.shape[0] // P
    return a.reshape(n, P, -1).transpose(1, 0, 2)


def kernel(**inputs):
    import numpy as np
    import concourse.bacc as bacc
    from concourse.bass_utils import run_bass_kernel_spmd

    w = {k: np.asarray(v) for k, v in inputs.items()}
    g = {k[8:]: v for k, v in w.items() if k.startswith("L0_conv_")}
    perm = np.concatenate([np.arange(0, C, 2), np.arange(1, C, 2)])

    ident = np.eye(P, dtype=np.float32)
    gmat = np.kron(np.eye(16, dtype=np.float32), np.full((8, 8), 1 / 16, np.float32))
    sel = np.zeros((96, 2 * N_STATE, P), np.float32)
    for r in range(96):
        sel[r, r % 32] = 1
    neg = np.zeros((P, P), np.float32)
    mask8 = np.zeros((P, KT), np.float32)
    for r in range(P):
        if r % 32 < KT:
            neg[r] = -1
            mask8[r, r % 32] = 1
    pos = np.linspace(0.0, 1.0, C, dtype=np.float32) * np.float32(C // 2 - 1)
    i0 = np.clip(np.floor(pos).astype(np.int32), 0, C // 2 - 2)
    frac = (pos - i0.astype(np.float32)).astype(np.float32)
    up = np.zeros((C, C // 2), np.float32)
    up[np.arange(C), i0] = np.float32(1.0) - frac
    up[np.arange(C), i0 + 1] = frac

    xrows = list(range(R_DT, R_DT + 2 * N_STATE)) * 3 + list(range(R_DT))
    cols = {"in_bx": g["in_b"][:D], "in_bz": g["in_b"][D:], "c1_b": g["c1_b"], "c2_b": g["c2_b"], "c3_b": g["c3_b"],
            "out_b": g["out_b"][perm], "q_b": w["L1_attn_qkv_b"][:C], "k_b": w["L1_attn_qkv_b"][C:2 * C], "v_b": w["L1_attn_qkv_b"][2 * C:],
            "proj_b": w["L1_attn_proj_b"][perm], "fc1_b": w["L1_ffn_fc1_b"], "fc2_b": w["L1_ffn_fc2_b"]}
    for s in (1, 2, 3):
        cols |= {f"{v}{s}": g[f"{v}{s}"] for v in ("dtb", "Dv", "g", "be")}
        cols[f"Al{s}"] = g[f"Al{s}"]
    vecs = np.concatenate([tiles(cols[n]).reshape(P, -1) for n in VEC], axis=1)
    arrays = {
        "x": w["x"].reshape(B, C, L1),
        "in_x": tiles(g["in_w"][:D][:, perm]), "in_z": tiles(g["in_w"][D:][:, perm].T), "c1": tiles(g["c1_w"].T),
        "c2": tiles(g["c2_w"].transpose(1, 2, 3, 0).reshape(D, -1)), "c3": tiles(g["c3_w"].transpose(1, 2, 3, 0).reshape(D, -1)),
        "out": tiles(g["out_w"][perm].T), "up": tiles(up), "fc1": tiles(w["L1_ffn_fc1_w"].T), "fc2": tiles(w["L1_ffn_fc2_w"].T),
        "qkv": tiles(w["L1_attn_qkv_w"][:, perm].T), "proj": tiles(w["L1_attn_proj_w"][perm].T),
        "vecs": vecs, "ident": ident, "gmat": gmat, "sel": sel, "neg": neg, "mask8": mask8,
    }
    for s in (1, 2, 3):
        arrays[f"xw{s}"] = tiles(g[f"xw{s}"][xrows].T)
        arrays[f"dtw{s}"] = g[f"dtw{s}"].T
    for k in ("c2", "c3"):
        arrays[k] = arrays[k].reshape(P, DT, 4, D)
    arrays = {k: np.ascontiguousarray(v) for k, v in arrays.items()}

    nc = bacc.Bacc("TRN2", target_bir_lowering=False, num_devices=1)
    t = {k: nc.dram_tensor(f"in_{k}", v.shape, mybir.dt.from_np(v.dtype), kind="ExternalInput").ap() for k, v in arrays.items()}
    t["y"] = nc.dram_tensor("out", (B, C, L1), F32, kind="ExternalOutput").ap()
    build(nc, t)
    r = run_bass_kernel_spmd(nc, [{f"in_{k}": v for k, v in arrays.items()}], core_ids=[0])
    return r.results[0]["out"].reshape(B, C, 32, 32)
```

```python
from contextlib import ExitStack

import concourse.bass as bass
from concourse import mybir

ALU = mybir.AluOpType
ACT = mybir.ActivationFunctionType
AX_X = mybir.AxisListType.X
F32 = mybir.dt.float32
F32R = mybir.dt.float32r
BF16 = mybir.dt.bfloat16

P = 128
BANK = 512
B = 8
C, CT = 512, 4
D, DT = 256, 2
L1, L2, L3 = 1024, 256, 64
N_STATE, R_DT = 16, 8
XD = 3 * 2 * N_STATE + R_DT
DT_ROW = 3 * 2 * N_STATE
HEADS, HD = 8, 64
LOWER, UPPER = slice(0, HD), slice(HD, 2 * HD)
KT = L1 // P
HID, HT = 2048, 16
LN_EPS = 1e-5
SCALE = HD ** -0.5
E_SMALL = 1 / 64

VEC = {}
_at = 0
for _name, _n in [("in_bx", 2), ("in_bz", 2), ("c1_b", 2), ("c2_b", 2), ("c3_b", 2), ("out_b", 4), ("qk_b", 8),
                  ("v_b", 4), ("proj_b", 4), ("fc1_b", 16), ("fc2_b", 2)] + \
        [(f"{v}{s}", 2) for s in (1, 2, 3) for v in ("dtb", "Dv", "g", "be")] + [(f"Al{s}", 32) for s in (1, 2, 3)]:
    VEC[_name] = (_at, _n)
    _at += _n
N_VEC = _at


SMAX_AFTER = {2: (0,), 3: (1, 2), 4: (3, 4), 5: (5, 6), 6: (7,)}
RING = [("project", 0, 0), ("project", 1, 0)] + [("smax", 0, _i) for _i in range(KT)]
for _h in range(HEADS):
    for _kt in range(KT):
        RING.append(("scores", _h, _kt))
        RING += [("smax", _h + 1, _i) for _i in SMAX_AFTER.get(_kt, ()) if _h + 1 < HEADS]
    if _h + 2 < HEADS:
        RING.append(("project", _h + 2, 0))
RING_AT = {_job: _i for _i, _job in enumerate(RING)}
PV_AFTER = {3: (0, 1), 4: (2,), 5: (3,), 6: (4,), 7: (5,)}
PV_LAST = (6, 7)


class Signal:

    def __init__(self, sem, per_image):
        self.sem, self.per_image = sem, per_image

    def __call__(self, k):
        assert 0 < k <= self.per_image
        return self.sem, k


class Group:

    def __init__(self, index, level, params, dirs, c0, n, first):
        self.index, self.level, self.params, self.dirs, self.c0, self.n, self.first = index, level, params, dirs, c0, n, first
        self.slot = index % 2
        self.width = n * len(dirs)
        self.cols = slice(c0, c0 + n)


GROUPS = [Group(i, *g) for i, g in enumerate([
    (3, 3, (0, 1), 0, L3, True),
    (2, 2, (0, 1), 0, L2, True),
    (1, 1, (0,), 0, BANK, True),
    (1, 1, (0,), BANK, BANK, False),
    (1, 2, (1,), BANK, BANK, True),
    (1, 2, (1,), 0, BANK, False),
])]
NG = len(GROUPS)
N_UNITS = NG * N_STATE
KEEPS = {2: 0, 4: 1}
LN_DVE = [5 + 2 * len(g.dirs) for g in GROUPS]
LN_DVE_AT = [sum(LN_DVE[:i]) for i in range(NG + 1)]
B_BANK, C_BANK, DECAY_BANK, Y_BANK, AUX_BANK = (0, 1), 2, (3, 4), (5, 6), 7


def build(nc, t):
    with ExitStack() as ctx:
        def sb(name, shape, dt=F32):
            return ctx.enter_context(nc.sbuf_tensor(name, shape, dt))

        signals = []

        def signal(name, per_image):
            signals.append(Signal(ctx.enter_context(nc.semaphore(name)), per_image))
            return signals[-1]

        def sem(name):
            return ctx.enter_context(nc.semaphore(name))

        wf = sb("wf", [P, CT, D])
        wz = sb("wz", [P, CT, D])
        wout = sb("wout", [P, DT, C])
        xw = {s: sb(f"xw{s}", [P, DT, XD]) for s in (1, 2, 3)}
        dtw = {s: sb(f"dtw{s}", [P, D]) for s in (1, 2, 3)}
        wqkv = sb("wqkv", [P, CT, 3 * C])
        w1 = sb("w1", [P, DT, HID])
        qk_parts = sb("qk_parts", [P, 2, 3, L1], F32R)
        vecs = sb("vecs", [P, N_VEC])
        ident = sb("ident", [P, P])
        gmat = sb("gmat", [P, P])
        ones = sb("ones", [P, P])
        ones_c = sb("ones_c", [P, P])
        ones_d = sb("ones_d", [P, P])
        zero_b = sb("zero_b", [P, 1])
        eps_b = sb("eps_b", [P, 1])
        one_b = sb("one_b", [P, 1])
        sel = sb("sel", [96, 2 * N_STATE, P], BF16)
        neg = sb("neg", [P, P], BF16)
        mask8 = sb("mask8", [P, KT])
        f1_b = sb("f1_b", [P, DT])
        o_b = sb("o_b", [P, CT])
        small = sb("small", [P, 96])
        gn_stats = small[:, 0:48].rearrange("p (c j s) -> p c j s", c=CT, j=2)
        gn_mv = small[:, 48:56].rearrange("p (c s) -> p c s", c=CT)
        gn_d, gn_sq, gn_m = small[:, 56:60], small[:, 60:64], small[:, 64:66]
        gn_r = small[:, 84:86]
        maxima = sb("maxima", [P, 2, 64])
        rows = sb("rows", [P, P], BF16)

        arena = sb("arena", [P, 28448])
        taken = [0]

        def region(at, shape, dt=F32):
            n = 1
            for s in shape:
                n *= s
            words = n if dt == F32 else n // 2
            taken[0] = max(taken[0], at + words)
            a = arena[:, at:at + words]
            if dt != F32:
                a = a.bitcast(dt)
            if len(shape) == 2:
                a = a.rearrange("p (a b) -> p a b", a=shape[0])
            elif len(shape) == 3:
                a = a.rearrange("p (a b c) -> p a b c", a=shape[0], b=shape[1])
            return a

        T = region(0, [CT, L1])
        XN = region(4096, [CT, L1])
        C2 = region(8192, [DT, 4, D])
        C3 = region(10240, [DT, 4, D])
        F1 = region(12288, [DT, L1])
        F2 = region(14336, [DT, L2])
        F3 = region(14848, [DT, L3])
        Z = region(14976, [DT, L1])
        Y1 = region(17024, [DT, L1])
        Y2 = region(19072, [DT, L2])
        Y3 = region(19584, [DT, L3])
        ZE = region(19712, [DT, L1])
        F = {1: F1, 2: F2, 3: F3}
        Y = {1: Y1, 2: Y2, 3: Y3}
        DELTA = region(4096, [2, DT, BANK])
        DU = region(6144, [2, DT, BANK])
        SPL = region(8192, [2, BANK], BF16)
        SPLR = region(8704, [BANK])
        DTS = region(9216, [BANK])
        SPLT = region(9728, [BANK], BF16)
        SPA = region(9984, [DT, BANK])
        SPE = region(11008, [DT, BANK])
        SPP = region(8704, [DT, BANK])
        DBX = region(19712, [3, BANK])
        H = region(21248, [4, BANK])
        HC = region(23296, [3, BANK])
        CB = region(24832, [2, BANK])
        LY = region(25856, [DT, BANK])
        LR = region(26880, [BANK])
        LSQS = region(27392, [DT, BANK])
        STATE = region(28416, [DT, N_STATE])
        TN = region(4096, [CT, L1])
        WPROJ = region(8192, [CT, C])
        V = region(12288, [KT, C])
        PR = region(16384, [4, L1])
        O = region(20480, [CT, L1])
        DEN = region(24576, [2, L1])
        REC = region(27136, [BANK])
        RH = region(26624, [KT, P], BF16)
        LSQ = region(24576, [2, BANK])
        LRS = region(25600, [BANK])
        W2 = region(20480, [HT, D])
        LL = region(8192, [DT, BANK])
        LS = region(9216, [DT, L1])
        HM = region(11264, [HT, BANK])
        DL = region(19456, [DT, BANK])
        S_INW = region(0, [DT, C])
        S_C1 = region(1024, [DT, D])
        S_U = region(1536, [CT, D])
        S_FC1 = region(2560, [CT, HID])
        S_SEL = region(10752, [2 * N_STATE, P])
        S_NEG = region(14848, [P])
        S_PROJ = region(15104, [CT, C])
        assert taken[0] <= 28448

        ps = ctx.enter_context(nc.psum_tensor("ps", [P, 8, BANK], F32))

        def vec(name, i, rows=slice(0, P)):
            a = VEC[name][0] + i
            return vecs[rows, a:a + 1]

        weights_in = sem("weights_in")
        consts_set = sem("consts_set")
        setup_pe = sem("setup_pe")
        setup_act = sem("setup_act")
        setup_dve = sem("setup_dve")

        x_in = signal("x_in", 32)
        c23_in = signal("c23_in", 32)
        proj_in = signal("proj_in", 16)
        w2_in = signal("w2_in", 16)
        stored = signal("stored", 32)
        gn_dve = signal("gn_dve", 8 + 4 + 3 + 1 + 4)
        gn_pe = signal("gn_pe", 2)
        gn_act = signal("gn_act", 2)
        conv_pe = signal("conv_pe", 8 + 4)
        conv_act = signal("conv_act", 4 + 4 + 4 + 2)
        conv_dve = signal("conv_dve", 6)
        prep_pe = signal("prep_pe", 3 * NG)
        prep_act = signal("prep_act", 10 * NG)
        prep_dve = signal("prep_dve", 10 * NG)
        b_rows = signal("b_rows", N_UNITS)
        c_rows = signal("c_rows", N_UNITS)
        c_kept = signal("c_kept", N_UNITS)
        decay = signal("decay", DT * N_UNITS)
        driven = signal("driven", DT * N_UNITS)
        scanned = signal("scanned", DT * N_UNITS)
        state_kept = signal("state_kept", DT * N_STATE * len(KEEPS))
        weighed = signal("weighed", DT * N_UNITS)
        summed = signal("summed", DT * N_UNITS)
        ln_pe = signal("ln_pe", 2 * NG)
        ln_act = signal("ln_act", 3 * NG)
        ln_dve = signal("ln_dve", LN_DVE_AT[NG])
        y_start = signal("y_start", 1 + 4 + 4)
        gated = signal("gated", 2)
        out_pe = signal("out_pe", 8)
        out_dve = signal("out_dve", 8)
        tn_pe = signal("tn_pe", 4)
        tn_sq = signal("tn_sq", 4 * 2)
        tn_dve = signal("tn_dve", 4 * 8)
        tn_act = signal("tn_act", 4 * 6)
        v_pe = signal("v_pe", KT)
        v_act = signal("v_act", KT)
        qk_pe = signal("qk_pe", HEADS)
        qk_hi = signal("qk_hi", 3 * HEADS)
        qk_lo = signal("qk_lo", 3 * HEADS)
        smax_pe = signal("smax_pe", KT * HEADS)
        smax_dve = signal("smax_dve", KT * HEADS)
        mt_dve = signal("mt_dve", 4 * HEADS)
        mt_pe = signal("mt_pe", HEADS)
        s_pe = signal("s_pe", KT * HEADS)
        s_exp = signal("s_exp", KT * HEADS)
        pv_pe = signal("pv_pe", KT * HEADS)
        den_pool = signal("den_pool", (KT - 1) * HEADS)
        den_pe = signal("den_pe", HEADS)
        o_dve = signal("o_dve", 3 * HEADS)
        proj_pe = signal("proj_pe", 8)
        proj_dve = signal("proj_dve", 8)
        ll_dve = signal("ll_dve", 6)
        fc1_pe = signal("fc1_pe", HT)
        fc1_act = signal("fc1_act", HT)
        fc2_pe = signal("fc2_pe", 2)
        fin_dve = signal("fin_dve", 4 + 8)

        def halves(n):
            return [(j, slice(BANK * j, BANK * j + BANK)) for j in range(n // BANK)]

        SETUP_DVE, SETUP_ACT, SETUP_PE, CONSTS = 4, 9, 10, 9
        W_ALL = 16 * 20

        with nc.Block() as block:
            @block.sync
            def _(sp):
                for dst, src in [
                    (S_INW, t["in_x"]), (S_C1, t["c1"]), (S_U, t["up"]), (S_FC1, t["fc1"]), (vecs[:], t["vecs"]), (ident[:], t["ident"]),
                    (gmat[:], t["gmat"]), (S_SEL[0:96], t["sel"]), (S_NEG, t["neg"]), (mask8[:], t["mask8"]),
                    (wz[:], t["in_z"]), (wout[:], t["out"]), (wqkv[:], t["qkv"]), (S_PROJ, t["proj"]),
                    (xw[1][:], t["xw1"]), (xw[2][:], t["xw2"]), (xw[3][:], t["xw3"]),
                    (dtw[1][DT_ROW:DT_ROW + R_DT, :], t["dtw1"]), (dtw[2][DT_ROW:DT_ROW + R_DT, :], t["dtw2"]),
                    (dtw[3][DT_ROW:DT_ROW + R_DT, :], t["dtw3"]),
                ]:
                    sp.dma_start(dst, src).then_inc(weights_in, 16)
                sp.wait_ge(setup_dve, SETUP_DVE)
                sp.wait_ge(setup_act, SETUP_ACT)
                sp.wait_ge(setup_pe, SETUP_PE)
            @block.tensor
            def _(pe):
                pe.wait_ge(weights_in, W_ALL)
                for ct in range(CT):
                    for m in range(DT):
                        mm = pe.matmul(ps[:, ct, 0:D], S_INW[:, m, P * ct:P * ct + P], S_C1[:, m, :], start=m == 0, stop=m == DT - 1)
                mm.then_inc(setup_pe, 1)
                for o in range(DT):
                    for m in range(DT):
                        pe.matmul(ps[:, 4, o:o + 1], S_C1[:, m, P * o:P * o + P], vec("in_bx", m), start=m == 0, stop=m == DT - 1)
                for o in range(CT):
                    for m in range(CT):
                        mm = pe.matmul(ps[:, 4, 2 + o:3 + o], S_PROJ[:, m, P * o:P * o + P], vec("v_b", m), start=m == 0, stop=m == CT - 1)
                mm.then_inc(setup_pe, 1)
                pe.wait_ge(setup_dve, 1 + 1)
                for j in range(DT):
                    for h in range(4):
                        if j == 1 and h == 0:
                            pe.wait_ge(setup_act, 4)
                        for ct in range(CT):
                            mm = pe.matmul(ps[:, h, :], S_U[:, ct, P * j:P * j + P], S_FC1[:, ct, BANK * h:BANK * h + BANK],
                                           start=ct == 0, stop=ct == CT - 1)
                        mm.then_inc(setup_pe, 1)
                pe.wait_ge(consts_set, CONSTS)

            @block.scalar
            def _(act):
                act.wait_ge(weights_in, W_ALL)
                act.wait_ge(consts_set, CONSTS)
                for h in range(4):
                    act.wait_ge(setup_pe, 3 + h)
                    nc.scalar.activation(w1[:, 0, BANK * h:BANK * h + BANK], ps[:, h, :], ACT.Copy).then_inc(setup_act, 1)
                for h in range(4):
                    act.wait_ge(setup_pe, 7 + h)
                    nc.scalar.activation(w1[:, 1, BANK * h:BANK * h + BANK], ps[:, h, :], ACT.Copy).then_inc(setup_act, 1)
                a, n = VEC["Al1"][0], 96
                nc.scalar.activation(vecs[:, a:a + n], vecs[:, a:a + n], ACT.Exp, bias=zero_b[:]).then_inc(setup_act, 1)

            @block.vector
            def _(dve):
                nc.vector.memset(ones[:], 1.0).then_inc(consts_set, 1)
                nc.vector.memset(ones_c[:], 1.0 / C).then_inc(consts_set, 1)
                nc.vector.memset(ones_d[:], 1.0 / D).then_inc(consts_set, 1)
                nc.vector.memset(zero_b[:], 0.0).then_inc(consts_set, 1)
                nc.vector.memset(eps_b[:], LN_EPS).then_inc(consts_set, 1)
                nc.vector.memset(one_b[:], 1.0).then_inc(consts_set, 1)
                dve.wait_ge(weights_in, W_ALL)
                nc.vector.tensor_copy(sel[:], S_SEL[0:96]).then_inc(consts_set, 1)
                nc.vector.tensor_copy(neg[:], S_NEG).then_inc(consts_set, 1)
                nc.vector.memset(maxima[:], 0.0).then_inc(consts_set, 1)
                dve.wait_ge(setup_pe, 1)
                nc.vector.tensor_copy(wf[:], ps[:, 0:4, 0:D]).then_inc(setup_dve, 1)
                dve.wait_ge(setup_pe, 2)
                a = VEC["c1_b"][0]
                nc.vector.tensor_tensor(f1_b[:], ps[:, 4, 0:2], vecs[:, a:a + 2], ALU.add).then_inc(setup_dve, 1)
                a = VEC["proj_b"][0]
                nc.vector.tensor_tensor(o_b[:], ps[:, 4, 2:6], vecs[:, a:a + 4], ALU.add).then_inc(setup_dve, 1)
                dve.wait_ge(setup_act, SETUP_ACT)
                a = VEC["Al1"][0]
                nc.vector.tensor_scalar(vecs[:, a:a + 96], vecs[:, a:a + 96], -1.0, None, ALU.mult).then_inc(setup_dve, 1)
                dve.wait_ge(setup_dve, SETUP_DVE)


        with nc.Fori(0, B) as b:
            with nc.Block() as block:
                @block.sync
                def _(sp):
                    for two in range(2):
                        sp.dma_start(T[:, 2 * two:2 * two + 2, :], t["x"][b].rearrange("(j p two) l -> two p j l", p=P, two=2)[two]).then_inc(x_in.sem, 16)
                    sp.dma_start(C2, t["c2"]).then_inc(c23_in.sem, 16)
                    sp.dma_start(C3, t["c3"]).then_inc(c23_in.sem, 16)
                    sp.wait_ge(*gated(2))
                    sp.dma_start(WPROJ, t["proj"]).then_inc(proj_in.sem, 16)
                    sp.wait_ge(*proj_pe(8))
                    sp.dma_start(W2, t["fc2"]).then_inc(w2_in.sem, 16)
                    sp.wait_ge(*fin_dve(12))
                    for two in range(2):
                        sp.dma_start(t["y"][b].rearrange("(j p two) l -> two p j l", p=P, two=2)[two], T[:, 2 * two:2 * two + 2, :]).then_inc(stored.sem, 16)
                    sp.wait_ge(*stored(32))

                @block.tensor
                def _(pe):
                    for k in range(2):
                        pe.wait_ge(*gn_dve((12, 15)[k]))
                        src = (gn_mv[:, :, 0], gn_sq)[k]
                        pe.matmul(ps[:, k, 0:2], gmat[:], src[:, 0:2], start=True, stop=False)
                        pe.matmul(ps[:, k, 0:2], gmat[:], src[:, 2:4], start=False, stop=True).then_inc(gn_pe.sem, 1)
                    pe.wait_ge(*gn_dve(20))
                    for k, w in enumerate((wf, wz)):
                        for o in range(DT):
                            for j, cs in halves(L1):
                                n = k * 4 + o * 2 + j
                                for ct in range(CT):
                                    mm = pe.matmul(ps[:, n, :], w[:, ct, P * o:P * o + P], XN[:, ct, cs], start=ct == 0, stop=ct == CT - 1)
                                mm.then_inc(conv_pe.sem, 1)
                    pe.wait_ge(*c23_in(32))
                    for k, (w, src, side) in enumerate([(C2, F1, 32), (C3, F2, 16)]):
                        pe.wait_ge(*conv_act((8, 10)[k]))
                        n = side * side // 4
                        for o in range(DT):
                            for ci in range(DT):
                                v = src[:, ci, :].rearrange("p (h a w c) -> p h a w c", h=side // 2, a=2, c=2)
                                for q in range(4):
                                    mm = pe.matmul(ps[:, 2 * k + o, 0:n], w[:, ci, q, P * o:P * o + P], v[:, :, q // 2, :, q % 2],
                                                   start=ci == 0 and q == 0, stop=ci == DT - 1 and q == 3)
                            mm.then_inc(conv_pe.sem, 1)

                    def project(g):
                        k = g.index
                        if k == 0:
                            pe.wait_ge(*conv_act(12))
                        else:
                            pe.wait_ge(*prep_act(8) if k == 1 else ln_act(3 * (k - 2) + 2))
                        for m in range(DT):
                            mm = pe.matmul(ps[0:XD, AUX_BANK, 0:g.n], xw[g.params][:, m, :], F[g.level][:, m, g.cols], start=m == 0, stop=m == DT - 1)
                        mm.then_inc(prep_pe.sem, 1)

                    def spread_dt(g, half):
                        k = g.index
                        if half == 0:
                            pe.wait_ge(*prep_act(10 * k + 2))
                            pe.wait_ge(*prep_dve(10 * k + 1))
                        else:
                            pe.wait_ge(*prep_act(10 * k + 6))
                        pe.matmul(ps[:, AUX_BANK, 0:g.n], dtw[g.params][DT_ROW:DT_ROW + R_DT, P * half:P * half + P],
                                  DTS[DT_ROW:DT_ROW + R_DT, 0:g.n], start=True, stop=True).then_inc(prep_pe.sem, 1)

                    def mean(g):
                        k = g.index
                        pe.wait_ge(*ln_dve(LN_DVE_AT[k] + 2))
                        pe.wait_ge(*prep_act(10 * (k + 1) + 8) if k + 1 < NG else ln_act(3 * (k - 1) + 2))
                        for h in range(DT):
                            mm = pe.matmul(ps[:, AUX_BANK, 0:g.width], ones_d[:], LY[:, h, 0:g.width], start=h == 0, stop=h == DT - 1)
                        mm.then_inc(ln_pe.sem, 1)

                    def variance(g):
                        pe.wait_ge(*ln_act(3 * g.index + 1))
                        pe.wait_ge(*ln_dve(LN_DVE_AT[g.index] + 3))
                        for h in range(DT):
                            mm = pe.matmul(ps[:, AUX_BANK, 0:g.width], ones_d[:], LSQS[:, h, 0:g.width], start=h == 0, stop=h == DT - 1)
                        mm.then_inc(ln_pe.sem, 1)

                    def b_row(u):
                        g, n = GROUPS[u // N_STATE], u % N_STATE
                        if n == 0:
                            pe.wait_ge(*prep_dve(10 * g.index + 2))
                            pe.wait_ge(*prep_act(10 * g.index + 4))
                        if u >= 2:
                            pe.wait_ge(*driven(2 * (u - 2) + 2))
                        pe.matmul(ps[:, B_BANK[u % 2], 0:g.n], sel[:, n, :], SPL[0:96, g.slot, 0:g.n], start=True, stop=True).then_inc(b_rows.sem, 1)

                    def c_row(u):
                        g, n = GROUPS[u // N_STATE], u % N_STATE
                        if u >= 1:
                            pe.wait_ge(*c_kept(u))
                        pe.matmul(ps[:, C_BANK, 0:g.n], sel[:, N_STATE + n, :], SPL[0:96, g.slot, 0:g.n], start=True, stop=True).then_inc(c_rows.sem, 1)

                    def sum_states(u):
                        g, n = GROUPS[u // N_STATE], u % N_STATE
                        for half in range(DT):
                            s = 2 * u + half
                            if n == 0 and g.index:
                                pe.wait_ge(*ln_dve(LN_DVE_AT[g.index - 1] + 1 + half))
                            pe.wait_ge(*weighed(s + 1))
                            pe.matmul(ps[:, Y_BANK[half], 0:g.width], ident[:], HC[:, s % 3, 0:g.width], start=n == 0, stop=n == N_STATE - 1)\
                                .then_inc(summed.sem, 1)

                    project(GROUPS[0])
                    spread_dt(GROUPS[0], 0)
                    spread_dt(GROUPS[0], 1)
                    b_row(0)
                    b_row(1)
                    c_row(0)
                    for u in range(N_UNITS):
                        g, n = GROUPS[u // N_STATE], u % N_STATE
                        if u + 2 < N_UNITS:
                            b_row(u + 2)
                        if u + 1 < N_UNITS:
                            c_row(u + 1)
                        if u >= 1:
                            sum_states(u - 1)
                        if g.index and n == 2:
                            mean(GROUPS[g.index - 1])
                        if g.index and n == 4:
                            variance(GROUPS[g.index - 1])
                        if g.index + 1 < NG:
                            if n == 6:
                                project(GROUPS[g.index + 1])
                            if n == 8:
                                spread_dt(GROUPS[g.index + 1], 0)
                            if n == 9:
                                spread_dt(GROUPS[g.index + 1], 1)
                    sum_states(N_UNITS - 1)
                    mean(GROUPS[NG - 1])
                    variance(GROUPS[NG - 1])

                    pe.wait_ge(*gated(2))
                    for ct in range(CT):
                        for j, cs in halves(L1):
                            n = ct * 2 + j
                            for m in range(DT):
                                mm = pe.matmul(ps[:, n, :], wout[:, m, P * ct:P * ct + P], Y1[:, m, cs], start=m == 0, stop=m == DT - 1)
                            mm.then_inc(out_pe.sem, 1)

                    def token_norm(which):
                        for j, cs in halves(L1):
                            k = which * 2 + j
                            if which == 0:
                                pe.wait_ge(*out_dve(8))
                            else:
                                pe.wait_ge(*proj_dve(8))
                            for ct in range(CT):
                                mm = pe.matmul(ps[:, 2 * j, :], ones_c[:], T[:, ct, cs], start=ct == 0, stop=ct == CT - 1)
                            mm.then_inc(tn_pe.sem, 1)
                            for ct in range(CT):
                                pe.wait_ge(*tn_act(6 * k + ct + 1))
                                mm = pe.matmul(ps[:, 2 * j + 1, :], ones_c[:], LSQ[:, ct % 2, :], start=ct == 0, stop=ct == CT - 1)
                                if ct in (1, 3):
                                    mm.then_inc(tn_sq.sem, 1)

                    token_norm(0)

                    pe.wait_ge(*tn_dve(16))
                    for kt in range(KT):
                        if kt >= 6:
                            pe.wait_ge(*v_act(kt - 5))
                        for ct in range(CT):
                            mm = pe.matmul(ps[:, kt % 6, :], TN[:, ct, P * kt:P * kt + P], wqkv[:, ct, 2 * C:3 * C], start=ct == 0, stop=ct == CT - 1)
                        mm.then_inc(v_pe.sem, 1)

                    def ring(job):
                        at = RING_AT[job]
                        if at < 3:
                            pe.wait_ge(*v_act(KT))
                        else:
                            kind, h, i = RING[at - 3]
                            pe.wait_ge(*{"project": qk_lo(3 * h + 3), "smax": smax_dve(KT * h + i + 1), "scores": s_exp(KT * h + i + 1)}[kind])
                        return 2 * (at % 3)

                    def project_qk(h):
                        bank = ring(("project", h, 0))
                        for j, cs in halves(L1):
                            for ct in range(CT):
                                mm = pe.matmul(ps[:, bank + j, :], wqkv[:, ct, P * h:P * h + P], TN[:, ct, cs], start=ct == 0, stop=ct == CT - 1)
                        mm.then_inc(qk_pe.sem, 1)

                    def smax(h, qt):
                        bank = ring(("smax", h, qt))
                        if qt == 0:
                            pe.wait_ge(*qk_lo(3 * h + 3))
                        q, k = qk_parts[:, h % 2, 0, :], qk_parts[:, h % 2, 1, :]
                        for j, cs in halves(L1):
                            mm = pe.matmul(ps[:, bank + j, :], q[:, P * qt:P * qt + P], k[:, cs], start=True, stop=True)
                        mm.then_inc(smax_pe.sem, 1)

                    def turn_maxima(h):
                        pe.wait_ge(*mt_dve(4 * h + 1))
                        if h >= 2:
                            pe.wait_ge(*o_dve(3 * (h - 2) + 1))
                        pe.transpose(ps[:, 7, 0:P], maxima[:].rearrange("p e m -> p (e m)"), ident[:]).then_inc(mt_pe.sem, 1)

                    def scores(h, kt):
                        bank = ring(("scores", h, kt))
                        if kt == 0:
                            pe.wait_ge(*mt_dve(4 * h + 4))
                        e = h % 2
                        q = qk_parts[:, e, 0, :]
                        for part in range(2):
                            k = qk_parts[:, e, 1 + part, P * kt:P * kt + P]
                            for j, cs in halves(L1):
                                pe.matmul(ps[:, bank + j, :], k, q[:, cs], start=part == 0, stop=False)
                        for j, cs in halves(L1):
                            mm = pe.matmul(ps[:, bank + j, :], neg[64 * e:64 * e + 64, :], RH[64 * e:64 * e + 64, 4 * j:4 * j + 4, :], start=False, stop=True)
                        mm.then_inc(s_pe.sem, 1)

                    def times_values(h, kt):
                        i = KT * h + kt
                        pe.wait_ge(*s_exp(i + 1))
                        if kt == 0 and h:
                            pe.wait_ge(*o_dve(3 * h))
                        for j, cs in halves(L1):
                            mm = pe.matmul(ps[64 * j:64 * j + 64, 6, :], V[:, kt, HD * h:HD * h + HD], PR[:, i % 4, cs], start=kt == 0, stop=kt == KT - 1)
                        mm.then_inc(pv_pe.sem, 1)

                    def sum_exps(h):
                        pe.wait_ge(*den_pool(7 * h + 7))
                        if h + 1 < HEADS:
                            pe.wait_ge(*mt_dve(4 * (h + 1) + 3))
                        for j, cs in halves(L1):
                            mm = pe.matmul(ps[64 * j:64 * j + 64, 7, :], ones[:, 0:64], DEN[:, h % 2, cs], start=True, stop=True)
                        mm.then_inc(den_pe.sem, 1)

                    project_qk(0)
                    project_qk(1)
                    for qt in range(KT):
                        smax(0, qt)
                    turn_maxima(0)
                    for h in range(HEADS):
                        for kt in range(KT):
                            scores(h, kt)
                            if kt == 0 and h:
                                sum_exps(h - 1)
                            if h + 1 < HEADS:
                                for qt in SMAX_AFTER.get(kt, ()):
                                    smax(h + 1, qt)
                            for pt in PV_AFTER.get(kt, ()):
                                times_values(h, pt)
                        if h + 1 < HEADS:
                            turn_maxima(h + 1)
                        if h + 2 < HEADS:
                            project_qk(h + 2)
                        for pt in PV_LAST:
                            times_values(h, pt)
                    sum_exps(HEADS - 1)

                    pe.wait_ge(*proj_in(16))
                    pe.wait_ge(*o_dve(3 * HEADS))
                    for ct in range(CT):
                        for j, cs in halves(L1):
                            for m in range(CT):
                                mm = pe.matmul(ps[:, ct * 2 + j, :], WPROJ[:, m, P * ct:P * ct + P], O[:, m, cs], start=m == 0, stop=m == CT - 1)
                            mm.then_inc(proj_pe.sem, 1)

                    token_norm(1)

                    pe.wait_ge(*ll_dve(6))
                    for ht in range(HT):
                        if ht >= 6:
                            pe.wait_ge(*fc1_act(ht - 5))
                        elif ht == 0:
                            pe.wait_ge(*tn_dve(32))
                        for j in range(DT):
                            mm = pe.matmul(ps[:, ht % 6, :], w1[:, j, P * ht:P * ht + P], LL[:, j, :], start=j == 0, stop=j == DT - 1)
                        mm.then_inc(fc1_pe.sem, 1)
                    pe.wait_ge(*w2_in(16))
                    for o in range(DT):
                        for ht in range(HT):
                            if o == 0:
                                pe.wait_ge(*fc1_act(ht + 1))
                            mm = pe.matmul(ps[:, 6 + o, :], W2[:, ht, P * o:P * o + P], HM[:, ht, :], start=ht == 0, stop=ht == HT - 1)
                        mm.then_inc(fc2_pe.sem, 1)

                @block.scalar
                def _(act):
                    act.wait_ge(*gn_pe(2))
                    nc.scalar.activation(small[:, 80:82], ps[:, 1, 0:2], ACT.Ln, bias=eps_b[:]).then_inc(gn_act.sem, 1)
                    act.wait_ge(*gn_act(1))
                    nc.scalar.activation(gn_r, small[:, 80:82], ACT.Exp, bias=zero_b[:], scale=-0.5).then_inc(gn_act.sem, 1)
                    for k, (dst, bias) in enumerate([(F1, f1_b), (Z, None)]):
                        for o in range(DT):
                            for j, cs in halves(L1):
                                n = k * 4 + o * 2 + j
                                act.wait_ge(*conv_pe(n + 1))
                                bb = f1_b[:, o:o + 1] if k == 0 else vec("in_bz", o)
                                nc.scalar.activation(dst[:, o, cs], ps[:, n, :], ACT.Identity, bias=bb).then_inc(conv_act.sem, 1)
                    for k, (dst, n, name) in enumerate([(F2, L2, "c2_b"), (F3, L3, "c3_b")]):
                        for o in range(DT):
                            act.wait_ge(*conv_pe(8 + 2 * k + o + 1))
                            nc.scalar.activation(dst[:, o, :], ps[:, 2 * k + o, 0:n], ACT.Identity, bias=vec(name, o)).then_inc(conv_act.sem, 1)
                    act.wait_ge(*conv_act(8))
                    for o in range(DT):
                        nc.scalar.activation(ZE[:, o, :], Z[:, o, :], ACT.Exp, bias=zero_b[:], scale=-1.0).then_inc(conv_act.sem, 1)

                    def split(g, part):
                        k = g.index
                        if part == 0:
                            act.wait_ge(*prep_pe(3 * k + 1))
                            if k >= 2:
                                act.wait_ge(*c_rows(N_STATE * (k - 1)))
                                act.wait_ge(*prep_dve(10 * k))
                            elif k == 1:
                                act.wait_ge(*prep_dve(10 * k))
                            nc.scalar.activation(SPL[0:96, g.slot, 0:g.n], ps[0:96, AUX_BANK, 0:g.n], ACT.Copy).then_inc(prep_act.sem, 1)
                            nc.scalar.activation(DTS[DT_ROW:DT_ROW + R_DT, 0:g.n], ps[DT_ROW:DT_ROW + R_DT, AUX_BANK, 0:g.n], ACT.Copy)\
                                .then_inc(prep_act.sem, 1)
                        else:
                            act.wait_ge(*prep_dve(10 * k + 1))
                            nc.scalar.activation(SPL[32:64, g.slot, 0:g.n], SPLR[32:64, 0:g.n], ACT.Copy).then_inc(prep_act.sem, 1)
                            nc.scalar.activation(SPLT[64:96, 0:g.n], SPLR[64:96, 0:g.n], ACT.Copy).then_inc(prep_act.sem, 1)

                    def softplus(g, half):
                        k = g.index
                        act.wait_ge(*prep_pe(3 * k + 2 + half))
                        if half == 0 and k >= 2:
                            act.wait_ge(*scanned(2 * N_STATE * (k - 1)))
                        nc.scalar.activation(SPA[:, half, 0:g.n], ps[:, AUX_BANK, 0:g.n], ACT.Abs, bias=vec(f"dtb{g.params}", half)).then_inc(prep_act.sem, 1)
                        nc.scalar.activation(DELTA[:, g.slot, half, 0:g.n], ps[:, AUX_BANK, 0:g.n], ACT.Relu, bias=vec(f"dtb{g.params}", half))\
                            .then_inc(prep_act.sem, 1)

                    def softplus_logs(g):
                        k = 10 * g.index
                        act.wait_ge(*prep_act(k + 7))
                        nc.scalar.activation(SPA[:, :, 0:g.n], SPA[:, :, 0:g.n], ACT.Exp, bias=zero_b[:], scale=-1.0).then_inc(prep_act.sem, 1)
                        act.wait_ge(*prep_act(k + 9))
                        nc.scalar.activation(SPE[:, :, 0:g.n], SPA[:, :, 0:g.n], ACT.Ln, bias=one_b[:]).then_inc(prep_act.sem, 1)

                    def squares(g):
                        act.wait_ge(*ln_dve(LN_DVE_AT[g.index] + 3))
                        nc.scalar.activation(LSQS[:, :, 0:g.width], LY[:, :, 0:g.width], ACT.Square, bias=zero_b[:]).then_inc(ln_act.sem, 1)

                    def inverse_std(g):
                        act.wait_ge(*ln_pe(2 * g.index + 2))
                        if g.index:
                            act.wait_ge(*ln_dve(LN_DVE_AT[g.index]))
                        nc.scalar.activation(LR[:, 0:g.width], ps[:, AUX_BANK, 0:g.width], ACT.Ln, bias=eps_b[:]).then_inc(ln_act.sem, 1)
                        act.wait_ge(*ln_act(3 * g.index + 2))
                        nc.scalar.activation(LR[:, 0:g.width], LR[:, 0:g.width], ACT.Exp, bias=zero_b[:], scale=-0.5).then_inc(ln_act.sem, 1)

                    def upsample(g):
                        act.wait_ge(*ln_dve(LN_DVE_AT[g.index + 1]))
                        side = {3: 8, 2: 16}[g.level]
                        for h in range(DT):
                            src = Y[g.level][:, h, :].rearrange("p (h w) -> p h w", h=side).unsqueeze(3).broadcast_to((P, side, side, 2))
                            dst = Y[g.level - 1][:, h, :].rearrange("p (h a w c) -> p h a w c", h=side, a=2, c=2)
                            for a in range(2):
                                nc.scalar.activation(dst[:, :, a, :, :], src, ACT.Copy).then_inc(y_start.sem, 1)

                    split(GROUPS[0], 0)
                    split(GROUPS[0], 1)
                    softplus(GROUPS[0], 0)
                    softplus(GROUPS[0], 1)
                    softplus_logs(GROUPS[0])
                    for u in range(N_UNITS):
                        g, n = GROUPS[u // N_STATE], u % N_STATE
                        act.wait_ge(*c_rows(u + 1))
                        if u >= 2:
                            act.wait_ge(*weighed(2 * (u - 2) + 2))
                        nc.scalar.activation(CB[:, u % 2, 0:g.n], ps[:, C_BANK, 0:g.n], ACT.Copy).then_inc(c_kept.sem, 1)
                        if n == 0:
                            act.wait_ge(*prep_dve(10 * g.index + 9))
                        for half in range(DT):
                            if u:
                                act.wait_ge(*scanned(2 * (u - 1) + half + 1))
                            a = VEC[f"Al{g.params}"][0] + N_STATE * half + n
                            nc.scalar.activation(ps[:, DECAY_BANK[half], 0:g.n], DELTA[:, g.slot, half, 0:g.n], ACT.Exp, bias=zero_b[:],
                                                 scale=vecs[:, a:a + 1]).then_inc(decay.sem, 1)
                        if g.index and n == 3:
                            squares(GROUPS[g.index - 1])
                        if g.index and n == 4:
                            inverse_std(GROUPS[g.index - 1])
                        if g.index in (1, 2) and n == 9:
                            upsample(GROUPS[g.index - 1])
                        if g.index + 1 < NG:
                            if n == 7:
                                split(GROUPS[g.index + 1], 0)
                            if n == 8:
                                split(GROUPS[g.index + 1], 1)
                            if n in (9, 10):
                                softplus(GROUPS[g.index + 1], n - 9)
                            if n == 11:
                                softplus_logs(GROUPS[g.index + 1])
                    squares(GROUPS[NG - 1])
                    inverse_std(GROUPS[NG - 1])

                    def token_norm(which):
                        for j, cs in halves(L1):
                            k = which * 2 + j
                            for ct in range(CT):
                                act.wait_ge(*tn_dve(8 * k + ct + 1))
                                if ct >= 2:
                                    act.wait_ge(*tn_sq(2 * k + 1))
                                elif k > 0:
                                    act.wait_ge(*tn_sq(2 * k))
                                nc.scalar.activation(LSQ[:, ct % 2, :], TN[:, ct, cs], ACT.Square, bias=zero_b[:]).then_inc(tn_act.sem, 1)
                            act.wait_ge(*tn_sq(2 * k + 2))
                            if j == 1:
                                act.wait_ge(*tn_dve(8 * k))
                            nc.scalar.activation(LRS, ps[:, 2 * j + 1, :], ACT.Ln, bias=eps_b[:]).then_inc(tn_act.sem, 1)
                            act.wait_ge(*tn_act(6 * k + 5))
                            nc.scalar.activation(LRS, LRS, ACT.Exp, bias=zero_b[:], scale=-0.5).then_inc(tn_act.sem, 1)

                    token_norm(0)
                    for kt in range(KT):
                        act.wait_ge(*v_pe(kt + 1))
                        nc.scalar.activation(V[:, kt, :], ps[:, kt % 6, :], ACT.Copy).then_inc(v_act.sem, 1)
                    def double_bank(job, rows):
                        bank = 2 * (RING_AT[job] % 3)
                        return ps[rows, bank:bank + 2, :].rearrange("p a b -> p (a b)")

                    def qk_high(h):
                        act.wait_ge(*qk_pe(h + 1))
                        if h >= 2:
                            act.wait_ge(*s_pe(KT * (h - 2) + KT))
                        for which, src in ((0, LOWER), (2, UPPER), (1, UPPER)):
                            dst = LOWER if which == 1 else src
                            nc.scalar.activation(qk_parts[dst, h % 2, which, :], double_bank(("project", h, 0), src), ACT.Identity, bias=vec("qk_b", h, src))\
                                .then_inc(qk_hi.sem, 1)

                    qk_high(0)
                    qk_high(1)
                    for h in range(HEADS):
                        for kt in range(KT):
                            i = KT * h + kt
                            act.wait_ge(*s_pe(i + 1))
                            if i >= 4:
                                lh, lk = (i - 4) // KT, (i - 4) % KT
                                act.wait_ge(*pv_pe(i - 4 + 1))
                                act.wait_ge(*den_pool(7 * lh + max(lk, 1)))
                            nc.scalar.activation(PR[:, i % 4, :], double_bank(("scores", h, kt), slice(0, P)), ACT.Exp, bias=zero_b[:], scale=SCALE)\
                                .then_inc(s_exp.sem, 1)
                        if h + 2 < HEADS:
                            qk_high(h + 2)
                    token_norm(1)
                    for ht in range(HT):
                        act.wait_ge(*fc1_pe(ht + 1))
                        nc.scalar.activation(HM[:, ht, :], ps[:, ht % 6, :], ACT.Gelu, bias=vec("fc1_b", ht)).then_inc(fc1_act.sem, 1)

                @block.vector
                def _(dve):
                    dve.wait_ge(*x_in(32))
                    for ct in range(CT):
                        for j, cs in halves(L1):
                            nc.vector.bn_stats(gn_stats[:, ct, j, :], T[:, ct, cs]).then_inc(gn_dve.sem, 1)
                    dve.wait_ge(*gn_dve(8))
                    for ct in range(CT):
                        nc.vector.bn_aggr(gn_mv[:, ct, :], gn_stats[:, ct, :, :]).then_inc(gn_dve.sem, 1)
                    dve.wait_ge(*gn_pe(1))
                    nc.vector.tensor_tensor(gn_d.rearrange("p (a c) -> p a c", a=2), gn_mv[:, :, 0].rearrange("p (a c) -> p a c", a=2),
                                            ps[:, 0, 0:2].unsqueeze(1).broadcast_to((P, 2, 2)), ALU.subtract).then_inc(gn_dve.sem, 1)
                    dve.wait_ge(*gn_dve(13))
                    nc.vector.tensor_tensor(gn_sq, gn_d, gn_d, ALU.mult).then_inc(gn_dve.sem, 1)
                    dve.wait_ge(*gn_dve(14))
                    nc.vector.tensor_tensor(gn_sq, gn_sq, gn_mv[:, :, 1], ALU.add).then_inc(gn_dve.sem, 1)
                    nc.vector.tensor_copy(gn_m, ps[:, 0, 0:2]).then_inc(gn_dve.sem, 1)
                    dve.wait_ge(*gn_dve(16))
                    dve.wait_ge(*gn_act(2))
                    for ct in range(CT):
                        nc.vector.tensor_scalar(XN[:, ct, :], T[:, ct, :], gn_m[:, ct % 2:ct % 2 + 1], gn_r[:, ct % 2:ct % 2 + 1],
                                                ALU.subtract, ALU.mult).then_inc(gn_dve.sem, 1)
                    nc.vector.memset(Y3, 0.0).then_inc(y_start.sem, 1)
                    for o in range(DT):
                        dve.wait_ge(*conv_act(13 + o))
                        nc.vector.tensor_scalar(ZE[:, o, :], ZE[:, o, :], 1.0, None, ALU.add).then_inc(conv_dve.sem, 1)
                    for o in range(DT):
                        dve.wait_ge(*conv_dve(1 + o))
                        nc.vector.reciprocal(ZE[:, o, :], ZE[:, o, :]).then_inc(conv_dve.sem, 1)
                    for o in range(DT):
                        dve.wait_ge(*conv_dve(3 + o))
                        nc.vector.tensor_tensor(Z[:, o, :], Z[:, o, :], ZE[:, o, :], ALU.mult).then_inc(conv_dve.sem, 1)

                    def both(v, g):
                        return v.unsqueeze(1).broadcast_to((P, DT, v.shape[-1]))

                    def split(g, part):
                        k = 10 * g.index
                        if part == 0:
                            dve.wait_ge(*prep_act(k + 2))
                            nc.vector.tensor_tensor(SPLR[0:96, 0:g.n], ps[0:96, AUX_BANK, 0:g.n], SPL[0:96, g.slot, 0:g.n], ALU.subtract).then_inc(prep_dve.sem, 1)
                        else:
                            dve.wait_ge(*prep_act(k + 4))
                            nc.vector.tensor_tensor(SPL[64:96, g.slot, 0:g.n], SPLR[64:96, 0:g.n], SPLT[64:96, 0:g.n], ALU.subtract).then_inc(prep_dve.sem, 1)

                    def softplus(g, part):
                        k = 10 * g.index
                        p, e, ln = SPP[:, :, 0:g.n], SPA[:, :, 0:g.n], SPE[:, :, 0:g.n]
                        if part == 0:
                            dve.wait_ge(*prep_act(k + 9))
                            dve.wait_ge(*prep_dve(k + 2))
                            nc.vector.tensor_scalar(p, e, -0.25, None, ALU.mult).then_inc(prep_dve.sem, 1)
                            for step, coef in enumerate((1 / 3, -0.5, 1.0)):
                                dve.wait_ge(*prep_dve(k + 3 + step))
                                nc.vector.scalar_tensor_tensor(out=p, in0=p, scalar=coef, in1=e, op0=ALU.add, op1=ALU.mult).then_inc(prep_dve.sem, 1)
                        else:
                            dve.wait_ge(*prep_act(k + 10))
                            nc.vector.scalar_tensor_tensor(out=ln, in0=e, scalar=E_SMALL, in1=ln, op0=ALU.is_ge, op1=ALU.mult).then_inc(prep_dve.sem, 1)
                            dve.wait_ge(*prep_dve(k + 7))
                            nc.vector.tensor_tensor(p, p, ln, ALU.max).then_inc(prep_dve.sem, 1)
                            dve.wait_ge(*prep_dve(k + 8))
                            delta, du = DELTA[:, g.slot, :, 0:g.n], DU[:, g.slot, :, 0:g.n]
                            nc.vector.tensor_tensor(delta, delta, p, ALU.add).then_inc(prep_dve.sem, 1)
                            dve.wait_ge(*prep_dve(k + 9))
                            if g.index >= 2:
                                dve.wait_ge(*driven(2 * N_STATE * (g.index - 1)))
                            nc.vector.tensor_tensor(du, delta, F[g.level][:, :, g.cols], ALU.mult).then_inc(prep_dve.sem, 1)

                    def drive(u, half):
                        g, s = GROUPS[u // N_STATE], 2 * u + half
                        dve.wait_ge(*b_rows(u + 1))
                        if u % N_STATE == 0:
                            dve.wait_ge(*prep_dve(10 * g.index + 10))
                        if u == 0:
                            dve.wait_ge(*conv_dve(6))
                        if s >= 3:
                            dve.wait_ge(*scanned(s - 2))
                        nc.vector.tensor_tensor(DBX[:, s % 3, 0:g.n], DU[:, g.slot, half, 0:g.n], ps[:, B_BANK[u % 2], 0:g.n], ALU.mult).then_inc(driven.sem, 1)

                    def scan(u, half):
                        g, n, s = GROUPS[u // N_STATE], u % N_STATE, 2 * u + half
                        dve.wait_ge(*driven(s + 1))
                        dve.wait_ge(*decay(s + 1))
                        if s >= 4:
                            dve.wait_ge(*weighed(s - 3))
                        start = 0.0
                        if not g.first:
                            dve.wait_ge(*state_kept(2 * N_STATE * KEEPS[g.index - 1] + 2 * n + half + 1))
                            start = STATE[:, half, n:n + 1]
                        for i, d in enumerate(g.dirs):
                            w = slice(None, None, -1 if d else 1)
                            ins = nc.vector.tensor_tensor_scan(H[:, s % 4, g.n * i:g.n * i + g.n][:, w], ps[:, DECAY_BANK[half], 0:g.n][:, w],
                                                               DBX[:, s % 3, 0:g.n][:, w], start, ALU.mult, ALU.add)
                        ins.then_inc(scanned.sem, 1)

                    def norm_sums(g):
                        k = LN_DVE_AT[g.index]
                        for h in range(DT):
                            dve.wait_ge(*summed(2 * N_STATE * g.index + 2 * N_STATE - 1 + h))
                            if g.index:
                                dve.wait_ge(*ln_dve(k))
                            f = F[g.level][:, h, g.cols].unsqueeze(1).broadcast_to((P, len(g.dirs), g.n))
                            o, y = (v.rearrange("p (d n) -> p d n", n=g.n) for v in (LY[:, h, 0:g.width], ps[:, Y_BANK[h], 0:g.width]))
                            nc.vector.scalar_tensor_tensor(out=o, in0=f, scalar=vec(f"Dv{g.params}", h), in1=y, op0=ALU.mult, op1=ALU.add).then_inc(ln_dve.sem, 1)

                    def norm_center(g):
                        dve.wait_ge(*ln_pe(2 * g.index + 1))
                        y = LY[:, :, 0:g.width]
                        nc.vector.tensor_tensor(y, y, both(ps[:, AUX_BANK, 0:g.width], g), ALU.subtract).then_inc(ln_dve.sem, 1)

                    def norm_scale(g):
                        dve.wait_ge(*ln_act(3 * g.index + 3))
                        for h in range(DT):
                            nc.vector.scalar_tensor_tensor(out=LY[:, h, 0:g.width], in0=LY[:, h, 0:g.width], scalar=vec(f"g{g.params}", h),
                                                           in1=LR[:, 0:g.width], op0=ALU.mult, op1=ALU.mult).then_inc(ln_dve.sem, 1)

                    def norm_add(g):
                        k = LN_DVE_AT[g.index]
                        dve.wait_ge(*y_start({3: 1, 2: 5, 1: 9}[g.level]))
                        for i, d in enumerate(g.dirs):
                            for h in range(DT):
                                dve.wait_ge(*ln_dve(k + 4 + h + 2 * i))
                                y = Y[g.level][:, h, g.cols]
                                nc.vector.scalar_tensor_tensor(out=y, in0=LY[:, h, g.n * i:g.n * i + g.n], scalar=vec(f"be{g.params}", h), in1=y,
                                                               op0=ALU.add, op1=ALU.add).then_inc(ln_dve.sem, 1)

                    split(GROUPS[0], 0)
                    split(GROUPS[0], 1)
                    softplus(GROUPS[0], 0)
                    softplus(GROUPS[0], 1)
                    drive(0, 0)
                    drive(0, 1)
                    for u in range(N_UNITS):
                        g, n = GROUPS[u // N_STATE], u % N_STATE
                        for half in range(DT):
                            scan(u, half)
                            if u + 1 < N_UNITS:
                                drive(u + 1, half)
                        if g.index and n == 0:
                            norm_sums(GROUPS[g.index - 1])
                        if g.index and n == 2:
                            norm_center(GROUPS[g.index - 1])
                        if g.index and n == 5:
                            norm_scale(GROUPS[g.index - 1])
                        if g.index and n == 6:
                            norm_add(GROUPS[g.index - 1])
                        if g.index + 1 < NG:
                            if n in (7, 8):
                                split(GROUPS[g.index + 1], n - 7)
                            if n in (12, 13):
                                softplus(GROUPS[g.index + 1], n - 12)
                    norm_sums(GROUPS[NG - 1])
                    norm_center(GROUPS[NG - 1])
                    norm_scale(GROUPS[NG - 1])
                    norm_add(GROUPS[NG - 1])
                    dve.wait_ge(*ln_dve(LN_DVE_AT[NG]))
                    dve.wait_ge(*conv_dve(6))
                    for h in range(DT):
                        nc.vector.tensor_tensor(Y1[:, h, :], Y1[:, h, :], Z[:, h, :], ALU.mult).then_inc(gated.sem, 1)
                    for ct in range(CT):
                        for j, cs in halves(L1):
                            n = ct * 2 + j
                            dve.wait_ge(*out_pe(n + 1))
                            nc.vector.scalar_tensor_tensor(out=T[:, ct, cs], in0=ps[:, n, :], scalar=vec("out_b", ct), in1=T[:, ct, cs],
                                                           op0=ALU.add, op1=ALU.add).then_inc(out_dve.sem, 1)

                    def token_norm(which):
                        for j, cs in halves(L1):
                            k = which * 2 + j
                            dve.wait_ge(*(out_dve, proj_dve)[which](8))
                            dve.wait_ge(*tn_pe(k + 1))
                            for ct in range(CT):
                                nc.vector.tensor_tensor(TN[:, ct, cs], T[:, ct, cs], ps[:, 2 * j, :], ALU.subtract).then_inc(tn_dve.sem, 1)
                            dve.wait_ge(*tn_act(6 * k + 6))
                            for ct in range(CT):
                                nc.vector.tensor_tensor(TN[:, ct, cs], TN[:, ct, cs], LRS, ALU.mult).then_inc(tn_dve.sem, 1)

                    token_norm(0)
                    def double_bank(job, rows):
                        bank = 2 * (RING_AT[job] % 3)
                        return ps[rows, bank:bank + 2, :].rearrange("p a b -> p (a b)")

                    def qk_low(h):
                        dve.wait_ge(*qk_hi(3 * h + 3))
                        for which, src in ((0, LOWER), (1, UPPER), (2, UPPER)):
                            dst = (UPPER, UPPER, LOWER)[which]
                            nc.vector.scalar_tensor_tensor(out=qk_parts[dst, h % 2, which, :], in0=double_bank(("project", h, 0), src),
                                                           scalar=vec("qk_b", h, src), in1=qk_parts[src, h % 2, 0 if which == 0 else 2, :],
                                                           op0=ALU.add, op1=ALU.subtract).then_inc(qk_lo.sem, 1)

                    def find_maxima(h):
                        e = h % 2
                        for qt in range(KT):
                            dve.wait_ge(*smax_pe(KT * h + qt + 1))
                            nc.vector.tensor_reduce(maxima[:, e, qt:qt + 1], double_bank(("smax", h, qt), slice(0, P)), AX_X, ALU.max)\
                                .then_inc(smax_dve.sem, 1)
                        dve.wait_ge(*smax_dve(KT * h + KT))
                        nc.vector.tensor_copy(maxima[:, e, 32:40], maxima[:, e, 0:8]).then_inc(mt_dve.sem, 1)

                    def rows_of_maxima(h):
                        half = slice(64 * (h % 2), 64 * (h % 2) + 64)
                        low = slice(half.start + 32, half.stop)
                        dve.wait_ge(*mt_pe(h + 1))
                        nc.vector.tensor_copy(rows[half, :], ps[half, 7, 0:P]).then_inc(mt_dve.sem, 1)
                        dve.wait_ge(*mt_dve(4 * h + 2))
                        nc.vector.tensor_tensor(rows[low, :], ps[low, 7, 0:P], rows[low, :], ALU.subtract).then_inc(mt_dve.sem, 1)
                        dve.wait_ge(*mt_dve(4 * h + 3))
                        nc.vector.tensor_tensor(RH[half], rows[half, :].unsqueeze(1).broadcast_to((64, KT, P)),
                                                mask8[half, :].unsqueeze(2).broadcast_to((64, KT, P)), ALU.mult).then_inc(mt_dve.sem, 1)

                    def divide(h):
                        dve.wait_ge(*den_pe(h + 1))
                        nc.vector.reciprocal(REC, ps[:, 7, :]).then_inc(o_dve.sem, 1)
                        dve.wait_ge(*o_dve(3 * h + 1))
                        dve.wait_ge(*pv_pe(KT * h + KT))
                        for j, cs in halves(L1):
                            src, dst = slice(64 * j, 64 * j + 64), slice(64 * (h % 2), 64 * (h % 2) + 64)
                            nc.vector.tensor_tensor(O[dst, h // 2, cs], REC[src, :], ps[src, 6, :], ALU.mult).then_inc(o_dve.sem, 1)

                    qk_low(0)
                    qk_low(1)
                    find_maxima(0)
                    rows_of_maxima(0)
                    for h in range(HEADS):
                        if h:
                            divide(h - 1)
                        if h + 1 < HEADS:
                            find_maxima(h + 1)
                            rows_of_maxima(h + 1)
                        if h + 2 < HEADS:
                            qk_low(h + 2)
                    divide(HEADS - 1)
                    for ct in range(CT):
                        for j, cs in halves(L1):
                            n = ct * 2 + j
                            dve.wait_ge(*proj_pe(n + 1))
                            nc.vector.scalar_tensor_tensor(out=T[:, ct, cs], in0=ps[:, n, :], scalar=o_b[:, ct:ct + 1], in1=T[:, ct, cs],
                                                           op0=ALU.add, op1=ALU.add).then_inc(proj_dve.sem, 1)
                    token_norm(1)
                    dve.wait_ge(*tn_dve(32))
                    for j in range(DT):
                        nc.vector.tensor_tensor(LS[:, j, :], TN[:, j, :], TN[:, j + 2, :], ALU.add).then_inc(ll_dve.sem, 1)
                    for j in range(DT):
                        dve.wait_ge(*ll_dve(1 + j))
                        nc.vector.tensor_tensor(LL[:, j, :], LS[:, j, 0:L1:2], LS[:, j, 1:L1:2], ALU.add).then_inc(ll_dve.sem, 1)
                    for j in range(DT):
                        dve.wait_ge(*ll_dve(3 + j))
                        nc.vector.tensor_scalar(LL[:, j, :], LL[:, j, :], 0.5, None, ALU.mult).then_inc(ll_dve.sem, 1)
                    dve.wait_ge(*ll_dve(6))
                    for ct in range(CT):
                        nc.vector.tensor_tensor(T[:, ct, :], T[:, ct, :], TN[:, ct, :], ALU.add).then_inc(fin_dve.sem, 1)
                    for o in range(DT):
                        dve.wait_ge(*fc2_pe(o + 1))
                        nc.vector.scalar_tensor_tensor(out=DL[:, o, :], in0=ps[:, 6 + o, :], scalar=vec("fc2_b", o), in1=LL[:, o, :],
                                                       op0=ALU.add, op1=ALU.subtract).then_inc(fin_dve.sem, 1)
                    for o in range(DT):
                        dve.wait_ge(*fin_dve(5 + o))
                        nc.vector.tensor_scalar(DL[:, o, :], DL[:, o, :], 0.5, None, ALU.mult).then_inc(fin_dve.sem, 1)
                    dve.wait_ge(*fin_dve(8))
                    for ct in range(CT):
                        tv = T[:, ct, :].rearrange("p (f two) -> p f two", two=2)
                        nc.vector.tensor_tensor(tv, tv, DL[:, ct % 2, :].unsqueeze(2).broadcast_to((P, BANK, 2)), ALU.add).then_inc(fin_dve.sem, 1)

                @block.gpsimd
                def _(pool):
                    for u in range(N_UNITS):
                        g, n = GROUPS[u // N_STATE], u % N_STATE
                        pool.wait_ge(*c_kept(u + 1))
                        c = CB[:, u % 2, 0:g.n].unsqueeze(1).broadcast_to((P, len(g.dirs), g.n))
                        for half in range(DT):
                            s = 2 * u + half
                            pool.wait_ge(*scanned(s + 1))
                            if g.index in KEEPS:
                                last = 0 if g.dirs[0] else g.n - 1
                                nc.gpsimd.tensor_copy(STATE[:, half, n:n + 1], H[:, s % 4, last:last + 1]).then_inc(state_kept.sem, 1)
                            if s >= 3:
                                pool.wait_ge(*summed(s - 2))
                            h, hc = (v[:, r, 0:g.width].rearrange("p (d n) -> p d n", n=g.n) for v, r in ((H, s % 4), (HC, s % 3)))
                            nc.gpsimd.tensor_tensor(hc, h, c, ALU.mult).then_inc(weighed.sem, 1)
                    for h in range(HEADS):
                        for kt in range(1, KT):
                            i = KT * h + kt
                            pool.wait_ge(*s_exp(i + 1))
                            if kt == 1 and h >= 2:
                                pool.wait_ge(*den_pe(h - 1))
                            if kt > 1:
                                pool.wait_ge(*den_pool(7 * h + kt - 1))
                            sums = DEN[:, h % 2, :]
                            nc.gpsimd.tensor_tensor(sums, PR[:, 0, :] if kt == 1 else sums, PR[:, i % 4, :], ALU.add).then_inc(den_pool.sem, 1)


            nc.all_engine_barrier(sems_to_clear=range(min(s.sem.num for s in signals), max(s.sem.num for s in signals) + 1))


def tiles(a):
    n = a.shape[0] // P
    return a.reshape(n, P, -1).transpose(1, 0, 2)


def kernel(**inputs):
    import numpy as np
    import concourse.bacc as bacc
    from concourse.bass_utils import run_bass_kernel_spmd

    w = {k: np.asarray(v) for k, v in inputs.items()}
    g = {k[8:]: v for k, v in w.items() if k.startswith("L0_conv_")}
    perm = np.concatenate([np.arange(0, C, 2), np.arange(1, C, 2)])

    ident = np.eye(P, dtype=np.float32)
    gmat = np.kron(np.eye(16, dtype=np.float32), np.full((8, 8), 1 / 16, np.float32))
    sel = np.zeros((96, 2 * N_STATE, P), np.float32)
    for r in range(96):
        sel[r, r % 32] = 1
    neg = np.zeros((P, P), np.float32)
    mask8 = np.zeros((P, KT), np.float32)
    for r in range(P):
        if r % 32 < KT:
            neg[r] = -1
            mask8[r, r % 32] = 1
    pos = np.linspace(0.0, 1.0, C, dtype=np.float32) * np.float32(C // 2 - 1)
    i0 = np.clip(np.floor(pos).astype(np.int32), 0, C // 2 - 2)
    frac = (pos - i0.astype(np.float32)).astype(np.float32)
    up = np.zeros((C, C // 2), np.float32)
    up[np.arange(C), i0] = np.float32(1.0) - frac
    up[np.arange(C), i0 + 1] = frac

    qk_rows = [part * C + HD * h + i for h in range(HEADS) for part in range(2) for i in range(HD)]
    xrows = list(range(R_DT, R_DT + 2 * N_STATE)) * 3 + list(range(R_DT))
    cols = {"in_bx": g["in_b"][:D], "in_bz": g["in_b"][D:], "c1_b": g["c1_b"], "c2_b": g["c2_b"], "c3_b": g["c3_b"],
            "out_b": g["out_b"][perm], "qk_b": w["L1_attn_qkv_b"][qk_rows], "v_b": w["L1_attn_qkv_b"][2 * C:],
            "proj_b": w["L1_attn_proj_b"][perm], "fc1_b": w["L1_ffn_fc1_b"], "fc2_b": w["L1_ffn_fc2_b"]}
    for s in (1, 2, 3):
        cols |= {f"{v}{s}": g[f"{v}{s}"] for v in ("dtb", "Dv", "g", "be")}
        cols[f"Al{s}"] = g[f"Al{s}"]
    vecs = np.concatenate([tiles(cols[n]).reshape(P, -1) for n in VEC], axis=1)
    arrays = {
        "x": w["x"].reshape(B, C, L1),
        "in_x": tiles(g["in_w"][:D][:, perm]), "in_z": tiles(g["in_w"][D:][:, perm].T), "c1": tiles(g["c1_w"].T),
        "c2": tiles(g["c2_w"].transpose(1, 2, 3, 0).reshape(D, -1)), "c3": tiles(g["c3_w"].transpose(1, 2, 3, 0).reshape(D, -1)),
        "out": tiles(g["out_w"][perm].T), "up": tiles(up), "fc1": tiles(w["L1_ffn_fc1_w"].T), "fc2": tiles(w["L1_ffn_fc2_w"].T),
        "qkv": tiles(w["L1_attn_qkv_w"][qk_rows + list(range(2 * C, 3 * C))][:, perm].T), "proj": tiles(w["L1_attn_proj_w"][perm].T),
        "vecs": vecs, "ident": ident, "gmat": gmat, "sel": sel, "neg": neg, "mask8": mask8,
    }
    for s in (1, 2, 3):
        arrays[f"xw{s}"] = tiles(g[f"xw{s}"][xrows].T)
        arrays[f"dtw{s}"] = g[f"dtw{s}"].T
    for k in ("c2", "c3"):
        arrays[k] = arrays[k].reshape(P, DT, 4, D)
    arrays = {k: np.ascontiguousarray(v) for k, v in arrays.items()}

    nc = bacc.Bacc("TRN2", target_bir_lowering=False, num_devices=1)
    t = {k: nc.dram_tensor(f"in_{k}", v.shape, mybir.dt.from_np(v.dtype), kind="ExternalInput").ap() for k, v in arrays.items()}
    t["y"] = nc.dram_tensor("out", (B, C, L1), F32, kind="ExternalOutput").ap()
    build(nc, t)
    r = run_bass_kernel_spmd(nc, [{f"in_{k}": v for k, v in arrays.items()}], core_ids=[0])
    return r.results[0]["out"].reshape(B, C, 32, 32)
```

```python
from contextlib import ExitStack

import numpy as np
import concourse.bass as bass
from concourse import mybir

ALU = mybir.AluOpType
ACT = mybir.ActivationFunctionType
AX_X = mybir.AxisListType.X
F32 = mybir.dt.float32
F32R = mybir.dt.float32r
BF16 = mybir.dt.bfloat16

P = 128
BANK = 512
B = 8
C, CT = 512, 4
D, DT = 256, 2
L1, L2, L3 = 1024, 256, 64
N_STATE, R_DT = 16, 8
XD = 3 * 2 * N_STATE + R_DT
DT_ROW = 3 * 2 * N_STATE
HEADS, HD = 8, 64
LOWER, UPPER = slice(0, HD), slice(HD, 2 * HD)
KT = L1 // P
HID, HT = 2048, 16
LN_EPS = 1e-5
SCALE = HD ** -0.5
E_SMALL = 1 / 64

VEC = {}
_at = 0
for _name, _n in [("in_bx", 2), ("in_bz", 2), ("c1_b", 2), ("c2_b", 2), ("c3_b", 2), ("out_b", 4), ("qk_b", 8),
                  ("v_b", 4), ("proj_b", 4), ("fc1_b", 16), ("fc2_b", 2)] + \
        [(f"{v}{s}", 2) for s in (1, 2, 3) for v in ("dtb", "Dv", "g", "be")] + [(f"Al{s}", 32) for s in (1, 2, 3)]:
    VEC[_name] = (_at, _n)
    _at += _n
N_VEC = _at


SMAX_AFTER = {2: (0,), 3: (1, 2), 4: (3, 4), 5: (5, 6), 6: (7,)}
RING = [("project", 0, 0), ("project", 1, 0)] + [("smax", 0, _i) for _i in range(KT)]
for _h in range(HEADS):
    for _kt in range(KT):
        RING.append(("scores", _h, _kt))
        RING += [("smax", _h + 1, _i) for _i in SMAX_AFTER.get(_kt, ()) if _h + 1 < HEADS]
    if _h + 2 < HEADS:
        RING.append(("project", _h + 2, 0))
RING_AT = {_job: _i for _i, _job in enumerate(RING)}
PV_AFTER = {3: (0, 1), 4: (2,), 5: (3,), 6: (4,), 7: (5,)}
PV_LAST = (6, 7)


class Signal:

    def __init__(self, sem, per_image):
        self.sem, self.per_image = sem, per_image

    def __call__(self, k):
        assert 0 < k <= self.per_image
        return self.sem, k


GN_RAISES = {"x_in": 32, "dve": 8 + 4 + 3 + 1 + 4, "pe": 2, "act": 2}


PREP_ACT, PREP_DVE = 11, 8

SERIES = np.roots([-1 / 4, 1 / 3, -1 / 2, 1])
ROOT_R = float(SERIES[abs(SERIES.imag) < 1e-9][0].real)
ROOT_A, ROOT_B = float(SERIES[SERIES.imag > 1e-9][0].real), float(SERIES[SERIES.imag > 1e-9][0].imag)


class Group:

    def __init__(self, index, level, params, dirs, c0, n, first):
        self.index, self.level, self.params, self.dirs, self.c0, self.n, self.first = index, level, params, dirs, c0, n, first
        self.slot = index % 2
        self.width = n * len(dirs)
        self.cols = slice(c0, c0 + n)


GROUPS = [Group(i, *g) for i, g in enumerate([
    (1, 1, (0,), 0, BANK, True),
    (1, 1, (0,), BANK, BANK, False),
    (3, 3, (0, 1), 0, L3, True),
    (2, 2, (0, 1), 0, L2, True),
    (1, 2, (1,), BANK, BANK, True),
    (1, 2, (1,), 0, BANK, False),
])]
NG = len(GROUPS)
N_UNITS = NG * N_STATE
KEEPS = {0: 0, 4: 1}
LN_DVE = [5 + 2 * len(g.dirs) for g in GROUPS]
LN_DVE_AT = [sum(LN_DVE[:i]) for i in range(NG + 1)]
B_BANK, C_BANK, DECAY_BANK, Y_BANK, AUX_BANK = (0, 1), 2, (3, 4), (5, 6), 7


def build(nc, t):
    with ExitStack() as ctx:
        def sb(name, shape, dt=F32):
            return ctx.enter_context(nc.sbuf_tensor(name, shape, dt))

        signals = []

        def signal(name, per_image):
            signals.append(Signal(ctx.enter_context(nc.semaphore(name)), per_image))
            return signals[-1]

        def sem(name):
            return ctx.enter_context(nc.semaphore(name))

        wf = sb("wf", [P, CT, D])
        wz = sb("wz", [P, CT, D])
        wout = sb("wout", [P, DT, C])
        xw = {s: sb(f"xw{s}", [P, DT, XD]) for s in (1, 2, 3)}
        dtw = {s: sb(f"dtw{s}", [P, D]) for s in (1, 2, 3)}
        wqkv = sb("wqkv", [P, CT, 3 * C])
        w1 = sb("w1", [P, DT, HID])
        qk_parts = sb("qk_parts", [P, 2, 3, L1], F32R)
        vecs = sb("vecs", [P, N_VEC])
        ident = sb("ident", [P, P])
        gmat = sb("gmat", [P, P])
        ones = sb("ones", [P, P])
        ones_c = sb("ones_c", [P, P])
        ones_d = sb("ones_d", [P, P])
        zero_b = sb("zero_b", [P, 1])
        eps_b = sb("eps_b", [P, 1])
        one_b = sb("one_b", [P, 1])
        root_b = sb("root_b", [P, 1])
        sel = sb("sel", [96, 2 * N_STATE, P], BF16)
        neg = sb("neg", [P, P], BF16)
        mask8 = sb("mask8", [P, KT])
        f1_b = sb("f1_b", [P, DT])
        o_b = sb("o_b", [P, CT])
        small = sb("small", [P, 96])
        gn_stats = small[:, 0:48].rearrange("p (c j s) -> p c j s", c=CT, j=2)
        gn_mv = small[:, 48:56].rearrange("p (c s) -> p c s", c=CT)
        gn_d, gn_sq, gn_m = small[:, 56:60], small[:, 60:64], small[:, 64:66]
        gn_r = small[:, 84:86]
        maxima = sb("maxima", [P, 2, 64])
        rows = sb("rows", [P, P], BF16)

        arena = sb("arena", [P, 28448])
        taken = [0]

        def region(at, shape, dt=F32):
            n = 1
            for s in shape:
                n *= s
            words = n if dt == F32 else n // 2
            taken[0] = max(taken[0], at + words)
            a = arena[:, at:at + words]
            if dt != F32:
                a = a.bitcast(dt)
            if len(shape) == 2:
                a = a.rearrange("p (a b) -> p a b", a=shape[0])
            elif len(shape) == 3:
                a = a.rearrange("p (a b c) -> p a b c", a=shape[0], b=shape[1])
            return a

        T = region(0, [CT, L1])
        XN = region(4096, [CT, L1])
        XP = region(18432, [CT, L1])
        C2 = region(22528, [DT, 4, D])
        C3 = region(24576, [DT, 4, D])
        F1 = region(12288, [DT, L1])
        F2 = region(14336, [DT, L2])
        F3 = region(14848, [DT, L3])
        Z = region(14976, [DT, L1])
        Y1 = region(17024, [DT, L1])
        Y2 = region(19072, [DT, L2])
        Y3 = region(19584, [DT, L3])
        ZE = region(19712, [DT, L1])
        F = {1: F1, 2: F2, 3: F3}
        Y = {1: Y1, 2: Y2, 3: Y3}
        DELTA = region(4096, [2, DT, BANK])
        DU = region(6144, [2, DT, BANK])
        SPL = region(8192, [2, BANK], BF16)
        SPLR = region(8704, [BANK])
        DTS = region(9216, [BANK])
        SPLT = region(9728, [BANK], BF16)
        SPA = region(9984, [DT, BANK])
        SPE = region(11008, [DT, BANK])
        SPP = region(8704, [DT, BANK])
        DBX = region(19712, [3, BANK])
        H = region(21248, [4, BANK])
        HC = region(23296, [3, BANK])
        CB = region(24832, [2, BANK])
        LY = region(25856, [DT, BANK])
        LR = region(26880, [BANK])
        LSQS = region(27392, [DT, BANK])
        STATE = region(28416, [DT, N_STATE])
        TN = region(4096, [CT, L1])
        WPROJ = region(8192, [CT, C])
        V = region(12288, [KT, C])
        PR = region(16384, [4, L1])
        O = region(20480, [CT, L1])
        DEN = region(24576, [2, L1])
        REC = region(27136, [BANK])
        RH = region(26624, [KT, P], BF16)
        LSQ = region(12288, [2 * CT, BANK])
        LRS = region(27648, [BANK])
        W2 = region(22528, [HT, D])
        LL = region(8192, [DT, BANK])
        LS = region(9216, [DT, L1])
        HM = region(9216, [HT, BANK])
        DL = region(17408, [DT, BANK])
        S_INW = region(0, [DT, C])
        S_C1 = region(1024, [DT, D])
        S_U = region(1536, [CT, D])
        S_FC1 = region(2560, [CT, HID])
        S_SEL = region(10752, [2 * N_STATE, P])
        S_NEG = region(14848, [P])
        S_PROJ = region(15104, [CT, C])
        assert taken[0] <= 28448

        ps = ctx.enter_context(nc.psum_tensor("ps", [P, 8, BANK], F32))

        def vec(name, i, rows=slice(0, P)):
            a = VEC[name][0] + i
            return vecs[rows, a:a + 1]

        weights_in = sem("weights_in")
        consts_set = sem("consts_set")
        setup_pe = sem("setup_pe")
        setup_act = sem("setup_act")
        setup_dve = sem("setup_dve")

        gn_first = {name: Signal(sem(f"gn_first_{name}"), n) for name, n in GN_RAISES.items()}

        x_in = signal("x_in", 32)
        c23_in = signal("c23_in", 32)
        proj_in = signal("proj_in", 16)
        w2_in = signal("w2_in", 16)
        stored = signal("stored", 16 * CT)
        gn_next = {name: signal(f"gn_{name}", n) for name, n in GN_RAISES.items()}
        conv_pe = signal("conv_pe", 8 + 4)
        conv_act = signal("conv_act", 4 + 4 + 4 + 2)
        conv_dve = signal("conv_dve", 6)
        prep_pe = signal("prep_pe", 3 * NG)
        prep_act = signal("prep_act", PREP_ACT * NG)
        prep_dve = signal("prep_dve", PREP_DVE * NG)
        b_rows = signal("b_rows", N_UNITS)
        c_rows = signal("c_rows", N_UNITS)
        c_kept = signal("c_kept", N_UNITS)
        decay = signal("decay", DT * N_UNITS)
        driven = signal("driven", DT * N_UNITS)
        scanned = signal("scanned", DT * N_UNITS)
        state_kept = signal("state_kept", DT * N_STATE * len(KEEPS))
        weighed = signal("weighed", DT * N_UNITS)
        summed = signal("summed", DT * N_UNITS)
        ln_pe = signal("ln_pe", 2 * NG)
        ln_act = signal("ln_act", 4 * NG)
        ln_dve = signal("ln_dve", LN_DVE_AT[NG])
        y_start = signal("y_start", 1 + 4)
        y_add = signal("y_add", 4)
        gated = signal("gated", 4)
        out_pe = signal("out_pe", 8)
        out_dve = signal("out_dve", 8)
        tn_pe = signal("tn_pe", 4)
        tn_sq = signal("tn_sq", 4)
        tn_dve = signal("tn_dve", 4 * 8)
        tn_act = signal("tn_act", 4 * 6)
        v_pe = signal("v_pe", KT)
        v_act = signal("v_act", KT)
        qk_pe = signal("qk_pe", HEADS)
        qk_hi = signal("qk_hi", 3 * HEADS)
        qk_lo = signal("qk_lo", 3 * HEADS)
        smax_pe = signal("smax_pe", KT * HEADS)
        smax_dve = signal("smax_dve", KT * HEADS)
        mt_dve = signal("mt_dve", 4 * HEADS)
        mt_pe = signal("mt_pe", HEADS)
        s_pe = signal("s_pe", KT * HEADS)
        s_exp = signal("s_exp", KT * HEADS)
        pv_pe = signal("pv_pe", KT * HEADS)
        den_pool = signal("den_pool", (KT - 1) * HEADS)
        den_pe = signal("den_pe", HEADS)
        o_dve = signal("o_dve", 3 * HEADS)
        proj_pe = signal("proj_pe", 8)
        proj_dve = signal("proj_dve", 8)
        ll_dve = signal("ll_dve", 8)
        fc1_pe = signal("fc1_pe", HT)
        fc1_act = signal("fc1_act", HT)
        fc2_pe = signal("fc2_pe", 2)
        fin_dve = signal("fin_dve", 4 + 8)

        CHUNKS = ((0, slice(BANK, L1)), (1, slice(0, BANK)))
        V_TILES = tuple(zip((4, 5, 6, 7, 0, 1, 2, 3), (2, 3, 6, 7, 6, 7, 6, 7)))

        def halves(n):
            return [(j, slice(BANK * j, BANK * j + BANK)) for j in range(n // BANK)]

        def load_ahead(sp, s, image):
            for two in range(2):
                sp.dma_start(XP[:, 2 * two:2 * two + 2, :], image.rearrange("(j p two) l -> two p j l", p=P, two=2)[two]).then_inc(s["x_in"].sem, 16)

        def group_means(pe, s, k, bank):
            pe.wait_ge(*s["dve"]((12, 15)[k]))
            src = (gn_mv[:, :, 0], gn_sq)[k]
            pe.matmul(ps[:, bank + k, 0:2], gmat[:], src[:, 0:2], start=True, stop=False)
            pe.matmul(ps[:, bank + k, 0:2], gmat[:], src[:, 2:4], start=False, stop=True).then_inc(s["pe"].sem, 1)

        def group_std(act, s, bank):
            act.wait_ge(*s["pe"](2))
            nc.scalar.activation(small[:, 80:82], ps[:, bank + 1, 0:2], ACT.Ln, bias=eps_b[:]).then_inc(s["act"].sem, 1)
            act.wait_ge(*s["act"](1))
            nc.scalar.activation(gn_r, small[:, 80:82], ACT.Exp, bias=zero_b[:], scale=-0.5).then_inc(s["act"].sem, 1)

        def group_norm(dve, s, bank):
            dve.wait_ge(*s["x_in"](32))
            for ct in range(CT):
                for j, cs in halves(L1):
                    nc.vector.bn_stats(gn_stats[:, ct, j, :], XP[:, ct, cs]).then_inc(s["dve"].sem, 1)
            dve.wait_ge(*s["dve"](8))
            for ct in range(CT):
                nc.vector.bn_aggr(gn_mv[:, ct, :], gn_stats[:, ct, :, :]).then_inc(s["dve"].sem, 1)
            dve.wait_ge(*s["pe"](1))
            nc.vector.tensor_tensor(gn_d.rearrange("p (a c) -> p a c", a=2), gn_mv[:, :, 0].rearrange("p (a c) -> p a c", a=2),
                                    ps[:, bank, 0:2].unsqueeze(1).broadcast_to((P, 2, 2)), ALU.subtract).then_inc(s["dve"].sem, 1)
            dve.wait_ge(*s["dve"](13))
            nc.vector.tensor_tensor(gn_sq, gn_d, gn_d, ALU.mult).then_inc(s["dve"].sem, 1)
            dve.wait_ge(*s["dve"](14))
            nc.vector.tensor_tensor(gn_sq, gn_sq, gn_mv[:, :, 1], ALU.add).then_inc(s["dve"].sem, 1)
            nc.vector.tensor_copy(gn_m, ps[:, bank, 0:2]).then_inc(s["dve"].sem, 1)
            dve.wait_ge(*s["dve"](16))
            dve.wait_ge(*s["act"](2))
            for ct in range(CT):
                nc.vector.tensor_scalar(XN[:, ct, :], XP[:, ct, :], gn_m[:, ct % 2:ct % 2 + 1], gn_r[:, ct % 2:ct % 2 + 1],
                                        ALU.subtract, ALU.mult).then_inc(s["dve"].sem, 1)

        SETUP_DVE, SETUP_ACT, SETUP_PE, CONSTS = 4, 9, 10, 10
        W_ALL = 16 * 20

        with nc.Block() as block:
            @block.sync
            def _(sp):
                for dst, src in [
                    (S_INW, t["in_x"]), (S_C1, t["c1"]), (S_U, t["up"]), (S_FC1, t["fc1"]), (vecs[:], t["vecs"]), (ident[:], t["ident"]),
                    (gmat[:], t["gmat"]), (S_SEL[0:96], t["sel"]), (S_NEG, t["neg"]), (mask8[:], t["mask8"]),
                    (wz[:], t["in_z"]), (wout[:], t["out"]), (wqkv[:], t["qkv"]), (S_PROJ, t["proj"]),
                    (xw[1][:], t["xw1"]), (xw[2][:], t["xw2"]), (xw[3][:], t["xw3"]),
                    (dtw[1][DT_ROW:DT_ROW + R_DT, :], t["dtw1"]), (dtw[2][DT_ROW:DT_ROW + R_DT, :], t["dtw2"]),
                    (dtw[3][DT_ROW:DT_ROW + R_DT, :], t["dtw3"]),
                ]:
                    sp.dma_start(dst, src).then_inc(weights_in, 16)
                load_ahead(sp, gn_first, t["x"][0])
                sp.wait_ge(setup_dve, SETUP_DVE)
                sp.wait_ge(setup_act, SETUP_ACT)
                sp.wait_ge(setup_pe, SETUP_PE)
            @block.tensor
            def _(pe):
                pe.wait_ge(weights_in, W_ALL)
                for ct in range(CT):
                    for m in range(DT):
                        mm = pe.matmul(ps[:, ct, 0:D], S_INW[:, m, P * ct:P * ct + P], S_C1[:, m, :], start=m == 0, stop=m == DT - 1)
                mm.then_inc(setup_pe, 1)
                for o in range(DT):
                    for m in range(DT):
                        pe.matmul(ps[:, 4, o:o + 1], S_C1[:, m, P * o:P * o + P], vec("in_bx", m), start=m == 0, stop=m == DT - 1)
                for o in range(CT):
                    for m in range(CT):
                        mm = pe.matmul(ps[:, 4, 2 + o:3 + o], S_PROJ[:, m, P * o:P * o + P], vec("v_b", m), start=m == 0, stop=m == CT - 1)
                mm.then_inc(setup_pe, 1)
                pe.wait_ge(setup_dve, 1 + 1)
                for j in range(DT):
                    for h in range(4):
                        if j == 1 and h == 0:
                            pe.wait_ge(setup_act, 4)
                        for ct in range(CT):
                            mm = pe.matmul(ps[:, h, :], S_U[:, ct, P * j:P * j + P], S_FC1[:, ct, BANK * h:BANK * h + BANK],
                                           start=ct == 0, stop=ct == CT - 1)
                        mm.then_inc(setup_pe, 1)
                pe.wait_ge(consts_set, CONSTS)
                for k in range(2):
                    group_means(pe, gn_first, k, 5)

            @block.scalar
            def _(act):
                act.wait_ge(weights_in, W_ALL)
                act.wait_ge(consts_set, CONSTS)
                for h in range(4):
                    act.wait_ge(setup_pe, 3 + h)
                    nc.scalar.activation(w1[:, 0, BANK * h:BANK * h + BANK], ps[:, h, :], ACT.Copy).then_inc(setup_act, 1)
                for h in range(4):
                    act.wait_ge(setup_pe, 7 + h)
                    nc.scalar.activation(w1[:, 1, BANK * h:BANK * h + BANK], ps[:, h, :], ACT.Copy).then_inc(setup_act, 1)
                a, n = VEC["Al1"][0], 96
                nc.scalar.activation(vecs[:, a:a + n], vecs[:, a:a + n], ACT.Exp, bias=zero_b[:]).then_inc(setup_act, 1)
                group_std(act, gn_first, 5)

            @block.vector
            def _(dve):
                nc.vector.memset(ones[:], 1.0).then_inc(consts_set, 1)
                nc.vector.memset(ones_c[:], 1.0 / C).then_inc(consts_set, 1)
                nc.vector.memset(ones_d[:], 1.0 / D).then_inc(consts_set, 1)
                nc.vector.memset(zero_b[:], 0.0).then_inc(consts_set, 1)
                nc.vector.memset(eps_b[:], LN_EPS).then_inc(consts_set, 1)
                nc.vector.memset(one_b[:], 1.0).then_inc(consts_set, 1)
                nc.vector.memset(root_b[:], -ROOT_A / 2).then_inc(consts_set, 1)
                dve.wait_ge(weights_in, W_ALL)
                nc.vector.tensor_copy(sel[:], S_SEL[0:96]).then_inc(consts_set, 1)
                nc.vector.tensor_copy(neg[:], S_NEG).then_inc(consts_set, 1)
                nc.vector.memset(maxima[:], 0.0).then_inc(consts_set, 1)
                dve.wait_ge(setup_pe, 1)
                nc.vector.tensor_copy(wf[:], ps[:, 0:4, 0:D]).then_inc(setup_dve, 1)
                dve.wait_ge(setup_pe, 2)
                a = VEC["c1_b"][0]
                nc.vector.tensor_tensor(f1_b[:], ps[:, 4, 0:2], vecs[:, a:a + 2], ALU.add).then_inc(setup_dve, 1)
                a = VEC["proj_b"][0]
                nc.vector.tensor_tensor(o_b[:], ps[:, 4, 2:6], vecs[:, a:a + 4], ALU.add).then_inc(setup_dve, 1)
                dve.wait_ge(setup_act, SETUP_ACT)
                a = VEC["Al1"][0]
                nc.vector.tensor_scalar(vecs[:, a:a + 96], vecs[:, a:a + 96], -1.0, None, ALU.mult).then_inc(setup_dve, 1)
                dve.wait_ge(setup_dve, SETUP_DVE)
                dve.wait_ge(setup_pe, SETUP_PE)
                group_norm(dve, gn_first, 5)
                dve.wait_ge(*gn_first["dve"](20))


        with nc.Fori(0, B) as b:
            with nc.Block() as block:
                @block.sync
                def _(sp):
                    sp.dma_start(C2, t["c2"]).then_inc(c23_in.sem, 16)
                    sp.dma_start(C3, t["c3"]).then_inc(c23_in.sem, 16)
                    for two in range(2):
                        sp.dma_start(T[:, 2 * two:2 * two + 2, :], t["x"][b].rearrange("(j p two) l -> two p j l", p=P, two=2)[two]).then_inc(x_in.sem, 16)
                    sp.wait_ge(*gated(4))
                    sp.dma_start(WPROJ, t["proj"]).then_inc(proj_in.sem, 16)
                    sp.wait_ge(*proj_pe(8))
                    load_ahead(sp, gn_next, t["x"][b + 1])
                    sp.dma_start(W2, t["fc2"]).then_inc(w2_in.sem, 16)
                    for ct, done in ((0, 7), (2, 8), (1, 11), (3, 12)):
                        sp.wait_ge(*fin_dve(done))
                        sp.dma_start(t["y"][b].rearrange("(j p two) l -> two j p l", p=P, two=2)[ct // 2, ct % 2], T[:, ct, :]).then_inc(stored.sem, 16)
                    sp.wait_ge(*stored(16 * CT))

                @block.tensor
                def _(pe):
                    for k, w in enumerate((wz, wf)):
                        for o in range(DT):
                            for j, cs in halves(L1):
                                n = k * 4 + o * 2 + j
                                for ct in range(CT):
                                    mm = pe.matmul(ps[:, n, :], w[:, ct, P * o:P * o + P], XN[:, ct, cs], start=ct == 0, stop=ct == CT - 1)
                                mm.then_inc(conv_pe.sem, 1)
                    def conv_2x2(k, o):
                        w, src, side, bank = ((C2, F1, 32, 5), (C3, F2, 16, 0))[k]
                        n = side * side // 4
                        for ci in range(DT):
                            v = src[:, ci, :].rearrange("p (h a w c) -> p h a w c", h=side // 2, a=2, c=2)
                            for q in range(4):
                                mm = pe.matmul(ps[:, bank + o, 0:n], w[:, ci, q, P * o:P * o + P], v[:, :, q // 2, :, q % 2],
                                               start=ci == 0 and q == 0, stop=ci == DT - 1 and q == 3)
                        mm.then_inc(conv_pe.sem, 1)

                    def project(g):
                        k = g.index
                        if k == 0:
                            pe.wait_ge(*conv_act(10))
                        else:
                            pe.wait_ge(*prep_act(8) if k == 1 else ln_act(4 * (k - 2) + 2))
                        for m in range(DT):
                            mm = pe.matmul(ps[0:XD, AUX_BANK, 0:g.n], xw[g.params][:, m, :], F[g.level][:, m, g.cols], start=m == 0, stop=m == DT - 1)
                        mm.then_inc(prep_pe.sem, 1)

                    def spread_dt(g, half):
                        k = g.index
                        if half == 0:
                            pe.wait_ge(*prep_act(PREP_ACT * k + 2))
                            pe.wait_ge(*prep_dve(PREP_DVE * k + 1))
                        else:
                            pe.wait_ge(*prep_act(PREP_ACT * k + 6))
                        pe.matmul(ps[:, AUX_BANK, 0:g.n], dtw[g.params][DT_ROW:DT_ROW + R_DT, P * half:P * half + P],
                                  DTS[DT_ROW:DT_ROW + R_DT, 0:g.n], start=True, stop=True).then_inc(prep_pe.sem, 1)

                    def mean(g):
                        k = g.index
                        pe.wait_ge(*ln_dve(LN_DVE_AT[k] + 2))
                        pe.wait_ge(*prep_act(PREP_ACT * (k + 1) + 8) if k + 1 < NG else ln_act(4 * (k - 1) + 2))
                        for h in range(DT):
                            mm = pe.matmul(ps[:, AUX_BANK, 0:g.width], ones_d[:], LY[:, h, 0:g.width], start=h == 0, stop=h == DT - 1)
                        mm.then_inc(ln_pe.sem, 1)

                    def variance(g):
                        pe.wait_ge(*ln_act(4 * g.index + 1))
                        pe.wait_ge(*ln_dve(LN_DVE_AT[g.index] + 3))
                        for h in range(DT):
                            mm = pe.matmul(ps[:, AUX_BANK, 0:g.width], ones_d[:], LSQS[:, h, 0:g.width], start=h == 0, stop=h == DT - 1)
                        mm.then_inc(ln_pe.sem, 1)

                    def b_row(u):
                        g, n = GROUPS[u // N_STATE], u % N_STATE
                        if n == 0:
                            pe.wait_ge(*prep_dve(PREP_DVE * g.index + 2))
                            pe.wait_ge(*prep_act(PREP_ACT * g.index + 4))
                        if u >= 2:
                            pe.wait_ge(*driven(2 * (u - 2) + 2))
                        pe.matmul(ps[:, B_BANK[u % 2], 0:g.n], sel[:, n, :], SPL[0:96, g.slot, 0:g.n], start=True, stop=True).then_inc(b_rows.sem, 1)

                    def c_row(u):
                        g, n = GROUPS[u // N_STATE], u % N_STATE
                        if u >= 1:
                            pe.wait_ge(*c_kept(u))
                        pe.matmul(ps[:, C_BANK, 0:g.n], sel[:, N_STATE + n, :], SPL[0:96, g.slot, 0:g.n], start=True, stop=True).then_inc(c_rows.sem, 1)

                    def sum_states(u):
                        g, n = GROUPS[u // N_STATE], u % N_STATE
                        for half in range(DT):
                            s = 2 * u + half
                            if n == 0 and g.index:
                                pe.wait_ge(*ln_dve(LN_DVE_AT[g.index - 1] + 1 + half))
                            pe.wait_ge(*weighed(s + 1))
                            pe.matmul(ps[:, Y_BANK[half], 0:g.width], ident[:], HC[:, s % 3, 0:g.width], start=n == 0, stop=n == N_STATE - 1)\
                                .then_inc(summed.sem, 1)

                    project(GROUPS[0])
                    pe.wait_ge(*c23_in(32))
                    conv_2x2(0, 0)
                    spread_dt(GROUPS[0], 0)
                    spread_dt(GROUPS[0], 1)
                    conv_2x2(0, 1)
                    pe.wait_ge(*conv_act(12))
                    conv_2x2(1, 0)
                    conv_2x2(1, 1)
                    pe.wait_ge(*conv_act(14))
                    b_row(0)
                    b_row(1)
                    c_row(0)
                    for u in range(N_UNITS):
                        g, n = GROUPS[u // N_STATE], u % N_STATE
                        if u + 2 < N_UNITS:
                            b_row(u + 2)
                        if u + 1 < N_UNITS:
                            c_row(u + 1)
                        if u >= 1:
                            sum_states(u - 1)
                        if g.index and n == 1:
                            mean(GROUPS[g.index - 1])
                        if g.index and n == 4:
                            variance(GROUPS[g.index - 1])
                        if g.index + 1 < NG:
                            if n == 5:
                                project(GROUPS[g.index + 1])
                            if n == 7:
                                spread_dt(GROUPS[g.index + 1], 0)
                            if n == 9:
                                spread_dt(GROUPS[g.index + 1], 1)
                    sum_states(N_UNITS - 1)

                    def out_conv(i, cs):
                        pe.wait_ge(*gated(2 * i + 2))
                        for ct in range(CT):
                            for m in range(DT):
                                mm = pe.matmul(ps[:, 4 * i + ct, :], wout[:, m, P * ct:P * ct + P], Y1[:, m, cs], start=m == 0, stop=m == DT - 1)
                            mm.then_inc(out_pe.sem, 1)

                    def token_means(which, i, cs):
                        pe.wait_ge(*(out_dve, proj_dve)[which](4 * i + 4))
                        for ct in range(CT):
                            mm = pe.matmul(ps[:, 4 * i, :], ones_c[:], T[:, ct, cs], start=ct == 0, stop=ct == CT - 1)
                        mm.then_inc(tn_pe.sem, 1)

                    def token_variances(which, i):
                        k = which * 2 + i
                        for ct in range(CT):
                            pe.wait_ge(*tn_act(6 * k + ct + 1))
                            mm = pe.matmul(ps[:, 4 * i + 1, :], ones_c[:], LSQ[:, CT * i + ct, :], start=ct == 0, stop=ct == CT - 1)
                        mm.then_inc(tn_sq.sem, 1)

                    def values(n):
                        kt, bank = V_TILES[n]
                        pe.wait_ge(*tn_dve(8 * (n // 4) + 8))
                        if n >= 4:
                            pe.wait_ge(*v_act(n - 1))
                        for ct in range(CT):
                            mm = pe.matmul(ps[:, bank, :], TN[:, ct, P * kt:P * kt + P], wqkv[:, ct, 2 * C:3 * C], start=ct == 0, stop=ct == CT - 1)
                        mm.then_inc(v_pe.sem, 1)

                    (first, first_cs), (second, second_cs) = CHUNKS
                    mean(GROUPS[NG - 1])
                    out_conv(first, first_cs)
                    variance(GROUPS[NG - 1])
                    token_means(0, first, first_cs)
                    out_conv(second, second_cs)
                    token_variances(0, first)
                    token_means(0, second, second_cs)
                    values(0)
                    token_variances(0, second)
                    for n in range(1, 4):
                        values(n)

                    def ring(job):
                        at = RING_AT[job]
                        if at < 3:
                            pe.wait_ge(*v_act(4))
                            pe.wait_ge(*tn_dve(16))
                        else:
                            kind, h, i = RING[at - 3]
                            pe.wait_ge(*{"project": qk_lo(3 * h + 2), "smax": smax_dve(KT * h + i + 1), "scores": s_exp(KT * h + i + 1)}[kind])
                        return 2 * (at % 3)

                    def project_qk(h, between=None):
                        bank = ring(("project", h, 0))
                        for j, cs in halves(L1):
                            for ct in range(CT):
                                mm = pe.matmul(ps[:, bank + j, :], wqkv[:, ct, P * h:P * h + P], TN[:, ct, cs], start=ct == 0, stop=ct == CT - 1)
                            if j == 0 and between is not None:
                                sum_exps(between)
                        mm.then_inc(qk_pe.sem, 1)

                    def smax(h, qt):
                        bank = ring(("smax", h, qt))
                        if qt == 0:
                            pe.wait_ge(*qk_hi(3 * h + 3))
                            pe.wait_ge(*qk_lo(3 * h + 3))
                        q, k = qk_parts[:, h % 2, 0, :], qk_parts[:, h % 2, 1, :]
                        for j, cs in halves(L1):
                            mm = pe.matmul(ps[:, bank + j, :], q[:, P * qt:P * qt + P], k[:, cs], start=True, stop=True)
                        mm.then_inc(smax_pe.sem, 1)

                    def turn_maxima(h):
                        pe.wait_ge(*mt_dve(4 * h + 1))
                        pe.wait_ge(*(o_dve(3 * (h - 2) + 1) if h >= 2 else v_act(KT)))
                        pe.transpose(ps[:, 7, 0:P], maxima[:].rearrange("p e m -> p (e m)"), ident[:]).then_inc(mt_pe.sem, 1)

                    def scores(h, kt):
                        bank = ring(("scores", h, kt))
                        if kt == 0:
                            pe.wait_ge(*mt_dve(4 * h + 4))
                        e = h % 2
                        q = qk_parts[:, e, 0, :]
                        for part in range(2):
                            k = qk_parts[:, e, 1 + part, P * kt:P * kt + P]
                            for j, cs in halves(L1):
                                pe.matmul(ps[:, bank + j, :], k, q[:, cs], start=part == 0, stop=False)
                        for j, cs in halves(L1):
                            mm = pe.matmul(ps[:, bank + j, :], neg[64 * e:64 * e + 64, :], RH[64 * e:64 * e + 64, 4 * j:4 * j + 4, :], start=False, stop=True)
                        mm.then_inc(s_pe.sem, 1)

                    def times_values(h, kt):
                        i = KT * h + kt
                        pe.wait_ge(*s_exp(i + 1))
                        if kt == 0:
                            pe.wait_ge(*(o_dve(3 * h) if h else v_act(KT)))
                        for j, cs in halves(L1):
                            mm = pe.matmul(ps[64 * j:64 * j + 64, 6, :], V[:, kt, HD * h:HD * h + HD], PR[:, i % 4, cs], start=kt == 0, stop=kt == KT - 1)
                        mm.then_inc(pv_pe.sem, 1)

                    def sum_exps(h):
                        pe.wait_ge(*den_pool(7 * h + 7))
                        if h + 1 < HEADS:
                            pe.wait_ge(*mt_dve(4 * (h + 1) + 3))
                        for j, cs in halves(L1):
                            mm = pe.matmul(ps[64 * j:64 * j + 64, 7, :], ones[:, 0:64], DEN[:, h % 2, cs], start=True, stop=True)
                        mm.then_inc(den_pe.sem, 1)

                    project_qk(0)
                    project_qk(1)
                    for qt in range(KT):
                        smax(0, qt)
                        if qt % 2:
                            values(4 + qt // 2)
                    turn_maxima(0)
                    for h in range(HEADS):
                        for kt in range(KT):
                            scores(h, kt)
                            if h + 1 < HEADS:
                                for qt in SMAX_AFTER.get(kt, ()):
                                    smax(h + 1, qt)
                            for pt in PV_AFTER.get(kt, ()):
                                times_values(h, pt)
                        if h + 1 < HEADS:
                            turn_maxima(h + 1)
                        if h + 2 < HEADS:
                            project_qk(h + 2, between=h)
                        for pt in PV_LAST:
                            times_values(h, pt)
                        if h == HEADS - 2:
                            sum_exps(h)

                    def project_out(i, cs, ct, ms=range(CT)):
                        for m in ms:
                            mm = pe.matmul(ps[:, 4 * i + ct, :], WPROJ[:, m, P * ct:P * ct + P], O[:, m, cs], start=m == 0, stop=m == CT - 1)
                        if m == CT - 1:
                            mm.then_inc(proj_pe.sem, 1)

                    pe.wait_ge(*proj_in(16))
                    pe.wait_ge(*s_exp(KT * HEADS))
                    pe.wait_ge(*o_dve(3 * (HEADS - 2)))
                    for ct in range(CT):
                        project_out(first, first_cs, ct, range(CT - 1))
                        if ct == 0:
                            sum_exps(HEADS - 1)
                    pe.wait_ge(*o_dve(3 * HEADS))
                    for ct in range(CT):
                        project_out(first, first_cs, ct, (CT - 1,))
                    project_out(second, second_cs, 0)
                    token_means(1, first, first_cs)
                    for ct in range(1, CT):
                        project_out(second, second_cs, ct)
                    token_variances(1, first)
                    token_means(1, second, second_cs)
                    token_variances(1, second)

                    for i in range(2):
                        pe.wait_ge(*ll_dve(4 * i + 4))
                        cs = CHUNKS[i][1]
                        lc = slice(cs.start // 2, cs.stop // 2)
                        for ht in range(4):
                            for j in range(DT):
                                mm = pe.matmul(ps[:, ht, lc], w1[:, j, P * ht:P * ht + P], LL[:, j, lc], start=j == 0, stop=j == DT - 1)
                            if i == 1:
                                mm.then_inc(fc1_pe.sem, 1)
                    for ht in range(4, HT):
                        if ht >= 6:
                            pe.wait_ge(*fc1_act(ht - 5))
                        for j in range(DT):
                            mm = pe.matmul(ps[:, ht % 6, :], w1[:, j, P * ht:P * ht + P], LL[:, j, :], start=j == 0, stop=j == DT - 1)
                        mm.then_inc(fc1_pe.sem, 1)
                    pe.wait_ge(*w2_in(16))
                    for o in range(DT):
                        for ht in range(HT):
                            if o == 0:
                                pe.wait_ge(*fc1_act(ht + 1))
                            elif ht in (0, 4):
                                group_means(pe, gn_next, ht // 4, 0)
                            mm = pe.matmul(ps[:, 6 + o, :], W2[:, ht, P * o:P * o + P], HM[:, ht, :], start=ht == 0, stop=ht == HT - 1)
                        mm.then_inc(fc2_pe.sem, 1)

                @block.scalar
                def _(act):
                    for k, (dst, bias) in enumerate([(Z, "in_bz"), (F1, None)]):
                        for o in range(DT):
                            for j, cs in halves(L1):
                                n = k * 4 + o * 2 + j
                                act.wait_ge(*conv_pe(n + 1))
                                bb = vec(bias, o) if bias else f1_b[:, o:o + 1]
                                nc.scalar.activation(dst[:, o, cs], ps[:, n, :], ACT.Identity, bias=bb).then_inc(conv_act.sem, 1)
                        if k == 0:
                            act.wait_ge(*conv_act(4))
                            for o in range(DT):
                                nc.scalar.activation(ZE[:, o, :], Z[:, o, :], ACT.Exp, bias=zero_b[:], scale=-1.0).then_inc(conv_act.sem, 1)

                    def keep_conv(k, o):
                        dst, n, name, bank = ((F2, L2, "c2_b", 5), (F3, L3, "c3_b", 0))[k]
                        act.wait_ge(*conv_pe(8 + 2 * k + o + 1))
                        nc.scalar.activation(dst[:, o, :], ps[:, bank + o, 0:n], ACT.Identity, bias=vec(name, o)).then_inc(conv_act.sem, 1)

                    def split(g, part):
                        k = g.index
                        if part == 0:
                            act.wait_ge(*prep_pe(3 * k + 1))
                            if k >= 2:
                                act.wait_ge(*c_rows(N_STATE * (k - 1)))
                                act.wait_ge(*prep_dve(PREP_DVE * k))
                            elif k == 1:
                                act.wait_ge(*prep_dve(PREP_DVE * k))
                            nc.scalar.activation(SPL[0:96, g.slot, 0:g.n], ps[0:96, AUX_BANK, 0:g.n], ACT.Copy).then_inc(prep_act.sem, 1)
                            nc.scalar.activation(DTS[DT_ROW:DT_ROW + R_DT, 0:g.n], ps[DT_ROW:DT_ROW + R_DT, AUX_BANK, 0:g.n], ACT.Copy)\
                                .then_inc(prep_act.sem, 1)
                        else:
                            act.wait_ge(*prep_dve(PREP_DVE * k + 1))
                            nc.scalar.activation(SPL[32:64, g.slot, 0:g.n], SPLR[32:64, 0:g.n], ACT.Copy).then_inc(prep_act.sem, 1)
                            nc.scalar.activation(SPLT[64:96, 0:g.n], SPLR[64:96, 0:g.n], ACT.Copy).then_inc(prep_act.sem, 1)

                    def softplus(g, half):
                        k = g.index
                        act.wait_ge(*prep_pe(3 * k + 2 + half))
                        if half == 0 and k >= 2:
                            act.wait_ge(*scanned(2 * N_STATE * (k - 1)))
                        nc.scalar.activation(SPA[:, half, 0:g.n], ps[:, AUX_BANK, 0:g.n], ACT.Abs, bias=vec(f"dtb{g.params}", half)).then_inc(prep_act.sem, 1)
                        nc.scalar.activation(DELTA[:, g.slot, half, 0:g.n], ps[:, AUX_BANK, 0:g.n], ACT.Relu, bias=vec(f"dtb{g.params}", half))\
                            .then_inc(prep_act.sem, 1)

                    def exp_and_square(g):
                        k, e = PREP_ACT * g.index, SPA[:, :, 0:g.n]
                        act.wait_ge(*prep_act(k + 7))
                        nc.scalar.activation(e, e, ACT.Exp, bias=zero_b[:], scale=-1.0).then_inc(prep_act.sem, 1)
                        act.wait_ge(*prep_act(k + 9))
                        if g.index >= 2:
                            act.wait_ge(*driven(2 * N_STATE * (g.index - 1)))
                        nc.scalar.activation(DU[:, g.slot, :, 0:g.n], e, ACT.Square, bias=root_b[:], scale=0.5).then_inc(prep_act.sem, 1)

                    def logarithms(g, norm):
                        if g:
                            act.wait_ge(*prep_act(PREP_ACT * g.index + 9))
                            nc.scalar.activation(SPE[:, :, 0:g.n], SPA[:, :, 0:g.n], ACT.Ln, bias=one_b[:]).then_inc(prep_act.sem, 1)
                        if norm:
                            k = 4 * norm.index
                            act.wait_ge(*ln_act(k + 2))
                            nc.scalar.activation(LR[:, 0:norm.width], LR[:, 0:norm.width], ACT.Ln, bias=eps_b[:]).then_inc(ln_act.sem, 1)
                            act.wait_ge(*ln_act(k + 3))
                            nc.scalar.activation(LR[:, 0:norm.width], LR[:, 0:norm.width], ACT.Exp, bias=zero_b[:], scale=-0.5).then_inc(ln_act.sem, 1)

                    def squares(g):
                        act.wait_ge(*ln_dve(LN_DVE_AT[g.index] + 3))
                        nc.scalar.activation(LSQS[:, :, 0:g.width], LY[:, :, 0:g.width], ACT.Square, bias=zero_b[:]).then_inc(ln_act.sem, 1)

                    def keep_variance(g):
                        act.wait_ge(*ln_pe(2 * g.index + 2))
                        if g.index:
                            act.wait_ge(*ln_dve(LN_DVE_AT[g.index]))
                        nc.scalar.activation(LR[:, 0:g.width], ps[:, AUX_BANK, 0:g.width], ACT.Copy).then_inc(ln_act.sem, 1)

                    def upsample(g):
                        act.wait_ge(*ln_dve(LN_DVE_AT[g.index + 1]))
                        for h in range(DT):
                            src = Y3[:, h, :].rearrange("p (h w) -> p h w", h=8).unsqueeze(3).broadcast_to((P, 8, 8, 2))
                            dst = Y2[:, h, :].rearrange("p (h a w c) -> p h a w c", h=8, a=2, c=2)
                            for a in range(2):
                                nc.scalar.activation(dst[:, :, a, :, :], src, ACT.Copy).then_inc(y_start.sem, 1)

                    split(GROUPS[0], 0)
                    split(GROUPS[0], 1)
                    softplus(GROUPS[0], 0)
                    softplus(GROUPS[0], 1)
                    keep_conv(0, 0)
                    exp_and_square(GROUPS[0])
                    logarithms(GROUPS[0], None)
                    keep_conv(0, 1)
                    keep_conv(1, 0)
                    keep_conv(1, 1)

                    def keep_state(u, half):
                        g, n = GROUPS[u // N_STATE], u % N_STATE
                        if g.index in KEEPS:
                            last = 0 if g.dirs[0] else g.n - 1
                            nc.scalar.activation(STATE[:, half, n:n + 1], H[:, (2 * u + half) % 4, last:last + 1], ACT.Copy).then_inc(state_kept.sem, 1)

                    for u in range(N_UNITS):
                        g, n = GROUPS[u // N_STATE], u % N_STATE
                        act.wait_ge(*c_rows(u + 1))
                        if u >= 2:
                            act.wait_ge(*weighed(2 * (u - 2) + 2))
                        nc.scalar.activation(CB[:, u % 2, 0:g.n], ps[:, C_BANK, 0:g.n], ACT.Copy).then_inc(c_kept.sem, 1)
                        if n == 0:
                            act.wait_ge(*prep_dve(PREP_DVE * g.index + 7))
                        for half in range(DT):
                            if u:
                                act.wait_ge(*scanned(2 * (u - 1) + half + 1))
                                keep_state(u - 1, half)
                            a = VEC[f"Al{g.params}"][0] + N_STATE * half + n
                            nc.scalar.activation(ps[:, DECAY_BANK[half], 0:g.n], DELTA[:, g.slot, half, 0:g.n], ACT.Exp, bias=zero_b[:],
                                                 scale=vecs[:, a:a + 1]).then_inc(decay.sem, 1)
                        if g.index and n == 3:
                            squares(GROUPS[g.index - 1])
                        if g.index == 4 and n == 1:
                            upsample(GROUPS[2])
                        if g.index and n == 5:
                            keep_variance(GROUPS[g.index - 1])
                        if g.index + 1 < NG:
                            if n in (7, 8):
                                split(GROUPS[g.index + 1], n - 7)
                            if n in (9, 11):
                                softplus(GROUPS[g.index + 1], (n - 9) // 2)
                            if n == 12:
                                exp_and_square(GROUPS[g.index + 1])
                        if n == 13:
                            logarithms(GROUPS[g.index + 1] if g.index + 1 < NG else None, GROUPS[g.index - 1] if g.index else None)
                    squares(GROUPS[NG - 1])
                    keep_variance(GROUPS[NG - 1])
                    logarithms(None, GROUPS[NG - 1])

                    def token_norm(which):
                        for i, cs in CHUNKS:
                            k = which * 2 + i
                            for ct in range(CT):
                                act.wait_ge(*tn_dve(8 * k + ct + 1))
                                nc.scalar.activation(LSQ[:, CT * i + ct, :], TN[:, ct, cs], ACT.Square, bias=zero_b[:]).then_inc(tn_act.sem, 1)
                            act.wait_ge(*tn_sq(k + 1))
                            if i == 1:
                                act.wait_ge(*tn_dve(8 * k))
                            nc.scalar.activation(LRS, ps[:, 4 * i + 1, :], ACT.Ln, bias=eps_b[:]).then_inc(tn_act.sem, 1)
                            act.wait_ge(*tn_act(6 * k + 5))
                            nc.scalar.activation(LRS, LRS, ACT.Exp, bias=zero_b[:], scale=-0.5).then_inc(tn_act.sem, 1)

                    token_norm(0)

                    def keep_values(n):
                        kt, bank = V_TILES[n]
                        act.wait_ge(*v_pe(n + 1))
                        nc.scalar.activation(V[:, kt, :], ps[:, bank, :], ACT.Copy).then_inc(v_act.sem, 1)

                    for n in range(4):
                        keep_values(n)
                    def double_bank(job, rows):
                        bank = 2 * (RING_AT[job] % 3)
                        return ps[rows, bank:bank + 2, :].rearrange("p a b -> p (a b)")

                    def qk_high(h):
                        act.wait_ge(*qk_pe(h + 1))
                        if h >= 2:
                            act.wait_ge(*s_pe(KT * (h - 2) + KT))
                        for which, rows_of in ((0, LOWER), (2, UPPER)):
                            nc.scalar.activation(qk_parts[rows_of, h % 2, which, :], double_bank(("project", h, 0), rows_of), ACT.Identity, bias=vec("qk_b", h, rows_of))\
                                .then_inc(qk_hi.sem, 1)
                        act.wait_ge(*qk_hi(3 * h + 2))
                        nc.scalar.activation(qk_parts[LOWER, h % 2, 1, :], qk_parts[UPPER, h % 2, 2, :], ACT.Copy).then_inc(qk_hi.sem, 1)

                    qk_high(0)
                    qk_high(1)
                    for n in range(4, KT):
                        keep_values(n)
                    for h in range(HEADS):
                        for kt in range(KT):
                            i = KT * h + kt
                            act.wait_ge(*s_pe(i + 1))
                            if i >= 4:
                                lh, lk = (i - 4) // KT, (i - 4) % KT
                                act.wait_ge(*pv_pe(i - 4 + 1))
                                act.wait_ge(*den_pool(7 * lh + max(lk, 1)))
                            nc.scalar.activation(PR[:, i % 4, :], double_bank(("scores", h, kt), slice(0, P)), ACT.Exp, bias=zero_b[:], scale=SCALE)\
                                .then_inc(s_exp.sem, 1)
                        if h + 2 < HEADS:
                            qk_high(h + 2)
                    token_norm(1)
                    for ht in range(HT):
                        act.wait_ge(*fc1_pe(ht + 1))
                        nc.scalar.activation(HM[:, ht, :], ps[:, ht % 6, :], ACT.Gelu, bias=vec("fc1_b", ht), scale=0.5).then_inc(fc1_act.sem, 1)
                    group_std(act, gn_next, 0)

                @block.vector
                def _(dve):
                    nc.vector.memset(Y3, 0.0).then_inc(y_start.sem, 1)
                    for o in range(DT):
                        dve.wait_ge(*conv_act(5 + o))
                        nc.vector.tensor_scalar(ZE[:, o, :], ZE[:, o, :], 1.0, None, ALU.add).then_inc(conv_dve.sem, 1)
                    for o in range(DT):
                        dve.wait_ge(*conv_dve(1 + o))
                        nc.vector.reciprocal(ZE[:, o, :], ZE[:, o, :]).then_inc(conv_dve.sem, 1)
                    for o in range(DT):
                        dve.wait_ge(*conv_dve(3 + o))
                        nc.vector.tensor_tensor(Z[:, o, :], Z[:, o, :], ZE[:, o, :], ALU.mult).then_inc(conv_dve.sem, 1)

                    def both(v, g):
                        return v.unsqueeze(1).broadcast_to((P, DT, v.shape[-1]))

                    def split(g, part):
                        k, ka = PREP_DVE * g.index, PREP_ACT * g.index
                        if part == 0:
                            dve.wait_ge(*prep_act(ka + 2))
                            nc.vector.tensor_tensor(SPLR[0:96, 0:g.n], ps[0:96, AUX_BANK, 0:g.n], SPL[0:96, g.slot, 0:g.n], ALU.subtract).then_inc(prep_dve.sem, 1)
                        else:
                            dve.wait_ge(*prep_act(ka + 4))
                            nc.vector.tensor_tensor(SPL[64:96, g.slot, 0:g.n], SPLR[64:96, 0:g.n], SPLT[64:96, 0:g.n], ALU.subtract).then_inc(prep_dve.sem, 1)

                    def softplus(g, part):
                        k, ka = PREP_DVE * g.index, PREP_ACT * g.index
                        p, e, ln = SPP[:, :, 0:g.n], SPA[:, :, 0:g.n], SPE[:, :, 0:g.n]
                        delta, du = DELTA[:, g.slot, :, 0:g.n], DU[:, g.slot, :, 0:g.n]
                        if part == 0:
                            dve.wait_ge(*prep_act(ka + 9))
                            dve.wait_ge(*prep_dve(k + 2))
                            nc.vector.scalar_tensor_tensor(out=p, in0=e, scalar=ROOT_R, in1=e, op0=ALU.subtract, op1=ALU.mult).then_inc(prep_dve.sem, 1)
                            dve.wait_ge(*prep_act(ka + 10))
                            dve.wait_ge(*prep_dve(k + 3))
                            nc.vector.scalar_tensor_tensor(out=p, in0=du, scalar=ROOT_B ** 2 / 4, in1=p, op0=ALU.add, op1=ALU.mult).then_inc(prep_dve.sem, 1)
                        elif part == 1:
                            dve.wait_ge(*prep_act(ka + 11))
                            nc.vector.scalar_tensor_tensor(out=ln, in0=e, scalar=E_SMALL, in1=ln, op0=ALU.is_ge, op1=ALU.mult).then_inc(prep_dve.sem, 1)
                            dve.wait_ge(*prep_dve(k + 5))
                            nc.vector.scalar_tensor_tensor(out=p, in0=p, scalar=-1.0, in1=ln, op0=ALU.mult, op1=ALU.max).then_inc(prep_dve.sem, 1)
                        elif part == 2:
                            dve.wait_ge(*prep_dve(k + 6))
                            nc.vector.tensor_tensor(delta, delta, p, ALU.add).then_inc(prep_dve.sem, 1)
                        else:
                            dve.wait_ge(*prep_dve(k + 7))
                            nc.vector.tensor_tensor(du, delta, F[g.level][:, :, g.cols], ALU.mult).then_inc(prep_dve.sem, 1)

                    def drive(u, half):
                        g, s = GROUPS[u // N_STATE], 2 * u + half
                        dve.wait_ge(*b_rows(u + 1))
                        if u % N_STATE == 0:
                            dve.wait_ge(*prep_dve(PREP_DVE * g.index + 8))
                        if u == 0:
                            dve.wait_ge(*conv_dve(6))
                        if s >= 3:
                            dve.wait_ge(*scanned(s - 2))
                        nc.vector.tensor_tensor(DBX[:, s % 3, 0:g.n], DU[:, g.slot, half, 0:g.n], ps[:, B_BANK[u % 2], 0:g.n], ALU.mult).then_inc(driven.sem, 1)

                    def scan(u, half):
                        g, n, s = GROUPS[u // N_STATE], u % N_STATE, 2 * u + half
                        dve.wait_ge(*driven(s + 1))
                        dve.wait_ge(*decay(s + 1))
                        if s >= 4:
                            dve.wait_ge(*weighed(s - 3))
                        start = 0.0
                        if not g.first:
                            dve.wait_ge(*state_kept(2 * N_STATE * KEEPS[g.index - 1] + 2 * n + half + 1))
                            start = STATE[:, half, n:n + 1]
                        for i, d in enumerate(g.dirs):
                            w = slice(None, None, -1 if d else 1)
                            ins = nc.vector.tensor_tensor_scan(H[:, s % 4, g.n * i:g.n * i + g.n][:, w], ps[:, DECAY_BANK[half], 0:g.n][:, w],
                                                               DBX[:, s % 3, 0:g.n][:, w], start, ALU.mult, ALU.add)
                        ins.then_inc(scanned.sem, 1)

                    def norm_sums(g):
                        k = LN_DVE_AT[g.index]
                        for h in range(DT):
                            dve.wait_ge(*summed(2 * N_STATE * g.index + 2 * N_STATE - 1 + h))
                            if g.index:
                                dve.wait_ge(*ln_dve(k))
                            f = F[g.level][:, h, g.cols].unsqueeze(1).broadcast_to((P, len(g.dirs), g.n))
                            o, y = (v.rearrange("p (d n) -> p d n", n=g.n) for v in (LY[:, h, 0:g.width], ps[:, Y_BANK[h], 0:g.width]))
                            nc.vector.scalar_tensor_tensor(out=o, in0=f, scalar=vec(f"Dv{g.params}", h), in1=y, op0=ALU.mult, op1=ALU.add).then_inc(ln_dve.sem, 1)

                    def norm_center(g):
                        dve.wait_ge(*ln_pe(2 * g.index + 1))
                        y = LY[:, :, 0:g.width]
                        nc.vector.tensor_tensor(y, y, both(ps[:, AUX_BANK, 0:g.width], g), ALU.subtract).then_inc(ln_dve.sem, 1)

                    def norm_scale(g):
                        dve.wait_ge(*ln_act(4 * g.index + 4))
                        for h in range(DT):
                            nc.vector.scalar_tensor_tensor(out=LY[:, h, 0:g.width], in0=LY[:, h, 0:g.width], scalar=vec(f"g{g.params}", h),
                                                           in1=LR[:, 0:g.width], op0=ALU.mult, op1=ALU.mult).then_inc(ln_dve.sem, 1)

                    def norm_add(g):
                        k = LN_DVE_AT[g.index]
                        if g.level > 1:
                            dve.wait_ge(*y_start({3: 1, 2: 5}[g.level]))
                        elif g.dirs[0]:
                            dve.wait_ge(*y_add(4))
                        for i, d in enumerate(g.dirs):
                            for h in range(DT):
                                dve.wait_ge(*ln_dve(k + 4 + h + 2 * i))
                                y, ly = Y[g.level][:, h, g.cols], LY[:, h, g.n * i:g.n * i + g.n]
                                if g.level == 1 and not g.dirs[0]:
                                    nc.vector.tensor_scalar(y, ly, vec(f"be{g.params}", h), None, ALU.add).then_inc(ln_dve.sem, 1)
                                else:
                                    nc.vector.scalar_tensor_tensor(out=y, in0=ly, scalar=vec(f"be{g.params}", h), in1=y,
                                                                   op0=ALU.add, op1=ALU.add).then_inc(ln_dve.sem, 1)

                    def add_upsampled(h, a):
                        dve.wait_ge(*ln_dve(LN_DVE_AT[4]))
                        src = Y2[:, h, :].rearrange("p (h w) -> p h w", h=16).unsqueeze(3).broadcast_to((P, 16, 16, 2))
                        dst = Y1[:, h, :].rearrange("p (h a w c) -> p h a w c", h=16, a=2, c=2)[:, :, a, :, :]
                        nc.vector.tensor_tensor(dst, dst, src, ALU.add).then_inc(y_add.sem, 1)

                    split(GROUPS[0], 0)
                    split(GROUPS[0], 1)
                    for part in range(4):
                        softplus(GROUPS[0], part)
                    drive(0, 0)
                    drive(0, 1)
                    for u in range(N_UNITS):
                        g, n = GROUPS[u // N_STATE], u % N_STATE
                        for half in range(DT):
                            scan(u, half)
                            if u + 1 < N_UNITS:
                                drive(u + 1, half)
                        if g.index and n == 0:
                            norm_sums(GROUPS[g.index - 1])
                        if g.index and n == 2:
                            norm_center(GROUPS[g.index - 1])
                        if g.index + 1 < NG:
                            if n in (7, 8):
                                split(GROUPS[g.index + 1], n - 7)
                            if n in (12, 13, 14):
                                softplus(GROUPS[g.index + 1], n - 12)
                            if n == 14:
                                softplus(GROUPS[g.index + 1], 3)
                        if g.index == 5 and n in (3, 4, 5, 6):
                            add_upsampled((n - 3) // 2, (n - 3) % 2)
                        if g.index and n == 15:
                            norm_scale(GROUPS[g.index - 1])
                        if g.index and n == 15:
                            norm_add(GROUPS[g.index - 1])

                    def gate(i, cs):
                        dve.wait_ge(*ln_dve(LN_DVE_AT[NG - 1 + i]))
                        dve.wait_ge(*conv_dve(6))
                        for h in range(DT):
                            nc.vector.tensor_tensor(Y1[:, h, cs], Y1[:, h, cs], Z[:, h, cs], ALU.mult).then_inc(gated.sem, 1)

                    def add_residual(i, cs, cts, made, bias, done):
                        for ct in cts:
                            dve.wait_ge(*made(4 * i + ct + 1))
                            nc.vector.scalar_tensor_tensor(out=T[:, ct, cs], in0=ps[:, 4 * i + ct, :], scalar=bias(ct), in1=T[:, ct, cs],
                                                           op0=ALU.add, op1=ALU.add).then_inc(done.sem, 1)

                    def token_center(which, i, cs):
                        k = which * 2 + i
                        dve.wait_ge(*(out_dve, proj_dve)[which](4 * i + 4))
                        dve.wait_ge(*tn_pe(k + 1))
                        for ct in range(CT):
                            nc.vector.tensor_tensor(TN[:, ct, cs], T[:, ct, cs], ps[:, 4 * i, :], ALU.subtract).then_inc(tn_dve.sem, 1)

                    def token_scale(which, i, cs):
                        dve.wait_ge(*tn_act(6 * (which * 2 + i) + 6))
                        for ct in range(CT):
                            nc.vector.tensor_tensor(TN[:, ct, cs], TN[:, ct, cs], LRS, ALU.mult).then_inc(tn_dve.sem, 1)

                    (first, first_cs), (second, second_cs) = CHUNKS
                    out_steps = (out_pe, lambda ct: vec("out_b", ct), out_dve)
                    gate(first, first_cs)
                    norm_sums(GROUPS[NG - 1])
                    norm_center(GROUPS[NG - 1])
                    dve.wait_ge(*x_in(32))
                    add_residual(first, first_cs, range(CT), *out_steps)
                    norm_scale(GROUPS[NG - 1])
                    norm_add(GROUPS[NG - 1])
                    gate(second, second_cs)
                    token_center(0, first, first_cs)
                    add_residual(second, second_cs, range(CT), *out_steps)
                    token_scale(0, first, first_cs)
                    token_center(0, second, second_cs)
                    token_scale(0, second, second_cs)

                    def double_bank(job, rows):
                        bank = 2 * (RING_AT[job] % 3)
                        return ps[rows, bank:bank + 2, :].rearrange("p a b -> p (a b)")

                    def qk_low(h):
                        dve.wait_ge(*qk_hi(3 * h + 2))
                        for which, src, of in ((0, LOWER, 0), (1, UPPER, 2)):
                            nc.vector.scalar_tensor_tensor(out=qk_parts[UPPER, h % 2, which, :], in0=double_bank(("project", h, 0), src),
                                                           scalar=vec("qk_b", h, src), in1=qk_parts[src, h % 2, of, :],
                                                           op0=ALU.add, op1=ALU.subtract).then_inc(qk_lo.sem, 1)

                    def k_low_again(h):
                        dve.wait_ge(*qk_lo(3 * h + 2))
                        nc.vector.tensor_copy(qk_parts[LOWER, h % 2, 2, :], qk_parts[UPPER, h % 2, 1, :]).then_inc(qk_lo.sem, 1)

                    def find_maxima(h):
                        e = h % 2
                        for qt in range(KT):
                            dve.wait_ge(*smax_pe(KT * h + qt + 1))
                            nc.vector.tensor_reduce(maxima[:, e, qt:qt + 1], double_bank(("smax", h, qt), slice(0, P)), AX_X, ALU.max)\
                                .then_inc(smax_dve.sem, 1)
                        dve.wait_ge(*smax_dve(KT * h + KT))
                        nc.vector.tensor_copy(maxima[:, e, 32:40], maxima[:, e, 0:8]).then_inc(mt_dve.sem, 1)

                    def rows_of_maxima(h):
                        half = slice(64 * (h % 2), 64 * (h % 2) + 64)
                        low = slice(half.start + 32, half.stop)
                        dve.wait_ge(*mt_pe(h + 1))
                        nc.vector.tensor_copy(rows[half, :], ps[half, 7, 0:P]).then_inc(mt_dve.sem, 1)
                        dve.wait_ge(*mt_dve(4 * h + 2))
                        nc.vector.tensor_tensor(rows[low, :], ps[low, 7, 0:P], rows[low, :], ALU.subtract).then_inc(mt_dve.sem, 1)
                        dve.wait_ge(*mt_dve(4 * h + 3))
                        nc.vector.tensor_tensor(RH[half], rows[half, :].unsqueeze(1).broadcast_to((64, KT, P)),
                                                mask8[half, :].unsqueeze(2).broadcast_to((64, KT, P)), ALU.mult).then_inc(mt_dve.sem, 1)

                    def invert_sums(h):
                        dve.wait_ge(*den_pe(h + 1))
                        nc.vector.reciprocal(REC, ps[:, 7, :]).then_inc(o_dve.sem, 1)

                    def divide(h):
                        dve.wait_ge(*o_dve(3 * h + 1))
                        dve.wait_ge(*pv_pe(KT * h + KT))
                        for j, cs in halves(L1):
                            src, dst = slice(64 * j, 64 * j + 64), slice(64 * (h % 2), 64 * (h % 2) + 64)
                            nc.vector.tensor_tensor(O[dst, h // 2, cs], REC[src, :], ps[src, 6, :], ALU.mult).then_inc(o_dve.sem, 1)

                    for h in range(2):
                        qk_low(h)
                        k_low_again(h)
                    find_maxima(0)
                    rows_of_maxima(0)
                    for h in range(HEADS):
                        if h + 1 < HEADS:
                            find_maxima(h + 1)
                            rows_of_maxima(h + 1)
                        invert_sums(h)
                        if h + 2 < HEADS:
                            qk_low(h + 2)
                        divide(h)
                        if h + 2 < HEADS:
                            k_low_again(h + 2)
                    proj_steps = (proj_pe, lambda ct: o_b[:, ct:ct + 1], proj_dve)
                    add_residual(first, first_cs, range(CT), *proj_steps)
                    add_residual(second, second_cs, range(1), *proj_steps)
                    token_center(1, first, first_cs)
                    add_residual(second, second_cs, range(1, CT), *proj_steps)
                    token_scale(1, first, first_cs)

                    def low_band(i, cs):
                        lc = slice(cs.start // 2, cs.stop // 2)
                        dve.wait_ge(*tn_dve(16 + 8 * i + 8))
                        for j in range(DT):
                            nc.vector.tensor_tensor(LS[:, j, cs], TN[:, j, cs], TN[:, j + 2, cs], ALU.add).then_inc(ll_dve.sem, 1)
                        for j in range(DT):
                            dve.wait_ge(*ll_dve(4 * i + 1 + j))
                            nc.vector.tensor_tensor(LL[:, j, lc], LS[:, j, cs.start:cs.stop:2], LS[:, j, cs.start + 1:cs.stop:2], ALU.add).then_inc(ll_dve.sem, 1)

                    token_center(1, second, second_cs)
                    low_band(first, first_cs)
                    token_scale(1, second, second_cs)
                    low_band(second, second_cs)
                    dve.wait_ge(*ll_dve(8))
                    for ct in range(CT):
                        nc.vector.tensor_tensor(T[:, ct, :], T[:, ct, :], TN[:, ct, :], ALU.add).then_inc(fin_dve.sem, 1)
                    dve.wait_ge(*fin_dve(4))
                    group_norm(dve, gn_next, 0)
                    for o in range(DT):
                        k = 4 + 4 * o
                        dve.wait_ge(*fc2_pe(o + 1))
                        nc.vector.scalar_tensor_tensor(out=DL[:, o, :], in0=LL[:, o, :], scalar=-0.5, in1=ps[:, 6 + o, :],
                                                       op0=ALU.mult, op1=ALU.add).then_inc(fin_dve.sem, 1)
                        dve.wait_ge(*fin_dve(k + 1))
                        nc.vector.tensor_scalar(DL[:, o, :], DL[:, o, :], vec("fc2_b", o), 0.5, ALU.add, ALU.mult).then_inc(fin_dve.sem, 1)
                        dve.wait_ge(*fin_dve(k + 2))
                        for ct in (o, 2 + o):
                            tv = T[:, ct, :].rearrange("p (f two) -> p f two", two=2)
                            nc.vector.tensor_tensor(tv, tv, DL[:, o, :].unsqueeze(2).broadcast_to((P, BANK, 2)), ALU.add).then_inc(fin_dve.sem, 1)

                @block.gpsimd
                def _(pool):
                    for u in range(N_UNITS):
                        g, n = GROUPS[u // N_STATE], u % N_STATE
                        pool.wait_ge(*c_kept(u + 1))
                        c = CB[:, u % 2, 0:g.n].unsqueeze(1).broadcast_to((P, len(g.dirs), g.n))
                        for half in range(DT):
                            s = 2 * u + half
                            pool.wait_ge(*scanned(s + 1))
                            if s >= 3:
                                pool.wait_ge(*summed(s - 2))
                            h, hc = (v[:, r, 0:g.width].rearrange("p (d n) -> p d n", n=g.n) for v, r in ((H, s % 4), (HC, s % 3)))
                            nc.gpsimd.tensor_tensor(hc, h, c, ALU.mult).then_inc(weighed.sem, 1)
                    for h in range(HEADS):
                        for kt in range(1, KT):
                            i = KT * h + kt
                            pool.wait_ge(*s_exp(i + 1))
                            if kt == 1 and h >= 2:
                                pool.wait_ge(*den_pe(h - 1))
                            if kt > 1:
                                pool.wait_ge(*den_pool(7 * h + kt - 1))
                            sums = DEN[:, h % 2, :]
                            nc.gpsimd.tensor_tensor(sums, PR[:, 0, :] if kt == 1 else sums, PR[:, i % 4, :], ALU.add).then_inc(den_pool.sem, 1)


            nc.all_engine_barrier(sems_to_clear=range(min(s.sem.num for s in signals), max(s.sem.num for s in signals) + 1))


def tiles(a):
    n = a.shape[0] // P
    return a.reshape(n, P, -1).transpose(1, 0, 2)


def kernel(**inputs):
    import numpy as np
    import concourse.bacc as bacc
    from concourse.bass_utils import run_bass_kernel_spmd

    w = {k: np.asarray(v) for k, v in inputs.items()}
    g = {k[8:]: v for k, v in w.items() if k.startswith("L0_conv_")}
    perm = np.concatenate([np.arange(0, C, 2), np.arange(1, C, 2)])

    ident = np.eye(P, dtype=np.float32)
    gmat = np.kron(np.eye(16, dtype=np.float32), np.full((8, 8), 1 / 16, np.float32))
    sel = np.zeros((96, 2 * N_STATE, P), np.float32)
    for r in range(96):
        sel[r, r % 32] = 1
    neg = np.zeros((P, P), np.float32)
    mask8 = np.zeros((P, KT), np.float32)
    for r in range(P):
        if r % 32 < KT:
            neg[r] = -1
            mask8[r, r % 32] = 1
    pos = np.linspace(0.0, 1.0, C, dtype=np.float32) * np.float32(C // 2 - 1)
    i0 = np.clip(np.floor(pos).astype(np.int32), 0, C // 2 - 2)
    frac = (pos - i0.astype(np.float32)).astype(np.float32)
    up = np.zeros((C, C // 2), np.float32)
    up[np.arange(C), i0] = np.float32(1.0) - frac
    up[np.arange(C), i0 + 1] = frac

    qk_rows = [part * C + HD * h + i for h in range(HEADS) for part in range(2) for i in range(HD)]
    xrows = list(range(R_DT, R_DT + 2 * N_STATE)) * 3 + list(range(R_DT))
    cols = {"in_bx": g["in_b"][:D], "in_bz": g["in_b"][D:], "c1_b": g["c1_b"], "c2_b": g["c2_b"], "c3_b": g["c3_b"],
            "out_b": g["out_b"][perm], "qk_b": w["L1_attn_qkv_b"][qk_rows], "v_b": w["L1_attn_qkv_b"][2 * C:],
            "proj_b": w["L1_attn_proj_b"][perm], "fc1_b": w["L1_ffn_fc1_b"], "fc2_b": w["L1_ffn_fc2_b"]}
    for s in (1, 2, 3):
        cols |= {f"{v}{s}": g[f"{v}{s}"] for v in ("dtb", "Dv", "g", "be")}
        cols[f"Al{s}"] = g[f"Al{s}"]
    vecs = np.concatenate([tiles(cols[n]).reshape(P, -1) for n in VEC], axis=1)
    arrays = {
        "x": w["x"].reshape(B, C, L1)[[*range(B), 0]],
        "in_x": tiles(g["in_w"][:D][:, perm]), "in_z": tiles(g["in_w"][D:][:, perm].T), "c1": tiles(g["c1_w"].T),
        "c2": tiles(g["c2_w"].transpose(1, 2, 3, 0).reshape(D, -1)), "c3": tiles(g["c3_w"].transpose(1, 2, 3, 0).reshape(D, -1)),
        "out": tiles(g["out_w"][perm].T), "up": tiles(up), "fc1": tiles(w["L1_ffn_fc1_w"].T), "fc2": tiles(w["L1_ffn_fc2_w"].T),
        "qkv": tiles(w["L1_attn_qkv_w"][qk_rows + list(range(2 * C, 3 * C))][:, perm].T), "proj": tiles(w["L1_attn_proj_w"][perm].T),
        "vecs": vecs, "ident": ident, "gmat": gmat, "sel": sel, "neg": neg, "mask8": mask8,
    }
    for s in (1, 2, 3):
        arrays[f"xw{s}"] = tiles(g[f"xw{s}"][xrows].T)
        arrays[f"dtw{s}"] = g[f"dtw{s}"].T
    for k in ("c2", "c3"):
        arrays[k] = arrays[k].reshape(P, DT, 4, D)
    arrays = {k: np.ascontiguousarray(v) for k, v in arrays.items()}

    nc = bacc.Bacc("TRN2", target_bir_lowering=False, num_devices=1)
    t = {k: nc.dram_tensor(f"in_{k}", v.shape, mybir.dt.from_np(v.dtype), kind="ExternalInput").ap() for k, v in arrays.items()}
    t["y"] = nc.dram_tensor("out", (B, C, L1), F32, kind="ExternalOutput").ap()
    build(nc, t)
    r = run_bass_kernel_spmd(nc, [{f"in_{k}": v for k, v in arrays.items()}], core_ids=[0])
    return r.results[0]["out"].reshape(B, C, 32, 32)
```
